# Optimizing a Trainium2 kernel written in Bass

```python
import numpy as np
import jax
import jax.numpy as jnp

def _softmax(x, axis=-1):
    return jax.nn.softmax(x, axis=axis)

def _gelu(x):
    return jax.nn.gelu(x, approximate=True)

def _silu(x):
    return jax.nn.silu(x)

def _sigmoid(x):
    return jax.nn.sigmoid(x)

def _layernorm(x, axis=-1, eps=1e-05):
    m = jnp.mean(x, axis=axis, keepdims=True)
    v = jnp.var(x, axis=axis, keepdims=True)
    return (x - m) / jnp.sqrt(v + eps)

def _scatter_add(tgt, idx, src, axis=0):
    return tgt.at[idx].add(src)

def _segment_sum(src, seg, n):
    return jax.ops.segment_sum(src, seg, n)
kernel_name = 'mk_adaln_d2_jaxref_r8_f8a209'

def setup_inputs(seed: int=0):
    np.random.seed(seed)
    _w = jnp.asarray

    def _L0_attn_setup():
        import jax, jax.numpy as jnp
        import numpy as np
        import math
        B, S, D = (4, 256, 128)
        H = 16
        HD = D // H
        DL = 32
        LAMBDA_DECAY = 0.01
        key = jax.random.key(seed)
        ks = jax.random.split(key, 8)
        sc = lambda fan_in: 1.0 / math.sqrt(fan_in)
        return {'x': jax.random.normal(ks[0], (B, S, D), dtype=jnp.float32), 'W_q': jax.random.normal(ks[1], (D, D), dtype=jnp.float32) * sc(D), 'W_k': jax.random.normal(ks[2], (D, D), dtype=jnp.float32) * sc(D), 'W_v': jax.random.normal(ks[3], (D, D), dtype=jnp.float32) * sc(D), 'W_o': jax.random.normal(ks[4], (D, D), dtype=jnp.float32) * sc(D), 'W_down_kv': jax.random.normal(ks[5], (D, DL), dtype=jnp.float32) * sc(D), 'W_up_k': jax.random.normal(ks[6], (DL, D), dtype=jnp.float32) * sc(DL), 'W_up_v': jax.random.normal(ks[7], (DL, D), dtype=jnp.float32) * sc(DL)}
    _L0_attn_in = _L0_attn_setup()

    def _L0_ffn_setup():
        import jax, jax.numpy as jnp
        import numpy as np
        NUM_EXPERTS = 8
        NUM_LANGS = 4
        TOP_K = 2
        D_MODEL = 128
        EXPERT_SIZE = 512
        B, S = (2, 256)
        key = jax.random.key(seed)
        ks = jax.random.split(key, 6)

        def xavier(k, shape, fan_in, fan_out):
            a = float(np.sqrt(6.0 / (fan_in + fan_out)))
            return jax.random.uniform(k, shape, jnp.float32, -a, a)
        return {'x': jax.random.normal(ks[0], (B, S, D_MODEL), jnp.float32), 'router_w': xavier(ks[1], (NUM_EXPERTS, D_MODEL), D_MODEL, NUM_EXPERTS), 'router_b': jnp.zeros((NUM_EXPERTS,), jnp.float32), 'lang_w': xavier(ks[2], (NUM_LANGS, D_MODEL), D_MODEL, NUM_LANGS), 'lang_b': jnp.zeros((NUM_LANGS,), jnp.float32), 'w1': xavier(ks[3], (NUM_EXPERTS, D_MODEL, EXPERT_SIZE), D_MODEL, EXPERT_SIZE), 'b1': jnp.zeros((NUM_EXPERTS, EXPERT_SIZE), jnp.float32), 'w2': xavier(ks[4], (NUM_EXPERTS, EXPERT_SIZE, D_MODEL), EXPERT_SIZE, D_MODEL), 'b2': jnp.zeros((NUM_EXPERTS, D_MODEL), jnp.float32)}
    _L0_ffn_in = _L0_ffn_setup()
    _L0_c = _w((lambda *s: np.random.randn(*s).astype(np.float32) * 0.05)(16, 128))
    _L0_wmod = _w((lambda *s: np.random.randn(*s).astype(np.float32) * 0.05)(128, 6 * 128) * 128 ** (-0.5))

    def _L1_attn_setup():
        import jax, jax.numpy as jnp
        import numpy as np
        D_MODEL = 128
        N_HEADS = 16
        D_HEAD = D_MODEL // N_HEADS
        WIN = 32
        NEG_INF = -1e+30

        def _band_mask(nb: int):
            ti = jnp.arange(WIN)[:, None]
            tj = jnp.arange(2 * WIN)[None, :]
            base = (tj >= ti + 1) & (tj <= ti + WIN)
            first = base & (tj >= WIN)
            rest = jnp.broadcast_to(base, (nb - 1, WIN, 2 * WIN))
            return jnp.concatenate([first[None], rest], axis=0)
        key = jax.random.key(seed)
        k1, k2, k3 = jax.random.split(key, 3)
        B, L = (4, 512)
        x = jax.random.normal(k1, (B, L, D_MODEL), dtype=jnp.float32)
        w_qkv = jax.random.normal(k2, (D_MODEL, 3 * D_MODEL), dtype=jnp.float32) * (1.0 / np.sqrt(D_MODEL))
        w_out = jax.random.normal(k3, (D_MODEL, D_MODEL), dtype=jnp.float32) * (1.0 / np.sqrt(D_MODEL))
        return {'x': x, 'w_qkv': w_qkv, 'w_out': w_out}
    _L1_attn_in = _L1_attn_setup()

    def _L1_ffn_setup():
        import jax, jax.numpy as jnp
        import numpy as np
        DIM = 128
        HIDDEN = 512
        E = 8
        B, S = (2, 512)
        key = jax.random.key(seed)
        ks = jax.random.split(key, 8)
        sd = 1.0 / np.sqrt(DIM)
        sh = 1.0 / np.sqrt(HIDDEN)
        return {'x': jax.random.normal(ks[0], (B, S, DIM), dtype=jnp.float32), 'router_w': jax.random.uniform(ks[1], (DIM, E), jnp.float32, -sd, sd), 'router_b': jax.random.uniform(ks[2], (E,), jnp.float32, -sd, sd), 'w1': jax.random.uniform(ks[3], (E, DIM, 2 * HIDDEN), jnp.float32, -sd, sd), 'b1': jax.random.uniform(ks[4], (E, 2 * HIDDEN), jnp.float32, -sd, sd), 'w2': jax.random.uniform(ks[5], (E, HIDDEN, DIM), jnp.float32, -sh, sh), 'b2': jax.random.uniform(ks[6], (E, DIM), jnp.float32, -sh, sh)}
    _L1_ffn_in = _L1_ffn_setup()
    _L1_c = _w((lambda *s: np.random.randn(*s).astype(np.float32) * 0.05)(16, 128))
    _L1_wmod = _w((lambda *s: np.random.randn(*s).astype(np.float32) * 0.05)(128, 6 * 128) * 128 ** (-0.5))
    _d = {'L0_attn_x': _L0_attn_in['x'], 'L0_attn_W_q': _L0_attn_in['W_q'], 'L0_attn_W_k': _L0_attn_in['W_k'], 'L0_attn_W_v': _L0_attn_in['W_v'], 'L0_attn_W_o': _L0_attn_in['W_o'], 'L0_attn_W_down_kv': _L0_attn_in['W_down_kv'], 'L0_attn_W_up_k': _L0_attn_in['W_up_k'], 'L0_attn_W_up_v': _L0_attn_in['W_up_v'], 'L0_ffn_router_w': _L0_ffn_in['router_w'], 'L0_ffn_router_b': _L0_ffn_in['router_b'], 'L0_ffn_lang_w': _L0_ffn_in['lang_w'], 'L0_ffn_lang_b': _L0_ffn_in['lang_b'], 'L0_ffn_w1': _L0_ffn_in['w1'], 'L0_ffn_b1': _L0_ffn_in['b1'], 'L0_ffn_w2': _L0_ffn_in['w2'], 'L0_ffn_b2': _L0_ffn_in['b2'], 'L0_c': _L0_c, 'L0_wmod': _L0_wmod, 'L1_attn_w_qkv': _L1_attn_in['w_qkv'], 'L1_attn_w_out': _L1_attn_in['w_out'], 'L1_ffn_router_w': _L1_ffn_in['router_w'], 'L1_ffn_router_b': _L1_ffn_in['router_b'], 'L1_ffn_w1': _L1_ffn_in['w1'], 'L1_ffn_b1': _L1_ffn_in['b1'], 'L1_ffn_w2': _L1_ffn_in['w2'], 'L1_ffn_b2': _L1_ffn_in['b2'], 'L1_c': _L1_c, 'L1_wmod': _L1_wmod}
    _x0 = _d['L0_attn_x']
    _d['L0_attn_x'] = jax.random.normal(jax.random.fold_in(jax.random.key(seed), 1), (16, 512, 128), dtype=_x0.dtype)
    del _x0
    return _d

def reference(L0_attn_x, L0_attn_W_q, L0_attn_W_k, L0_attn_W_v, L0_attn_W_o, L0_attn_W_down_kv, L0_attn_W_up_k, L0_attn_W_up_v, L0_ffn_router_w, L0_ffn_router_b, L0_ffn_lang_w, L0_ffn_lang_b, L0_ffn_w1, L0_ffn_b1, L0_ffn_w2, L0_ffn_b2, L0_c, L0_wmod, L1_attn_w_qkv, L1_attn_w_out, L1_ffn_router_w, L1_ffn_router_b, L1_ffn_w1, L1_ffn_b1, L1_ffn_w2, L1_ffn_b2, L1_c, L1_wmod):

    def _L0_attn_ref(x, W_q, W_k, W_v, W_o, W_down_kv, W_up_k, W_up_v):
        import jax, jax.numpy as jnp
        import numpy as np
        import math
        B, S, D = (4, 256, 128)
        H = 16
        HD = D // H
        DL = 32
        LAMBDA_DECAY = 0.01
        b, s, d = x.shape
        q = x @ W_q
        k = x @ W_k
        v = x @ W_v
        latent_kv = (k + v) @ W_down_kv
        k_rec = (latent_kv @ W_up_k).reshape(b, s, H, HD).transpose(0, 2, 1, 3)
        v_rec = (latent_kv @ W_up_v).reshape(b, s, H, HD).transpose(0, 2, 1, 3)
        qh = q.reshape(b, s, H, HD).transpose(0, 2, 1, 3)
        scores = jnp.einsum('bhqd,bhkd->bhqk', qh, k_rec) / math.sqrt(d)
        t = jnp.arange(s, dtype=jnp.float32)
        decay = jnp.exp(-LAMBDA_DECAY * jnp.abs(t[:, None] - t[None, :]))
        scores = scores * decay[None, None, :, :]
        attn = jax.nn.softmax(scores, axis=-1)
        out = jnp.einsum('bhqk,bhkd->bhqd', attn, v_rec)
        out = out.transpose(0, 2, 1, 3).reshape(b, s, d)
        return out @ W_o

    def _L0_ffn_ref(x, router_w, router_b, lang_w, lang_b, w1, b1, w2, b2):
        import jax, jax.numpy as jnp
        import numpy as np
        NUM_EXPERTS = 8
        NUM_LANGS = 4
        TOP_K = 2
        D_MODEL = 128
        EXPERT_SIZE = 512
        B, S = (2, 256)
        lang_logits = x @ lang_w.T + lang_b
        lang_probs = jax.nn.softmax(lang_logits, axis=-1)
        lp_pad = jnp.pad(lang_probs, ((0, 0), (0, 0), (0, 1)))
        idx = jnp.arange(NUM_EXPERTS) % NUM_LANGS
        expert_weights = lp_pad[..., idx] + lp_pad[..., idx + 1]
        router_logits = x @ router_w.T + router_b + 0.1 * expert_weights
        router_probs = jax.nn.softmax(router_logits, axis=-1)
        top_p, top_i = jax.lax.top_k(router_probs, TOP_K)
        top_p = top_p / top_p.sum(axis=-1, keepdims=True)
        h = jax.nn.gelu(jnp.einsum('bsd,edh->bseh', x, w1) + b1, approximate=False)
        expert_out = jnp.einsum('bseh,ehd->bsed', h, w2) + b2
        sel = jnp.take_along_axis(expert_out, top_i[..., None], axis=2)
        return (top_p[..., None] * sel).sum(axis=2)

    def _L1_attn_ref(x, w_qkv, w_out):
        import jax, jax.numpy as jnp
        import numpy as np
        D_MODEL = 128
        N_HEADS = 16
        D_HEAD = D_MODEL // N_HEADS
        WIN = 32
        NEG_INF = -1e+30

        def _band_mask(nb: int):
            ti = jnp.arange(WIN)[:, None]
            tj = jnp.arange(2 * WIN)[None, :]
            base = (tj >= ti + 1) & (tj <= ti + WIN)
            first = base & (tj >= WIN)
            rest = jnp.broadcast_to(base, (nb - 1, WIN, 2 * WIN))
            return jnp.concatenate([first[None], rest], axis=0)
        B, L, D = x.shape
        nb = L // WIN
        qkv = (x @ w_qkv).reshape(B, L, 3, N_HEADS, D_HEAD)
        q, k, v = (qkv[:, :, 0], qkv[:, :, 1], qkv[:, :, 2])

        def to_blocks(t):
            return t.transpose(0, 2, 1, 3).reshape(B, N_HEADS, nb, WIN, D_HEAD)
        qb, kb, vb = (to_blocks(q), to_blocks(k), to_blocks(v))
        zero_blk = jnp.zeros_like(kb[:, :, :1])
        k_kv = jnp.concatenate([jnp.concatenate([zero_blk, kb[:, :, :-1]], axis=2), kb], axis=3)
        v_kv = jnp.concatenate([jnp.concatenate([zero_blk, vb[:, :, :-1]], axis=2), vb], axis=3)
        scale = 1.0 / np.sqrt(D_HEAD)
        scores = jnp.einsum('bhnqd,bhnkd->bhnqk', qb, k_kv) * scale
        scores = jnp.where(_band_mask(nb), scores, NEG_INF)
        attn = jax.nn.softmax(scores, axis=-1)
        ob = jnp.einsum('bhnqk,bhnkd->bhnqd', attn, v_kv)
        out = ob.reshape(B, N_HEADS, L, D_HEAD).transpose(0, 2, 1, 3).reshape(B, L, D)
        return out @ w_out

    def _L1_ffn_ref(x, router_w, router_b, w1, b1, w2, b2):
        import jax, jax.numpy as jnp
        import numpy as np
        DIM = 128
        HIDDEN = 512
        E = 8
        B, S = (2, 512)
        logits = jnp.einsum('bsd,de->bse', x, router_w) + router_b
        probs = jax.nn.softmax(logits, axis=-1)
        top1 = jnp.argmax(probs, axis=-1)
        out = jnp.zeros_like(x)
        for i in range(E):
            h = jnp.einsum('bsd,df->bsf', x, w1[i]) + b1[i]
            a, g = jnp.split(h, 2, axis=-1)
            y = jnp.einsum('bsh,hd->bsd', a * jax.nn.sigmoid(g), w2[i]) + b2[i]
            out = out + jnp.where((top1 == i)[..., None], y, 0.0)
        return out
    x = L0_attn_x
    mod = (_silu(L0_c) @ L0_wmod).reshape(L0_c.shape[0], 6, 1, -1)
    sa, ca, ga, sb, cb, gb = (mod[:, 0], mod[:, 1], mod[:, 2], mod[:, 3], mod[:, 4], mod[:, 5])
    ga = (2 * (ga >= 0) - 1) * jnp.maximum(jnp.abs(ga), 0.25)
    gb = (2 * (gb >= 0) - 1) * jnp.maximum(jnp.abs(gb), 0.25)
    h = _layernorm(x, axis=-1) * (1 + ca) + sa
    x = x + ga * _L0_attn_ref(h, L0_attn_W_q, L0_attn_W_k, L0_attn_W_v, L0_attn_W_o, L0_attn_W_down_kv, L0_attn_W_up_k, L0_attn_W_up_v)
    h = _layernorm(x, axis=-1) * (1 + cb) + sb
    x = x + gb * _L0_ffn_ref(h, L0_ffn_router_w, L0_ffn_router_b, L0_ffn_lang_w, L0_ffn_lang_b, L0_ffn_w1, L0_ffn_b1, L0_ffn_w2, L0_ffn_b2)
    mod = (_silu(L1_c) @ L1_wmod).reshape(L1_c.shape[0], 6, 1, -1)
    sa, ca, ga, sb, cb, gb = (mod[:, 0], mod[:, 1], mod[:, 2], mod[:, 3], mod[:, 4], mod[:, 5])
    ga = (2 * (ga >= 0) - 1) * jnp.maximum(jnp.abs(ga), 0.25)
    gb = (2 * (gb >= 0) - 1) * jnp.maximum(jnp.abs(gb), 0.25)
    h = _layernorm(x, axis=-1) * (1 + ca) + sa
    x = x + ga * _L1_attn_ref(h, L1_attn_w_qkv, L1_attn_w_out)
    h = _layernorm(x, axis=-1) * (1 + cb) + sb
    x = x + gb * _L1_ffn_ref(h, L1_ffn_router_w, L1_ffn_router_b, L1_ffn_w1, L1_ffn_b1, L1_ffn_w2, L1_ffn_b2)
    return x

_drawn_inputs = setup_inputs


def setup_inputs(seed=0):
    import zlib

    import numpy as np

    out = dict(_drawn_inputs(seed))
    spreads = {'L0_ffn_router_b': (0.0, 2.0),
     'L0_ffn_lang_b': (0.0, 2.0),
     'L0_ffn_b1': (0.0, 2.0),
     'L0_ffn_b2': (0.0, 2.0)}
    factors = {'L0_attn_W_q': 4.747,
     'L0_attn_W_k': 4.001,
     'L0_attn_W_v': 4.173,
     'L0_attn_W_down_kv': 2.801,
     'L0_attn_W_up_k': 4.706,
     'L0_attn_W_up_v': 2.714,
     'L0_ffn_lang_w': 56.68,
     'L1_ffn_router_b': 33.456,
     'L1_ffn_b1': 64.0,
     'L1_ffn_b2': 178.865,
     'L0_ffn_router_w': 5.448,
     'L0_ffn_w1': 7.263,
     'L0_ffn_w2': 5.535,
     'L1_attn_w_qkv': 7.86,
     'L1_attn_w_out': 7.746,
     'L1_ffn_router_w': 8.0,
     'L1_ffn_w1': 8.0,
     'L1_ffn_w2': 8.0,
     'L1_c': 6.022,
     'L1_wmod': 6.035}
    for name, (base, spread) in spreads.items():
        noise = np.random.default_rng([zlib.crc32(name.encode()), seed]).standard_normal(out[name].shape)
        drawn = base * np.exp(spread * noise) if base else spread * noise
        out[name] = jnp.asarray(drawn.astype(out[name].dtype))
    for name, factor in factors.items():
        out[name] = (out[name] * factor).astype(out[name].dtype)
    return out
```

```python
from contextlib import ExitStack

import numpy as np

import concourse.bass as bass
from concourse import mybir

F32 = mybir.dt.float32
BF16 = mybir.dt.bfloat16
ALU = mybir.AluOpType
ACT = mybir.ActivationFunctionType
AX = mybir.AxisListType

P = 128
NB, S, D = 16, 512, 128
NH, HD = 16, 8
NC = S // P
NU = NH // 4
DL = 32
LN_EPS = 1e-5
GATE_MIN = 0.25
DECAY = 0.01
LOWEST = -3.0e38

PART_Q = (0, 0, 1, 0, 2, 1)
PART_K = (0, 1, 0, 2, 0, 1)
SIDE = 8 * len(PART_Q)
KMAX = 2 * SIDE
KEXP = KMAX + 3
LEAD = 6
STEPS = 4 * NU


def constants():
    i = np.arange(S)
    q_behind = np.exp(-DECAY * (i - S / 2)) / np.sqrt(D)
    q_before = np.exp(DECAY * (i - S / 2)) / np.sqrt(D)
    k_behind = np.exp(DECAY * (i - S / 2))
    k_before = np.exp(-DECAY * (i - S / 2))
    rows = np.stack([q_behind, q_before, k_behind, k_before]).astype(np.float32)
    width = 2 * S - P
    ahead = np.arange(width)[None, :] - np.arange(P)[:, None] - (S - P)
    late = np.exp(-2 * DECAY * np.maximum(ahead, 0)).astype(np.float32)
    ident = np.eye(P, dtype=np.float32)
    prefix = np.triu(np.ones((P, P), np.float32), 1)
    iota = np.tile(np.arange(NE, dtype=np.float32), (NC, 1))
    base = np.arange(NE, dtype=np.float32) * REGION
    row = (np.arange(P)[:, None] + np.array([[0, P]])).astype(np.float32)
    tiles = np.arange(2 * NB * S // TILE + NE, dtype=np.float32)
    head = (np.arange(P)[:, None] // HD % 4 == np.arange(4)[None, :]).astype(np.float32)
    q, k = np.arange(P)[:, None] % WIN, np.arange(2 * WIN)[None, :]
    inside = (k >= q + 1) & (k <= q + WIN)
    band = np.broadcast_to(np.where(inside, 0.0, -1e30)[:, None, None, :], (P, 2, BPU, 2 * WIN)).astype(np.float32)
    band[:, 0, 0, :] = np.where(inside & (k >= WIN), 0.0, -1e30)
    return {"k_head": head, "k_band": band, "k_rows": rows, "k_late": late, "k_ident": ident, "k_prefix": prefix, "k_iota": iota, "k_base": base,
            "k_row": row, "k_tiles": tiles}


def semaphores_of(nc, ctx, prefix):
    taken = []

    def sem(name):
        taken.append(nc.alloc_semaphore(name=prefix + name))
        return taken[-1]

    def give_back():
        nc.clear_and_free_semaphores(taken)
        nc.all_engine_barrier()

    ctx.callback(give_back)
    return sem


def modulation(nc, cT, wmod, cols, gates, shifts):
    with ExitStack() as ctx:
        sb = lambda n, s, d=F32: ctx.enter_context(nc.sbuf_tensor(n, s, d))
        sem = semaphores_of(nc, ctx, "mo_")
        c = sb("mod_c", [P, 2, NB])
        e = sb("mod_e", [P, 2, NB])
        w = sb("mod_w", [P, 2, 6 * D])
        colt = sb("mod_cols", [P, 2, NB, 4])
        g = sb("mod_g", [NB, 2, 2, D])
        sgn = sb("mod_sgn", [NB, 2, 2, D])
        mag = sb("mod_mag", [NB, 2, 2, D])
        sh = sb("mod_sh", [NB, 2, 2, D])
        pc = ctx.enter_context(nc.psum_tensor("mod_pc", [P, 512], F32))
        psh = ctx.enter_context(nc.psum_tensor("mod_psh", [P, 512], F32))
        pg = ctx.enter_context(nc.psum_tensor("mod_pg", [P, 512], F32))
        loaded, expd, dve, mm_cols, mm_gates, stored = (sem("mod_" + n) for n in
                                                        ("loaded", "expd", "dve", "mmc", "mmg", "stored"))
        with nc.Block() as block:
            @block.sync
            def _(sp):
                for l in range(2):
                    sp.dma_start(c[:, l, :], cT[l]).then_inc(loaded, 16)
                    sp.dma_start(w[:, l, :], wmod[l]).then_inc(loaded, 16)
                sp.wait_ge(dve, 7)
                for l in range(2):
                    sp.dma_start(cols[l].rearrange("b f j -> f b j"), colt[:, l]).then_inc(stored, 16)
                    sp.dma_start(gates[l].rearrange("g b f -> b g f"), g[:, l]).then_inc(stored, 16)
                    sp.dma_start(shifts[l], sh[:, l]).then_inc(stored, 16)
                sp.wait_ge(stored, 96)

            @block.scalar
            def _(act):
                act.wait_ge(loaded, 64)
                nc.scalar.activation(e[:], c[:], ACT.Exp, scale=-1.0).then_inc(expd, 1)

            @block.vector
            def _(v):
                v.wait_ge(expd, 1)
                nc.vector.tensor_scalar(e[:], e[:], 1.0, None, ALU.add).then_inc(dve, 1)
                v.wait_ge(dve, 1)
                nc.vector.reciprocal(e[:], e[:]).then_inc(dve, 1)
                v.wait_ge(dve, 2)
                nc.vector.tensor_tensor(c[:], c[:], e[:], ALU.mult).then_inc(dve, 1)
                v.wait_ge(mm_cols, 1)
                v.wait_ge(mm_gates, 1)
                pcv = pc[:, 0:2 * 4 * NB].rearrange("p (l j b) -> p l j b", l=2, j=4)
                for l in range(2):
                    for j in range(4):
                        last = nc.vector.tensor_scalar(colt[:, l, :, j], pcv[:, l, j, :], float(j % 2), None, ALU.add)
                pshv = psh[0:NB, :].rearrange("p (l g f) -> p l g f", l=2, g=2)
                for j in range(2):
                    nc.vector.tensor_scalar(sh[:, :, j, :], pshv[:, :, j, :], float(j), None, ALU.add)
                pgv = pg[0:NB, :].rearrange("p (l g f) -> p l g f", l=2, g=2)
                nc.vector.tensor_copy(g[:], pgv).then_inc(dve, 1)
                v.wait_ge(dve, 4)
                nc.vector.scalar_tensor_tensor(out=mag[:], in0=g[:], scalar=-1.0, in1=g[:], op0=ALU.mult, op1=ALU.max)
                nc.vector.tensor_scalar(sgn[:], g[:], 0.0, 2.0, ALU.is_ge, ALU.mult).then_inc(dve, 1)
                v.wait_ge(dve, 5)
                nc.vector.tensor_scalar(sgn[:], sgn[:], 1.0, None, ALU.subtract).then_inc(dve, 1)
                v.wait_ge(dve, 6)
                nc.vector.scalar_tensor_tensor(out=g[:], in0=mag[:], scalar=GATE_MIN, in1=sgn[:], op0=ALU.max,
                                               op1=ALU.mult).then_inc(dve, 1)

            @block.tensor
            def _(pe):
                pe.wait_ge(dve, 3)
                for l in range(2):
                    for j, part in enumerate((0, 1, 3, 4)):
                        o = (4 * l + j) * NB
                        last = nc.tensor.matmul(pc[:, o:o + NB], w[:, l, part * D:part * D + D], c[:, l, :],
                                                start=True, stop=True)
                last.then_inc(mm_cols, 1)
                for l in range(2):
                    for j, (dst, part) in enumerate(((pg, 2), (pg, 5), (psh, 3), (psh, 4))):
                        o = (2 * l + j % 2) * D
                        last = nc.tensor.matmul(dst[0:NB, o:o + D], c[:, l, :], w[:, l, part * D:part * D + D],
                                                start=True, stop=True)
                last.then_inc(mm_gates, 1)


def decayed_attention(nc, x, xo, cols, gates, w_q, w_k, w_v, w_o, w_down, w_up_k, w_up_v, k_rows, k_late, k_ident):
    with ExitStack() as ctx:
        sb = lambda n, s, d=F32: ctx.enter_context(nc.sbuf_tensor(n, s, d))
        ps = lambda n, s: ctx.enter_context(nc.psum_tensor(n, s, F32))
        sem = semaphores_of(nc, ctx, "da_")

        ident = sb("ident", [P, P])
        identb = sb("identb", [P, P], BF16)
        late = sb("late", [P, 2 * S - P])
        rows = sb("rows", [P, 4, S])
        wq, wk, wv, wo = (sb("w" + n, [P, D]) for n in "qkvo")
        wdown = sb("wdown", [P, DL])
        wup = sb("wup", [DL, 2, D])
        wq_turned = sb("wq_turned", [P, D])
        wup_turned = sb("wup_turned", [DL, D])
        xin = [sb(f"xin{i}", [P, NC, D]) for i in range(2)]
        mcol = [sb(f"mcol{i}", [P, 4]) for i in range(2)]
        xres = [sb(f"xres{i}", [P, NC, D]) for i in range(2)]
        gate = [sb(f"gate{i}", [P, D]) for i in range(2)]
        stack_q = [sb(f"stack_q{i}", [P, NH, S], BF16) for i in range(2)]
        stack_kb = [sb(f"stack_kb{i}", [P, NH, S], BF16) for i in range(2)]
        stack_ka = [sb(f"stack_ka{i}", [P, NH, S], BF16) for i in range(2)]
        vx = [sb(f"vx{i}", [P, NC, NH, 16]) for i in range(2)]
        stat = sb("stat", [P, NC, 6])
        mv = sb("mv", [P, NC, 2])
        rstd = sb("rstd", [P, NC])
        half = sb("half", [P, NC])
        nmr = sb("nmr", [P, NC])
        xn = sb("xn", [P, NC, D])
        hT = sb("hT", [P, S])
        kvT = sb("kvT", [P, S])
        latT = sb("latT", [DL, S])
        full = sb("full", [P, 2, S])
        rest = sb("rest", [P, 2, S])
        parts = [sb(f"parts{n}", [P, 2, 3, S], BF16) for n in "qk"]
        sd = [sb(f"sd{i}", [P, S]) for i in range(4)]
        sdc = sb("sdc", [P, 8, 4, P])
        cmax = sb("cmax", [P, 2, NC, 4])
        cpart = sb("cpart", [P, 2, NC, 3, 4], BF16)
        crest = sb("crest", [P, NC, 4])
        cT = [sb(f"cT{i}", [12, S], BF16) for i in range(2)]
        pt = [sb(f"pt{i}", [P, 4, S]) for i in range(2)]
        oTs = sb("oTs", [P, S])
        rsum = sb("rsum", [P, NC, 4])
        otok = sb("otok", [P, NC, D])
        oT = sb("oT", [P, S])
        xout = oT[:].rearrange("p (c d) -> p c d", c=NC)

        pmax = [ps(f"pmax{i}", [P, S]) for i in range(2)]
        pst = [ps(f"pst{i}", [P, 2, S]) for i in range(2)]
        pot = ps("pot", [P, S])
        pmisc = ps("pmisc", [P, S])

        const_in = sem("const_in")
        turned = sem("turned")
        cleared = sem("cleared")
        x_in = [sem(f"x_in{i}") for i in range(2)]
        res_in = [sem(f"res_in{i}") for i in range(2)]
        stack_in = sem("stack_in")
        c_in = [sem(f"c_in{i}") for i in range(2)]
        out_done = sem("out_done")
        stats = sem("stats")
        rstd_ready = sem("rstd_ready")
        nmr_ready = sem("nmr_ready")
        xn_ready = sem("xn_ready")
        ht_ready = sem("ht_ready")
        kv_ready = sem("kv_ready")
        lat_ready = sem("lat_ready")
        full_ready = sem("full_ready")
        hi_ready = sem("hi_ready")
        rest_ready = sem("rest_ready")
        mid_ready = sem("mid_ready")
        low_ready = sem("low_ready")
        v_ready = sem("v_ready")
        misc_full = sem("misc_full")
        misc_free = sem("misc_free")
        max_scored = sem("max_scored")
        max_taken = sem("max_taken")
        diag_ready = sem("diag_ready")
        csplit = sem("csplit")
        cT_ready = sem("cT_ready")
        s_ready = sem("s_ready")
        p_ready = sem("p_ready")
        pv_done = sem("pv_done")
        ot_free = sem("ot_free")
        oTs_ready = sem("oTs_ready")
        recip = sem("recip")
        otok_ready = sem("otok_ready")
        oT_ready = sem("oT_ready")
        gated = sem("gated")
        xout_ready = sem("xout_ready")
        tick = {e: sem("tick_" + e) for e in ("pe", "dve", "act", "pool", "sp")}

        ORDER = ["O3p", "c1", "T2p", "V", "O0", "WOp", "c2", "h", "q", "O1", "kv", "c3", "lat", "k", "O2", "c0n"]
        PREV = ("O3p", "T2p", "WOp")
        PROLOGUE = ["h", "q", "kv", "lat", "k", "V", "h1", "q1", "kv1", "lat1", "k1", "c0"]

        def body_uses(prev, next_v, next_p, next_m):
            skip = set() if prev else set(PREV)
            skip |= set() if next_v else {"V"}
            skip |= set() if next_p else {"h", "q", "kv", "lat", "k"}
            skip |= set() if next_m else {"c0n"}
            return [n for n in ORDER if n not in skip]

        FIRST = body_uses(False, True, True, True)
        FULL = body_uses(True, True, True, True)

        class Body:

            def __init__(self, b, half, par, at, prev=True, next_v=True, next_p=True, next_m=True):
                self.b, self.half, self.par, self.at = b, half, par, at
                self.prev, self.next_v, self.next_p, self.next_m = prev, next_v, next_p, next_m
                self.uses = body_uses(prev, next_v, next_p, next_m)

            def nth(self, d):
                return self.half + (self.par + d) // 2

            def use(self, name):
                return self.at + self.uses.index(name)

        def batches(eng, body):
            at1 = len(PROLOGUE) + len(FIRST)
            body(Body(0, 0, 0, len(PROLOGUE), prev=False))
            with eng.Fori(0, (NB - 4) // 2) as i:
                i = eng.snap(i)
                body(Body(2 * i + 1, i, 1, 2 * len(FULL) * i + at1))
                body(Body(2 * i + 2, i + 1, 0, 2 * len(FULL) * i + at1 + len(FULL)))
            at = at1 + (NB - 4) * len(FULL)
            body(Body(NB - 3, NB // 2 - 2, 1, at))
            at += len(FULL)
            last2 = Body(NB - 2, NB // 2 - 1, 0, at, next_p=False)
            body(last2)
            last1 = Body(NB - 1, NB // 2 - 1, 1, at + len(last2.uses), next_v=False, next_p=False, next_m=False)
            body(last1)
            return last1.at + len(last1.uses)

        with nc.Block() as block:
            @block.sync
            def _(sp):
                for dst, src in ((ident[:], k_ident), (late[:], k_late), (wq[:], w_q), (wk[:], w_k), (wv[:], w_v),
                                 (wo[:], w_o), (wdown[:], w_down), (wup[:, 0, :], w_up_k), (wup[:, 1, :], w_up_v)):
                    sp.dma_start(dst, src).then_inc(const_in, 16)
                sp.dma_start(rows[:], k_rows[None, :, :].to_broadcast([P, 4, S])).then_inc(const_in, 16)

                def hold(s, v):
                    sp.wait_ge(s, v)
                    sp.sem_inc(tick["sp"], 1)

                def load_x(p, par):
                    if not isinstance(p, int) or p >= 2:
                        hold(ht_ready, p - 1)
                    sp.dma_start(xin[par][:], x[p].rearrange("(c p) d -> p c d", p=P)).then_inc(x_in[par], 16)
                    sp.dma_start(mcol[par][:], cols[p]).then_inc(x_in[par], 16)

                def load_stacks(p, par):
                    hold(low_ready, 2 * p + 2)
                    if not isinstance(p, int) or p >= 2:
                        hold(s_ready, 2 * STEPS * (p - 1))
                    for side in range(2):
                        stack_k = (stack_kb, stack_ka)[side][par]
                        for r in range(len(PART_Q)):
                            o = SIDE * side + HD * r
                            for dst, src in ((stack_q[par], parts[0][:, side, PART_Q[r], :]),
                                             (stack_k, parts[1][:, side, PART_K[r], :])):
                                sp.dma_start(dst[o:o + HD, :, :], src).then_inc(stack_in, 16)

                def load_residual(b, par):
                    sp.dma_start(xres[par][:], x[b].rearrange("(c p) d -> p c d", p=P)).then_inc(res_in[par], 16)
                    sp.dma_start(gate[par][:], gates[b].unsqueeze(0).to_broadcast([P, D])).then_inc(res_in[par], 16)

                def store_maxima(unit, par, u):
                    hold(cT_ready, unit + 1)
                    sp.dma_start(stack_q[par][KMAX:KEXP, 4 * u:4 * u + 4, :], cT[u % 2][:]).then_inc(c_in[u % 2], 16)

                def store_out(b):
                    hold(xout_ready, b + 1)
                    sp.dma_start(xo[b].rearrange("(c p) d -> p c d", p=P), xout).then_inc(out_done, 16)

                sp.sem_inc(out_done, 16)
                load_x(0, 0)
                load_x(1, 1)
                sp.wait_ge(cleared, 7)
                load_stacks(0, 0)
                store_maxima(0, 0, 0)

                def body(k):
                    b, par = k.b, k.par
                    if k.next_v:
                        load_stacks(b + 1, 1 - par)
                    if k.next_p:
                        load_x(b + 2, par)
                    store_maxima(NU * b + 1, par, 1)
                    if k.prev:
                        store_out(b - 1)
                    load_residual(b, par)
                    store_maxima(NU * b + 2, par, 2)
                    store_maxima(NU * b + 3, par, 3)
                    if k.next_m:
                        store_maxima(NU * b + 4, 1 - par, 0)

                batches(sp, body)
                store_out(NB - 1)
                sp.wait_ge(out_done, 16 * (NB + 1))

            @block.tensor
            def _(pe):
                def hold(s, v):
                    pe.wait_ge(s, v)
                    pe.sem_inc(tick["pe"], 1)

                def misc(n):
                    if not isinstance(n, int) or n > 0:
                        hold(misc_free, n)

                def project(p, uses):
                    misc(uses("h"))
                    hold(xn_ready, p + 1)
                    for c in range(NC):
                        last = nc.tensor.transpose(pmisc[:, c * P:(c + 1) * P], xn[:, c, :], ident[:])
                    last.then_inc(misc_full, 1)

                def project_q(p, n):
                    misc(n)
                    hold(ht_ready, p + 1)
                    nc.tensor.matmul(pmisc[:], wq_turned[:], hT[:], start=True, stop=True).then_inc(misc_full, 1)

                def project_kv(n):
                    misc(n)
                    nc.tensor.matmul(pmisc[:], wk[:], hT[:], start=True, stop=False)
                    nc.tensor.matmul(pmisc[:], wv[:], hT[:], start=False, stop=True).then_inc(misc_full, 1)

                def project_lat(p, n):
                    misc(n)
                    hold(kv_ready, p + 1)
                    nc.tensor.matmul(pmisc[0:DL, :], wdown[:], kvT[:], start=True, stop=True).then_inc(misc_full, 1)

                def project_k(p, n):
                    misc(n)
                    hold(lat_ready, p + 1)
                    nc.tensor.matmul(pmisc[:], wup_turned[:], latT[:], start=True, stop=True).then_inc(misc_full, 1)

                def project_v(n):
                    misc(n)
                    for c in range(NC):
                        last = nc.tensor.matmul(pmisc[:, c * P:(c + 1) * P], latT[:, c * P:(c + 1) * P], wup[:, 1, :],
                                                start=True, stop=True)
                    last.then_inc(misc_full, 1)

                def score_for_max(b, par, m, j):
                    n = 4 * (STEPS * b + m) + j
                    h, c = 4 * (m // NC) + j, m % NC
                    if not isinstance(n, int) or n >= 2:
                        hold(max_taken, n - 1)
                    nc.tensor.matmul(pmax[j % 2][:], stack_q[par][0:KMAX, h, c * P:(c + 1) * P],
                                     stack_kb[par][0:KMAX, h, :], start=True, stop=True).then_inc(max_scored, 1)

                def transpose_maxima(unit, u, n):
                    misc(n)
                    hold(csplit, 4 * unit + 4)
                    out = pmisc[0:12, :].bitcast(BF16)
                    for c in range(NC):
                        last = nc.tensor.transpose(out[:, c * P:(c + 1) * P],
                                                   cpart[:, u % 2, c].rearrange("p a b -> p (a b)"), identb[:])
                    last.then_inc(misc_full, 1)

                def scores(b, par, f, pair):
                    e = 2 * (STEPS * b + f) + pair
                    u, c = f // NC, f % NC
                    if not isinstance(e, int) or e >= 2:
                        hold(p_ready, e - 1)
                    if c == 0 and pair == 0:
                        hold(c_in[u % 2], 16 * (2 * b + u // 2 + 1))
                    hold(diag_ready, 4 * (STEPS * b + f) + 2 * pair + 2)
                    keys = slice(c * P, (c + 1) * P)
                    for k in range(2):
                        h = 4 * u + 2 * pair + k
                        out = pst[e_par(f, pair)][:, k, :]
                        if c < NC - 1:
                            behind = slice((c + 1) * P, S)
                            nc.tensor.matmul(out[:, behind], stack_kb[par][0:KEXP, h, keys],
                                             stack_q[par][0:KEXP, h, behind], start=True, stop=True)
                        if c > 0:
                            ahead = slice(0, c * P)
                            nc.tensor.matmul(out[:, ahead], stack_ka[par][0:KEXP, h, keys],
                                             stack_q[par][0:KEXP, h, ahead], start=True, stop=True)
                        last = nc.tensor.transpose(out[:, keys], sdc[:, f % 8, 2 * pair + k, :], ident[:])
                    last.then_inc(s_ready, 1)

                def e_par(f, pair):
                    return pair

                def weigh(b, par, f):
                    u, c = f // NC, f % NC
                    hold(p_ready, 2 * (STEPS * b + f) + 2)
                    if c == 0:
                        hold(v_ready, b + 1)
                        if not isinstance(b, int) or NU * b + u > 0:
                            hold(ot_free, NU * b + u)
                    for j in range(4):
                        last = nc.tensor.matmul(pot[32 * j:32 * j + 16, :], vx[par][:, c, 4 * u + j, :], pt[f % 2][:, j, :],
                                                start=(c == 0), stop=(c == NC - 1), skip_group_check=True)
                    last.then_inc(pv_done, 1)

                def turn_heads(unit, n):
                    misc(n)
                    hold(oTs_ready, unit + 1)
                    for c in range(NC):
                        last = nc.tensor.transpose(pmisc[:, c * P:(c + 1) * P], oTs[:, c * P:(c + 1) * P], ident[:])
                    last.then_inc(misc_full, 1)

                def turn_tokens(b, n):
                    misc(n)
                    hold(otok_ready, NU * b + NU)
                    for c in range(NC):
                        last = nc.tensor.transpose(pmisc[:, c * P:(c + 1) * P], otok[:, c, :], ident[:])
                    last.then_inc(misc_full, 1)

                def project_out(b, n):
                    misc(n)
                    hold(oT_ready, b + 1)
                    for c in range(NC):
                        last = nc.tensor.matmul(pmisc[:, c * P:(c + 1) * P], oT[:, c * P:(c + 1) * P], wo[:],
                                                start=True, stop=True)
                    last.then_inc(misc_full, 1)

                pe.wait_ge(const_in, 160)
                pe.wait_ge(cleared, 7)
                pe.wait_ge(turned, 3)
                for p in range(2):
                    at = 6 * p
                    project(p, lambda n: at)
                    project_q(p, at + 1)
                    project_kv(at + 2)
                    project_lat(p, at + 3)
                    project_k(p, at + 4)
                    if p == 0:
                        project_v(5)
                pe.wait_ge(stack_in, 24 * 16)
                for m in range(LEAD):
                    for j in range(4):
                        score_for_max(0, 0, m, j)
                    if m == 4:
                        transpose_maxima(0, 0, 11)

                def body(k):
                    b, par = k.b, k.par
                    for f in range(STEPS):
                        m = f + LEAD
                        if m < STEPS:
                            mb, mpar, mm = b, par, m
                        else:
                            mb, mpar, mm = b + 1, 1 - par, m - STEPS
                        if m == STEPS and k.next_m:
                            hold(stack_in, 24 * 16 * (b + 2))
                        for pair in range(2):
                            scores(b, par, f, pair)
                            if m < STEPS or k.next_m:
                                score_for_max(mb, mpar, mm, 2 * pair)
                                score_for_max(mb, mpar, mm, 2 * pair + 1)
                        if f > 0:
                            weigh(b, par, f - 1)
                        elif k.prev:
                            weigh(b - 1, 1 - par, STEPS - 1)
                        if f == 1 and k.prev:
                            turn_heads(NU * b - 1, k.use("O3p"))
                        if f == 2:
                            transpose_maxima(NU * b + 1, 1, k.use("c1"))
                        if f == 3 and k.prev:
                            turn_tokens(b - 1, k.use("T2p"))
                        if f == 4 and k.next_v:
                            project_v(k.use("V"))
                        if f == 5:
                            turn_heads(NU * b, k.use("O0"))
                            if k.prev:
                                project_out(b - 1, k.use("WOp"))
                        if f == 6:
                            transpose_maxima(NU * b + 2, 0, k.use("c2"))
                        if f == 8 and k.next_p:
                            project(b + 2, k.use)
                        if f == 9:
                            if k.next_p:
                                project_q(b + 2, k.use("q"))
                            turn_heads(NU * b + 1, k.use("O1"))
                        if f == 10:
                            if k.next_p:
                                project_kv(k.use("kv"))
                            transpose_maxima(NU * b + 3, 1, k.use("c3"))
                        if f == 11 and k.next_p:
                            project_lat(b + 2, k.use("lat"))
                        if f == 12 and k.next_p:
                            project_k(b + 2, k.use("k"))
                        if f == 13:
                            turn_heads(NU * b + 2, k.use("O2"))
                        if f == 14 and k.next_m:
                            transpose_maxima(NU * b + 4, 0, k.use("c0n"))

                at = batches(pe, body)
                weigh(NB - 1, 1, STEPS - 1)
                turn_heads(NU * NB - 1, at)
                turn_tokens(NB - 1, at + 1)
                project_out(NB - 1, at + 2)

            @block.scalar
            def _(act):
                def hold(s, v):
                    act.wait_ge(s, v)
                    act.sem_inc(tick["act"], 1)

                def normalise(p, par):
                    hold(nmr_ready, p + 1)
                    if not isinstance(p, int) or p >= 1:
                        hold(ht_ready, p)
                    for c in range(NC):
                        last = nc.scalar.activation(xn[:, c, :], xin[par][:, c, :], ACT.Identity,
                                                    bias=nmr[:, c:c + 1], scale=rstd[:, c:c + 1])
                    last.then_inc(xn_ready, 1)

                def modulate(p, par, n):
                    hold(misc_full, n + 1)
                    nc.scalar.activation(hT[:], pmisc[:], ACT.Identity, bias=mcol[par][:, 0:1],
                                         scale=mcol[par][:, 1:2]).then_inc(misc_free, 1)

                def keep(dst, src, n, ready):
                    hold(misc_full, n + 1)
                    nc.scalar.activation(dst, src, ACT.Copy).then_inc(misc_free, 1)

                def high(p, which):
                    i = 2 * p + which
                    hold(full_ready, i + 1)
                    if not isinstance(p, int) or p >= 1:
                        hold(stack_in, 24 * 16 * p)
                    nc.scalar.activation(parts[which][:, :, 0, :], full[:], ACT.Copy).then_inc(hi_ready, 1)

                def middle(p, which):
                    i = 2 * p + which
                    hold(rest_ready, i + 1)
                    nc.scalar.activation(parts[which][:, :, 1, :], rest[:], ACT.Copy).then_inc(mid_ready, 1)

                def keep_maxima(nth, u, n):
                    hold(misc_full, n + 1)
                    if not isinstance(nth, int) or nth >= 1:
                        hold(c_in[u % 2], 16 * nth)
                    nc.scalar.activation(cT[u % 2][:], pmisc[0:12, :].bitcast(BF16)[:, 0:S], ACT.Copy)\
                        .then_inc(misc_free, 1)
                    hold(misc_free, n + 1)
                    act.sem_inc(cT_ready, 1)

                def keep_turned(b, n):
                    hold(out_done, 16 * (b + 1))
                    keep(oT[:], pmisc[:], n, oT_ready)
                    after(misc_free, n + 1, oT_ready)

                def exponentials(b, f, pair):
                    e = 2 * (STEPS * b + f) + pair
                    hold(s_ready, e + 1)
                    if pair == 0 and (not isinstance(b, int) or b > 0 or f >= 2):
                        hold(pv_done, STEPS * b + f - 1)
                    nc.scalar.activation(pt[f % 2][:, 2 * pair:2 * pair + 2, :], pst[pair][:], ACT.Exp)\
                        .then_inc(p_ready, 1)

                def keep_unit(unit):
                    hold(pv_done, NC * (unit + 1))
                    if not isinstance(unit, int) or unit >= 1:
                        hold(otok_ready, unit)
                    nc.scalar.activation(oTs[:], pot[:], ACT.Copy).then_inc(ot_free, 1)
                    hold(ot_free, unit + 1)
                    act.sem_inc(oTs_ready, 1)

                act.wait_ge(const_in, 160)
                nc.scalar.activation(identb[:], ident[:], ACT.Copy).then_inc(turned, 1)
                nc.scalar.activation(wq_turned[:].rearrange("p (d h) -> p d h", d=HD),
                                     wq[:].rearrange("p (h d) -> p d h", d=HD), ACT.Copy).then_inc(turned, 1)
                nc.scalar.activation(wup_turned[:].rearrange("p (d h) -> p d h", d=HD),
                                     wup[:, 0, :].rearrange("p (h d) -> p d h", d=HD), ACT.Copy).then_inc(turned, 1)

                def after(s_from, value, s_to):
                    hold(s_from, value)
                    act.sem_inc(s_to, 1)

                def projections(p, par, uses, steps):
                    pass

                def ht(p, par, n):
                    modulate(p, par, n)
                    after(misc_free, n + 1, ht_ready)

                def kv(p, n):
                    keep(kvT[:], pmisc[:], n, kv_ready)
                    after(misc_free, n + 1, kv_ready)

                def lat(p, n):
                    keep(latT[:], pmisc[0:DL, :], n, lat_ready)
                    after(misc_free, n + 1, lat_ready)

                def values(b, par, n):
                    hold(misc_full, n + 1)
                    nc.scalar.activation(vx[par][:, :, :, 0:HD], pmisc[:].rearrange("p (c h d) -> p c h d", c=NC, h=NH),
                                         ACT.Copy).then_inc(misc_free, 1)
                    after(misc_free, n + 1, v_ready)

                for p in range(2):
                    at = 6 * p
                    normalise(p, p)
                    ht(p, p, at)
                    high(p, 0)
                    kv(p, at + 2)
                    middle(p, 0)
                    lat(p, at + 3)
                    high(p, 1)
                    if p == 0:
                        values(0, 0, 5)
                    middle(p, 1)
                keep_maxima(0, 0, 11)

                def body(k):
                    b, par = k.b, k.par
                    for f in range(STEPS):
                        exponentials(b, f, 0)
                        exponentials(b, f, 1)
                        if f == 0 and k.prev:
                            keep_unit(NU * b - 1)
                        if f == 2:
                            keep_maxima(2 * b, 1, k.use("c1"))
                        if f == 3 and k.prev:
                            keep_turned(b - 1, k.use("T2p"))
                        if f == 4:
                            if k.next_v:
                                values(b + 1, 1 - par, k.use("V"))
                            keep_unit(NU * b)
                        if f == 6:
                            keep_maxima(2 * b + 1, 0, k.use("c2"))
                        if f == 7 and k.next_p:
                            normalise(b + 2, par)
                        if f == 8:
                            if k.next_p:
                                ht(b + 2, par, k.use("h"))
                            keep_unit(NU * b + 1)
                        if f == 10:
                            if k.next_p:
                                high(b + 2, 0)
                                kv(b + 2, k.use("kv"))
                            keep_maxima(2 * b + 1, 1, k.use("c3"))
                        if f == 11 and k.next_p:
                            middle(b + 2, 0)
                            lat(b + 2, k.use("lat"))
                        if f == 12:
                            keep_unit(NU * b + 2)
                        if f == 13 and k.next_p:
                            high(b + 2, 1)
                        if f == 14 and k.next_m:
                            keep_maxima(2 * b + 2, 0, k.use("c0n"))
                        if f == 15 and k.next_p:
                            middle(b + 2, 1)

                at = batches(act, body)
                keep_unit(NU * NB - 1)
                keep_turned(NB - 1, at + 1)

            @block.vector
            def _(dve):
                def hold(s, v):
                    dve.wait_ge(s, v)
                    dve.sem_inc(tick["dve"], 1)

                for par in range(2):
                    nc.vector.memset(vx[par][:, :, :, HD:HD + 1], 1.0).then_inc(cleared, 1)
                    nc.vector.memset(vx[par][:, :, :, HD + 1:], 0.0)
                    nc.vector.memset(stack_kb[par][0:KMAX, :, :], 0.0)
                    nc.vector.memset(stack_kb[par][KMAX:P, :, :], 1.0).then_inc(cleared, 1)
                    nc.vector.memset(stack_ka[par][0:KMAX, :, :], 0.0)
                    nc.vector.memset(stack_ka[par][KMAX:P, :, :], 1.0).then_inc(cleared, 1)
                nc.vector.memset(half[:], -0.5)
                nc.vector.memset(pot[:], 0.0).then_inc(cleared, 1)
                dve.wait_ge(const_in, 160)

                def statistics(p, par, nth):
                    hold(x_in[par], 32 * nth + 32)
                    if not isinstance(p, int) or p >= 1:
                        hold(xn_ready, p)
                    for c in range(NC):
                        last = nc.vector.bn_stats(stat[:, c, :], xin[par][:, c, :])
                    last.then_inc(stats, 1)
                    hold(stats, 3 * p + 1)
                    for c in range(NC):
                        last = nc.vector.bn_aggr(mv[:, c, :], stat[:, c, :])
                    last.then_inc(stats, 1)
                    hold(stats, 3 * p + 2)
                    nc.vector.tensor_scalar(mv[:, :, 1], mv[:, :, 1], LN_EPS, None, ALU.add).then_inc(stats, 1)

                def shift(p):
                    hold(rstd_ready, p + 1)
                    nc.vector.scalar_tensor_tensor(out=nmr[:], in0=mv[:, :, 0], scalar=-1.0, in1=rstd[:],
                                                   op0=ALU.mult, op1=ALU.mult).then_inc(nmr_ready, 1)

                def decay(p, which, n):
                    hold(misc_full, n + 1)
                    i = 2 * p + which
                    if not isinstance(i, int) or i >= 1:
                        hold(rest_ready, i)
                        hold(hi_ready, i)
                    nc.vector.tensor_tensor(full[:, 0, :], pmisc[:], rows[:, 2 * which, :], ALU.mult)
                    nc.vector.tensor_tensor(full[:, 1, :], pmisc[:], rows[:, 2 * which + 1, :], ALU.mult)\
                        .then_inc(misc_free, 1)
                    hold(misc_free, n + 1)
                    dve.sem_inc(full_ready, 1)

                def maxima(b, m, j):
                    n = 4 * (STEPS * b + m) + j
                    c = m % NC
                    hold(max_scored, n + 1)
                    if not isinstance(n, int) or n >= 4:
                        hold(diag_ready, n - 3)
                    o = S - P - c * P
                    nc.vector.tensor_tensor_reduce(out=sd[j][:], in0=pmax[j % 2][:], in1=late[:, o:o + S], scale=1.0,
                                                   scalar=LOWEST, op0=ALU.mult, op1=ALU.max,
                                                   accum_out=cmax[:, (m // NC) % 2, c, j:j + 1]).then_inc(max_taken, 1)

                def split_maxima(unit, u):
                    par = u % 2
                    hold(max_taken, 16 * (unit + 1))
                    c = cmax[:, par].rearrange("p c j -> p c j")
                    nc.vector.tensor_scalar(cpart[:, par, :, 0, :], c, -1.0, None, ALU.mult).then_inc(csplit, 1)
                    hold(csplit, 4 * unit + 1)
                    nc.vector.scalar_tensor_tensor(out=crest[:], in0=c, scalar=-1.0, in1=cpart[:, par, :, 0, :],
                                                   op0=ALU.mult, op1=ALU.subtract).then_inc(csplit, 1)
                    hold(csplit, 4 * unit + 2)
                    nc.vector.tensor_copy(cpart[:, par, :, 1, :], crest[:]).then_inc(csplit, 1)
                    hold(csplit, 4 * unit + 3)
                    nc.vector.tensor_tensor(cpart[:, par, :, 2, :], crest[:], cpart[:, par, :, 1, :], ALU.subtract)\
                        .then_inc(csplit, 1)

                def normalise_heads(unit, u, n):
                    hold(misc_full, n + 1)
                    if u == 0 and (not isinstance(unit, int) or unit > 0):
                        hold(oT_ready, unit_batch(unit, u))
                    t = pmisc[:].rearrange("p (c j r) -> p c j r", c=NC, j=4)
                    nc.vector.reciprocal(rsum[:], t[:, :, :, HD]).then_inc(recip, 1)
                    hold(recip, unit + 1)
                    nc.vector.tensor_tensor(otok[:, :, 32 * u:32 * u + 32].rearrange("p c (j d) -> p c j d", j=4),
                                            t[:, :, :, 0:HD],
                                            rsum[:].unsqueeze(3).to_broadcast([P, NC, 4, HD]),
                                            ALU.mult).then_inc(misc_free, 1)
                    hold(misc_free, n + 1)
                    dve.sem_inc(otok_ready, 1)

                batch_of = {}

                def unit_batch(unit, u):
                    return batch_of["b"]

                def add_residual(b, par, nth, n):
                    hold(misc_full, n + 1)
                    hold(res_in[par], 32 * (nth + 1))
                    nc.vector.tensor_tensor(xout, pmisc[:].rearrange("p (c d) -> p c d", c=NC),
                                            gate[par][:].unsqueeze(1).to_broadcast([P, NC, D]), ALU.mult)\
                        .then_inc(misc_free, 1)
                    hold(misc_free, n + 1)
                    nc.vector.tensor_tensor(xout, xout, xres[par][:], ALU.add).then_inc(xout_ready, 1)

                for p in range(2):
                    at = 6 * p
                    statistics(p, p, 0)
                    shift(p)
                    decay(p, 0, at + 1)
                    decay(p, 1, at + 4)
                for m in range(LEAD):
                    for j in range(4):
                        maxima(0, m, j)
                    if m == 3:
                        split_maxima(0, 0)

                def body(k):
                    b, par = k.b, k.par
                    for f in range(STEPS):
                        m = f + LEAD
                        for j in range(4):
                            if m < STEPS:
                                maxima(b, m, j)
                            elif k.next_m:
                                maxima(b + 1, m - STEPS, j)
                        if f == 1:
                            split_maxima(NU * b + 1, 1)
                            if k.prev:
                                normalise_heads(NU * b - 1, 3, k.use("O3p"))
                        if f == 5:
                            split_maxima(NU * b + 2, 0)
                            batch_of["b"] = b
                            normalise_heads(NU * b, 0, k.use("O0"))
                            if k.next_p:
                                statistics(b + 2, par, k.nth(2))
                        if f == 6:
                            if k.prev:
                                add_residual(b - 1, 1 - par, k.nth(-1), k.use("WOp"))
                            if k.next_p:
                                shift(b + 2)
                        if f == 9:
                            split_maxima(NU * b + 3, 1)
                            if k.next_p:
                                decay(b + 2, 0, k.use("q"))
                            normalise_heads(NU * b + 1, 1, k.use("O1"))
                        if f == 12 and k.next_p:
                            decay(b + 2, 1, k.use("k"))
                        if f == 13:
                            if k.next_m:
                                split_maxima(NU * b + 4, 0)
                            normalise_heads(NU * b + 2, 2, k.use("O2"))

                at = batches(dve, body)
                normalise_heads(NU * NB - 1, 3, at)
                add_residual(NB - 1, 1, NB // 2 - 1, at + 2)

            @block.gpsimd
            def _(pool):
                def hold(s, v):
                    pool.wait_ge(s, v)
                    pool.sem_inc(tick["pool"], 1)

                def deviation(p):
                    hold(stats, 3 * p + 3)
                    nc.gpsimd.tensor_tensor(rstd[:], mv[:, :, 1], half[:], ALU.pow).then_inc(rstd_ready, 1)

                def remainder(p, which):
                    hold(hi_ready, 2 * p + which + 1)
                    if not isinstance(p, int) or p + which >= 1:
                        hold(low_ready, 2 * p + which)
                    nc.gpsimd.tensor_tensor(rest[:], full[:], parts[which][:, :, 0, :], ALU.subtract)\
                        .then_inc(rest_ready, 1)

                def low(p, which):
                    hold(mid_ready, 2 * p + which + 1)
                    nc.gpsimd.tensor_tensor(parts[which][:, :, 2, :], rest[:], parts[which][:, :, 1, :], ALU.subtract)\
                        .then_inc(low_ready, 1)

                def diagonal(b, m, j):
                    n = 4 * (STEPS * b + m) + j
                    hold(max_taken, n + 1)
                    if j == 0 and (not isinstance(b, int) or STEPS * b + m >= 8):
                        hold(s_ready, 2 * (STEPS * b + m - 8) + 2)
                    c = m % NC
                    nc.gpsimd.tensor_scalar(sdc[:, m % 8, j, :], sd[j][:, c * P:(c + 1) * P],
                                            cmax[:, (m // NC) % 2, c, j:j + 1], None, ALU.subtract)\
                        .then_inc(diag_ready, 1)

                pool.wait_ge(cleared, 7)
                for p in range(2):
                    deviation(p)
                    for which in range(2):
                        remainder(p, which)
                        low(p, which)
                for m in range(LEAD):
                    for j in range(4):
                        diagonal(0, m, j)

                def body(k):
                    b = k.b
                    for f in range(STEPS):
                        m = f + LEAD
                        for j in range(4):
                            if m < STEPS:
                                diagonal(b, m, j)
                            elif k.next_m:
                                diagonal(b + 1, m - STEPS, j)
                        if k.next_p:
                            if f == 5:
                                deviation(b + 2)
                            if f == 10:
                                remainder(b + 2, 0)
                            if f == 11:
                                low(b + 2, 0)
                            if f == 13:
                                remainder(b + 2, 1)
                            if f == 15:
                                low(b + 2, 1)

                batches(pool, body)


TILE = 256
NE = 8
DEEP = 4
HID = 512
REGION = NB * S + TILE


class Chain:

    def __init__(self, eng, sem, tick):
        self.eng, self.sem, self.tick, self.base, self.count = eng, sem, tick, 0, 0

    def start(self, base):
        self.base, self.count = base, 0

    def __call__(self, ins):
        ins.then_inc(self.sem, 1)
        self.count += 1
        self.eng.wait_ge(self.sem, self.base + self.count)
        self.eng.sem_inc(self.tick, 1)


def pairs(eng, body, n):
    body(0)
    with eng.Fori(1, n) as i:
        body(eng.snap(i))


def later(i):
    return not isinstance(i, int) or i > 0


def route(nc, name, x, shifts, w_router, biases, k_ident, k_prefix, k_iota, k_base, k_row, xs, pos_out, weight_out, cnt_out,
          top):
    nl = w_router.shape[1]
    with ExitStack() as ctx:
        sb = lambda n, s, d=F32: ctx.enter_context(nc.sbuf_tensor(f"{name}_{n}", s, d))
        ps = lambda n, s: ctx.enter_context(nc.psum_tensor(f"{name}_{n}", s, F32))
        sem = semaphores_of(nc, ctx, name + "_")
        U32 = mybir.dt.uint32
        ident = sb("ident", [P, P])
        before = sb("before", [P, P])
        ones = sb("ones", [P, P])
        wr = sb("wr", [P, nl])
        bias = sb("bias", [P, nl])
        iota = sb("iota", [P, NC, NE])
        base0 = sb("base0", [P, NE])
        half = sb("half", [P, NC])
        zero = sb("zero", [P, D])
        row = sb("row", [P, 2])
        xin = sb("xin", [P, NC, D])
        shift = sb("shift", [P, 2, D])
        stat = sb("stat", [P, NC, 6])
        mv = sb("mv", [P, NC, 2])
        rstd = sb("rstd", [P, NC])
        h = [sb(f"h{i}", [P, NC, D]) for i in range(2)]
        hT = sb("hT", [P, S])
        lg = sb("lg", [P, NC, nl])
        lang = sb("lang", [P, NC, 5])
        ew = sb("ew", [P, NC, 4])
        m = sb("m", [P, NC])
        prob = sb("prob", [P, NC, NE])
        best = sb("best", [P, NC, 8])
        bidx = sb("bidx", [P, NC, 8], U32)
        idxf = sb("idxf", [P, NC, 2])
        hot = sb("hot", [P, 2, NC, NE])
        both = sb("both", [P, NC, NE])
        wts = [sb(f"wts{i}", [P, NC, 2]) for i in range(2)]
        rank = sb("rank", [P, NC, NE])
        picked = sb("picked", [P, 2, NC, NE])
        place = [sb(f"place{i}", [P, 2, NC, top]) for i in range(2)]
        pos = [sb(f"pos{i}", [P, NC, top], U32) for i in range(2)]
        base = sb("base", [P, NE])
        tail = sb("tail", [P, NE])
        tails = sb("tails", [P, 2, NE], U32)
        ph = ps("ph", [P, S])
        plog = ps("plog", [P, 512])
        ppre = ps("ppre", [P, 512])
        const_in, cleared, x_in, x_used, h_ready, hT_full, hT_ready, log_full, exp_in, exp_out, hot_ready, pre_full, \
            pos_ready, stats, rstd_ready, chain_s, tail_ready, cnt_saved = (
                sem(n) for n in ("const_in", "cleared", "x_in", "x_used", "h_ready", "hT_full", "hT_ready",
                                 "log_full", "exp_in", "exp_out", "hot_ready", "pre_full", "pos_ready",
                                 "stats", "rstd_ready", "chain", "tail_ready", "cnt_saved"))
        scattered = [sem(f"scattered{i}") for i in range(2)]
        saved = [sem(f"saved{i}") for i in range(2)]
        zeroed = sem("zeroed")
        zeroed2 = sem("zeroed2")
        tick = {e: sem("tick_" + e) for e in ("pe", "dve", "act", "pool", "sp")}
        nexp = 2 if top == 2 else 1

        with nc.Block() as block:
            @block.sync
            def _(sp):
                def hold(s, v):
                    sp.wait_ge(s, v)
                    sp.sem_inc(tick["sp"], 1)

                for dst, src in ((ident[:], k_ident), (before[:], k_prefix), (wr[:], w_router),
                                 (row[:], k_row),
                                 (iota[:], k_iota.unsqueeze(0).to_broadcast([P, NC, NE])),
                                 (base0[:], k_base.unsqueeze(0).to_broadcast([P, NE]))):
                    sp.dma_start(dst, src).then_inc(const_in, 16)
                o = 0
                for bvec in biases:
                    n = bvec.shape[0]
                    sp.dma_start(bias[:, o:o + n], bvec.unsqueeze(0).to_broadcast([P, n])).then_inc(const_in, 16)
                    o += n
                sp.wait_ge(cleared, 1)
                for r in range(NE * TILE // P):
                    sp.dma_start(xs[NE * REGION + r * P:NE * REGION + (r + 1) * P, :], zero[:]).then_inc(zeroed, 16)
                sp.sem_inc(x_used, 1)
                with sp.Fori(0, NB) as b:
                    b = sp.snap(b)
                    hold(x_used, b + 1)
                    sp.dma_start(xin[:], x[b].rearrange("(c p) d -> p c d", p=P)).then_inc(x_in, 16)
                    sp.dma_start(shift[:], shifts[b].unsqueeze(0).to_broadcast([P, 2, D])).then_inc(x_in, 16)
                sp.wait_ge(tail_ready, 1)
                sp.dma_start(cnt_out, tail[0:1, :]).then_inc(cnt_saved, 16)
                sp.wait_ge(cnt_saved, 16)
                sp.wait_ge(zeroed, 16 * (NE * TILE // P))

            @block.tensor
            def _(pe):
                def hold(s, v):
                    pe.wait_ge(s, v)
                    pe.sem_inc(tick["pe"], 1)

                pe.wait_ge(const_in, 16 * (6 + len(biases)))
                pe.wait_ge(cleared, 1)

                def batch(b, par):
                    hold(h_ready, b + 1)
                    for c in range(NC):
                        last = nc.tensor.transpose(ph[:, c * P:(c + 1) * P], h[par][:, c, :], ident[:])
                    last.then_inc(hT_full, 1)
                    hold(hT_ready, b + 1)
                    for c in range(NC):
                        last = nc.tensor.matmul(plog[:, c * nl:(c + 1) * nl], hT[:, c * P:(c + 1) * P], wr[:],
                                                start=True, stop=True, skip_group_check=True)
                    last.then_inc(log_full, 1)
                    hold(hot_ready, b + 1)
                    for c in range(NC):
                        for cc in range(c + 1):
                            nc.tensor.matmul(ppre[:, c * NE:(c + 1) * NE], (before if cc == c else ones)[:],
                                             both[:, cc, :], start=(cc == 0), stop=(cc == c), skip_group_check=True)
                    for cc in range(NC):
                        last = nc.tensor.matmul(ppre[:, NC * NE:(NC + 1) * NE], ones[:], both[:, cc, :],
                                                start=(cc == 0), stop=(cc == NC - 1), skip_group_check=True)
                    last.then_inc(pre_full, 1)

                with pe.Fori(0, NB // 2) as i:
                    i = pe.snap(i)
                    for par in range(2):
                        batch(2 * i + par, par)

            @block.scalar
            def _(act):
                def hold(s, v):
                    act.wait_ge(s, v)
                    act.sem_inc(tick["act"], 1)

                with act.Fori(0, NB) as b:
                    b = act.snap(b)
                    hold(hT_full, b + 1)
                    nc.scalar.activation(hT[:], ph[:], ACT.Copy).then_inc(hT_ready, 1)
                    if top == 2:
                        hold(exp_in, nexp * b + 1)
                        nc.scalar.activation(lang[:, :, 0:4], lang[:, :, 0:4], ACT.Exp).then_inc(exp_out, 1)
                    hold(exp_in, nexp * b + nexp)
                    nc.scalar.activation(prob[:], prob[:], ACT.Exp).then_inc(exp_out, 1)

            @block.vector
            def _(dve):
                def hold(s, v):
                    dve.wait_ge(s, v)
                    dve.sem_inc(tick["dve"], 1)

                chain = Chain(dve, chain_s, tick["dve"])
                nc.vector.memset(zero[:], 0.0)
                nc.vector.memset(ones[:], 1.0)
                nc.vector.memset(lang[:], 0.0)
                nc.vector.memset(half[:], -0.5).then_inc(cleared, 1)
                dve.wait_ge(const_in, 16 * (6 + len(biases)))
                chain.start(0)
                chain(nc.vector.tensor_copy(base[:], base0[:]))

                def per_token(v, n):
                    return v.unsqueeze(2).to_broadcast([P, NC, n])

                def softmax(v, n, e):
                    chain(nc.vector.tensor_reduce(m[:], v, AX.X, ALU.max))
                    chain(nc.vector.tensor_tensor(v, v, per_token(m[:], n), ALU.subtract))
                    dve.sem_inc(exp_in, 1)
                    hold(exp_out, e)
                    chain(nc.vector.tensor_reduce(m[:], v, AX.X, ALU.add))
                    chain(nc.vector.reciprocal(m[:], m[:]))
                    chain(nc.vector.tensor_tensor(v, v, per_token(m[:], n), ALU.mult))

                def batch(b, i, par):
                    chain.start(1 + CHAIN * b)
                    hold(x_in, 32 * b + 32)
                    for c in range(NC):
                        last = nc.vector.bn_stats(stat[:, c, :], xin[:, c, :])
                    chain(last)
                    for c in range(NC):
                        last = nc.vector.bn_aggr(mv[:, c, :], stat[:, c, :])
                    chain(last)
                    nc.vector.tensor_scalar(mv[:, :, 1], mv[:, :, 1], LN_EPS, None, ALU.add).then_inc(stats, 1)
                    hold(rstd_ready, b + 1)
                    for c in range(NC):
                        last = nc.vector.tensor_scalar(xin[:, c, :], xin[:, c, :], mv[:, c, 0:1], rstd[:, c:c + 1],
                                                       ALU.subtract, ALU.mult)
                    chain(last)
                    chain(nc.vector.tensor_tensor(xin[:], xin[:], shift[:, 1, :].unsqueeze(1).to_broadcast([P, NC, D]),
                                                  ALU.mult))
                    if later(i):
                        hold(scattered[par], 16 * NC * top * i)
                    chain(nc.vector.tensor_tensor(h[par][:], xin[:],
                                                  shift[:, 0, :].unsqueeze(1).to_broadcast([P, NC, D]), ALU.add))
                    dve.sem_inc(x_used, 1)
                    dve.sem_inc(h_ready, 1)
                    hold(log_full, b + 1)
                    lgv = plog[:, 0:NC * nl].rearrange("p (c n) -> p c n", c=NC)
                    if top == 2:
                        nc.vector.tensor_tensor(lang[:, :, 0:4], lgv[:, :, NE:nl],
                                                bias[:, NE:nl].unsqueeze(1).to_broadcast([P, NC, 4]), ALU.add)
                    chain(nc.vector.tensor_tensor(prob[:], lgv[:, :, 0:NE],
                                                  bias[:, 0:NE].unsqueeze(1).to_broadcast([P, NC, NE]), ALU.add))
                    if top == 2:
                        softmax(lang[:, :, 0:4], 4, 2 * b + 1)
                        chain(nc.vector.tensor_tensor(ew[:], lang[:, :, 0:4], lang[:, :, 1:5], ALU.add))
                        for q in range(2):
                            o = prob[:, :, 4 * q:4 * q + 4]
                            last = nc.vector.scalar_tensor_tensor(out=o, in0=ew[:], scalar=0.1, in1=o, op0=ALU.mult,
                                                                  op1=ALU.add)
                        chain(last)
                    softmax(prob[:], NE, nexp * b + nexp)
                    for c in range(NC):
                        last = nc.vector.max(best[:, c, :], prob[:, c, :])
                    chain(last)
                    for c in range(NC):
                        last = nc.vector.max_index(bidx[:, c, :], best[:, c, :], prob[:, c, :])
                    chain(last)
                    if later(i):
                        hold(saved[par], 16 * top * i)
                    nc.vector.tensor_copy(place[par][:, 1], bidx[:, :, 0:top])
                    chain(nc.vector.tensor_copy(idxf[:], bidx[:, :, 0:2]))
                    for k in range(top):
                        last = nc.vector.tensor_tensor(hot[:, k], iota[:], per_token(idxf[:, :, k], NE), ALU.is_equal)
                    chain(last)
                    if top == 2:
                        chain(nc.vector.tensor_tensor(both[:], hot[:, 0], hot[:, 1], ALU.add))
                        chain(nc.vector.tensor_tensor(m[:], best[:, :, 0], best[:, :, 1], ALU.add))
                        chain(nc.vector.reciprocal(m[:], m[:]))
                        chain(nc.vector.tensor_tensor(wts[par][:], best[:, :, 0:2], per_token(m[:], 2), ALU.mult))
                    else:
                        chain(nc.vector.tensor_copy(both[:], hot[:, 0]))
                    dve.sem_inc(hot_ready, 1)
                    hold(pre_full, b + 1)
                    chain(nc.vector.tensor_tensor(rank[:], ppre[:, 0:NC * NE].rearrange("p (c e) -> p c e", c=NC),
                                                  base[:].unsqueeze(1).to_broadcast([P, NC, NE]), ALU.add))
                    for k in range(top):
                        last = nc.vector.tensor_tensor(picked[:, k], rank[:], hot[:, k], ALU.mult)
                    chain(last)
                    for k in range(top):
                        last = nc.vector.tensor_reduce(place[par][:, 0, :, k], picked[:, k], AX.X, ALU.add)
                    chain(last)
                    nc.vector.tensor_copy(pos[par][:], place[par][:, 0]).then_inc(pos_ready, 1)
                    chain(nc.vector.tensor_tensor(base[:], ppre[:, NC * NE:(NC + 1) * NE], base[:], ALU.add))

                CHAIN = (3 + 2 + 1 + 5 * nexp + (2 if top == 2 else 0) + 4 + (4 if top == 2 else 1) + 4)

                def pair(i):
                    for par in range(2):
                        batch(2 * i + par, i, par)
                        assert chain.count == CHAIN, (chain.count, CHAIN)

                pairs(dve, pair, NB // 2)
                chain.start(1 + CHAIN * NB)
                for q in range(2):
                    last = nc.vector.tensor_scalar(picked[:, q, 0, :], base[:], row[:, q:q + 1], None, ALU.add)
                chain(last)
                nc.vector.tensor_tensor(tail[:], base[:], base0[:], ALU.subtract)
                nc.vector.tensor_copy(tails[:], picked[:, :, 0, :]).then_inc(tail_ready, 1)

            @block.gpsimd
            def _(pool):
                def hold(s, v):
                    pool.wait_ge(s, v)
                    pool.sem_inc(tick["pool"], 1)

                pool.wait_ge(cleared, 1)
                with pool.Fori(0, NB // 2) as i:
                    i = pool.snap(i)
                    for par in range(2):
                        b = 2 * i + par
                        hold(stats, b + 1)
                        nc.gpsimd.tensor_tensor(rstd[:], mv[:, :, 1], half[:], ALU.pow).then_inc(rstd_ready, 1)
                        hold(pos_ready, b + 1)
                        pool.dma_start(pos_out[b], place[par][:]).then_inc(saved[par], 16)
                        if top == 2:
                            pool.dma_start(weight_out[b], wts[par][:]).then_inc(saved[par], 16)
                        for c in range(NC):
                            for k in range(top):
                                nc.gpsimd.indirect_dma_start(
                                    out=xs[:, :], out_offset=bass.IndirectOffsetOnAxis(ap=pos[par][:, c, k:k + 1], axis=0),
                                    in_=h[par][:, c, :], in_offset=None).then_inc(scattered[par], 16)
                pool.wait_ge(tail_ready, 1)
                for e in range(NE):
                    for q in range(TILE // P):
                        nc.gpsimd.indirect_dma_start(
                            out=xs[:, :], out_offset=bass.IndirectOffsetOnAxis(ap=tails[:, q, e:e + 1], axis=0),
                            in_=zero[:], in_offset=None).then_inc(zeroed2, 16)
                for par in range(2):
                    pool.wait_ge(scattered[par], 16 * NC * top * (NB // 2))
                    pool.wait_ge(saved[par], 16 * top * (NB // 2))
                pool.wait_ge(zeroed2, 16 * NE * (TILE // P))


def tiles_before(nc, chain, cn, cni, tiles, cum):
    chain(nc.vector.tensor_scalar(cni[:], cn[:], float(TILE - 1), None, ALU.add))
    chain(nc.vector.tensor_single_scalar(cni[:], cni[:], int(np.log2(TILE)), ALU.logical_shift_right))
    chain(nc.vector.tensor_copy(tiles[:], cni[:]))
    chain(nc.vector.tensor_copy(cum[:], tiles[:]))
    for e in range(1, NE):
        chain(nc.vector.tensor_tensor(cum[:, e:e + 1], cum[:, e - 1:e], tiles[:, e:e + 1], ALU.add))


def experts(nc, name, xs, ys, cnt, w1, b1T, w2, b2, k_ident, k_tiles, glu, top):
    NT = top * NB * S // TILE + NE
    NJ = HID // P
    with ExitStack() as ctx:
        sb = lambda n, s, d=F32: ctx.enter_context(nc.sbuf_tensor(f"{name}_{n}", s, d))
        ps = lambda n, s: ctx.enter_context(nc.psum_tensor(f"{name}_{n}", s, F32))
        sem = semaphores_of(nc, ctx, name + "_")
        I32 = mybir.dt.int32
        ident = sb("ident", [P, P])
        ids = sb("ids", [1, NT])
        cn = sb("cn", [1, NE])
        cni = sb("cni", [1, NE], I32)
        cnt_t = sb("cnt_t", [1, NE])
        cum = sb("cum", [1, NE])
        hit = sb("hit", [1, 2, NE, NT])
        who = sb("who", [1, NT])
        first = sb("first", [1, NT])
        rowf = sb("rowf", [1, NT])
        plan = sb("plan", [1, 2, NT], I32)
        xt = [sb(f"xt{i}", [P, 2, D]) for i in range(DEEP)]
        w1s = [sb(f"w1s{i}", [P, HID * (2 if glu else 1)]) for i in range(DEEP)]
        w2s = [sb(f"w2s{i}", [P, NJ, D]) for i in range(DEEP)]
        b1s = [sb(f"b1s{i}", [P, NJ * (2 if glu else 1)]) for i in range(DEEP)]
        b2s = [sb(f"b2s{i}", [P, D]) for i in range(DEEP)]
        xT = [sb(f"xT{i}", [P, TILE]) for i in range(2)]
        act_out = [sb(f"act_out{i}", [P, NJ, TILE]) for i in range(2)]
        sig = [sb(f"sig{i}", [P, NJ, TILE]) for i in range(2)] if glu else None
        ysb = [sb(f"ysb{i}", [P, 2, D]) for i in range(2)]
        pT = [ps(f"pT{i}", [P, 512]) for i in range(2)]
        phid = [ps(f"phid{j}", [P, 2, TILE]) for j in range(NJ)]
        py = [ps(f"py{i}", [P, 512]) for i in range(2)]
        const_in, planned, chain_s, turned, xT_ready, hidden, sig_ready, act_ready, y_full, y_ready = (
            sem(n) for n in ("const_in", "planned", "chain", "turned", "xT_ready", "hidden", "sig_ready",
                             "act_ready", "y_full", "y_ready"))
        loaded = [sem(f"loaded{i}") for i in range(DEEP)]
        stored = [sem(f"stored{i}") for i in range(2)]
        tick = {e: sem("tick_" + e) for e in ("pe", "dve", "act", "pool", "sp")}
        LOADS = 16 * 5

        with nc.Block() as block:
            @block.sync
            def _(sp):
                def hold(s, v):
                    sp.wait_ge(s, v)
                    sp.sem_inc(tick["sp"], 1)

                sp.dma_start(ident[:], k_ident).then_inc(const_in, 16)
                sp.dma_start(ids[:], k_tiles[0:NT].unsqueeze(0)).then_inc(const_in, 16)
                sp.dma_start(cn[:], cnt).then_inc(const_in, 16)
                sp.wait_ge(planned, 1)
                sp.sem_inc(y_ready, DEEP)
                with sp.Fori(0, NT // DEEP) as i:
                    i = sp.snap(i)
                    for par in range(DEEP):
                        t = DEEP * i + par
                        row = sp.value_load(plan[0:1, 0, bass.ds(t, 1)], min_val=0, max_val=(NE + 1) * REGION - TILE)
                        ex = sp.value_load(plan[0:1, 1, bass.ds(t, 1)], min_val=0, max_val=NE - 1)
                        hold(y_ready, t + 1)
                        sp.dma_start(xt[par][:], xs[bass.ds(row, TILE), :].rearrange("(c p) d -> p c d", p=P))\
                            .then_inc(loaded[par], 16)
                        sp.dma_start(w1s[par][:], w1[ex]).then_inc(loaded[par], 16)
                        sp.dma_start(b1s[par][:], b1T[ex]).then_inc(loaded[par], 16)
                        sp.dma_start(w2s[par][:], w2[ex].rearrange("(j p) d -> p j d", p=P)).then_inc(loaded[par], 16)
                        sp.dma_start(b2s[par][:], b2[ex].unsqueeze(0).to_broadcast([P, D])).then_inc(loaded[par], 16)

            @block.tensor
            def _(pe):
                def hold(s, v):
                    pe.wait_ge(s, v)
                    pe.sem_inc(tick["pe"], 1)

                pe.wait_ge(const_in, 48)
                pe.sem_inc(act_ready, NJ * 2)

                def turn(i, t, q):
                    hold(loaded[q % DEEP], LOADS * (i + q // DEEP + 1))
                    for c in range(2):
                        last = nc.tensor.transpose(pT[q % 2][:, c * P:(c + 1) * P], xt[q % DEEP][:, c, :], ident[:])
                    last.then_inc(turned, 1)

                def up(t, q):
                    hold(xT_ready, t + 1)
                    w = w1s[q % DEEP]
                    for j in range(NJ):
                        hold(act_ready, NJ * (t + 1) + j + 1)
                        last = nc.tensor.matmul(phid[j][:, 0, :], w[:, j * P:(j + 1) * P], xT[q % 2][:],
                                                start=True, stop=True, skip_group_check=True)
                        if glu:
                            o = HID + j * P
                            last = nc.tensor.matmul(phid[j][:, 1, :], w[:, o:o + P], xT[q % 2][:],
                                                    start=True, stop=True, skip_group_check=True)
                        last.then_inc(hidden, 1)

                def down(t, q):
                    hold(y_ready, DEEP + t - 1)
                    for j in range(NJ):
                        hold(act_ready, NJ * (t + 2) + j + 1)
                        for c in range(2):
                            last = nc.tensor.matmul(py[q % 2][:, c * D:(c + 1) * D],
                                                    act_out[q % 2][:, j, c * P:(c + 1) * P],
                                                    w2s[q % DEEP][:, j, :], start=(j == 0 and c == 0), stop=(j == NJ - 1),
                                                    skip_group_check=True)
                    last.then_inc(y_full, 1)

                def steps(i, end=False):
                    for q in range(DEEP):
                        t = DEEP * i + q
                        if not end or q + 2 < DEEP:
                            turn(i, t + 2, q + 2)
                        if not end or q + 1 < DEEP:
                            up(t + 1, q + 1)
                        down(t, q)

                turn(0, 0, 0)
                up(0, 0)
                turn(0, 1, 1)
                with pe.Fori(0, NT // DEEP - 1) as i:
                    steps(pe.snap(i))
                steps(NT // DEEP - 1, True)

            @block.scalar
            def _(act):
                def hold(s, v):
                    act.wait_ge(s, v)
                    act.sem_inc(tick["act"], 1)

                with act.Fori(0, NT // DEEP) as i:
                    i = act.snap(i)
                    for q in range(DEEP):
                        t, par = DEEP * i + q, q % 2
                        for j in range(NJ):
                            hold(hidden, NJ * t + j + 1)
                            if glu:
                                nc.scalar.activation(sig[par][:, j, :], phid[j][:, 1, :], ACT.Sigmoid,
                                                     bias=b1s[q][:, NJ + j:NJ + j + 1]).then_inc(sig_ready, 1)
                            else:
                                nc.scalar.activation(act_out[par][:, j, :], phid[j][:, 0, :], ACT.Gelu,
                                                     bias=b1s[q][:, j:j + 1]).then_inc(act_ready, 1)

            @block.vector
            def _(dve):
                def hold(s, v):
                    dve.wait_ge(s, v)
                    dve.sem_inc(tick["dve"], 1)

                chain = Chain(dve, chain_s, tick["dve"])
                chain.start(0)
                dve.wait_ge(const_in, 48)
                tiles_before(nc, chain, cn, cni, cnt_t, cum)
                for e in range(NE):
                    nc.vector.tensor_scalar(hit[:, 0, e, :], ids[:], cum[:, e:e + 1], None, ALU.is_ge)
                    last = nc.vector.tensor_scalar(hit[:, 1, e, :], ids[:], cum[:, e:e + 1], cnt_t[:, e:e + 1], ALU.is_ge,
                                                   ALU.mult)
                chain(last)
                nc.vector.tensor_reduce(who[:], hit[:, 0].rearrange("p e t -> p t e"), AX.X, ALU.add)
                chain(nc.vector.tensor_reduce(first[:], hit[:, 1].rearrange("p e t -> p t e"), AX.X, ALU.add))
                chain(nc.vector.tensor_tensor(rowf[:], ids[:], first[:], ALU.subtract))
                chain(nc.vector.tensor_scalar(rowf[:], rowf[:], float(TILE), None, ALU.mult))
                chain(nc.vector.scalar_tensor_tensor(out=rowf[:], in0=who[:], scalar=float(REGION), in1=rowf[:],
                                                     op0=ALU.mult, op1=ALU.add))
                nc.vector.tensor_copy(plan[:, 0, :], rowf[:])
                nc.vector.tensor_scalar(plan[:, 1, :], who[:], float(NE - 1), None, ALU.min).then_inc(planned, 1)

                def turn(t, q):
                    hold(turned, t + 1)
                    nc.vector.tensor_copy(xT[q % 2][:], pT[q % 2][:, 0:TILE]).then_inc(xT_ready, 1)

                def up(t, q):
                    for j in range(NJ if glu else 0):
                        hold(sig_ready, NJ * t + j + 1)
                        nc.vector.scalar_tensor_tensor(out=act_out[q % 2][:, j, :], in0=phid[j][:, 0, :],
                                                       scalar=b1s[q % DEEP][:, j:j + 1], in1=sig[q % 2][:, j, :],
                                                       op0=ALU.add, op1=ALU.mult).then_inc(act_ready, 1)

                def down(i, t, q):
                    hold(y_full, t + 1)
                    if later(i) or q >= 2:
                        hold(stored[q % 2], 16 * (DEEP // 2 * i + q // 2))
                    nc.vector.tensor_tensor(ysb[q % 2][:], py[q % 2][:, 0:2 * D].rearrange("p (c d) -> p c d", c=2),
                                            b2s[q][:].unsqueeze(1).to_broadcast([P, 2, D]), ALU.add)\
                        .then_inc(y_ready, 1)

                def steps(i, end=False):
                    for q in range(DEEP):
                        t = DEEP * i + q
                        if not end or q + 2 < DEEP:
                            turn(t + 2, q + 2)
                        if not end or q + 1 < DEEP:
                            up(t + 1, q + 1)
                        down(i, t, q)

                turn(0, 0)
                up(0, 0)
                turn(1, 1)
                steps(0)
                with dve.Fori(1, NT // DEEP - 1) as i:
                    steps(dve.snap(i))
                steps(NT // DEEP - 1, True)

            @block.gpsimd
            def _(pool):
                def hold(s, v):
                    pool.wait_ge(s, v)
                    pool.sem_inc(tick["pool"], 1)

                pool.wait_ge(planned, 1)
                with pool.Fori(0, NT // 2) as i:
                    i = pool.snap(i)
                    for par in range(2):
                        t = 2 * i + par
                        hold(y_ready, DEEP + t + 1)
                        pool.dma_start(ys[bass.ds(t * TILE, TILE), :].rearrange("(c p) d -> p c d", p=P), ysb[par][:])\
                            .then_inc(stored[par], 16)
                for par in range(2):
                    pool.wait_ge(stored[par], 16 * (NT // 2))


def combine(nc, name, x, xo, ys, pos_in, weight_in, cnt, gates, k_iota, k_base, top):
    with ExitStack() as ctx:
        sb = lambda n, s, d=F32: ctx.enter_context(nc.sbuf_tensor(f"{name}_{n}", s, d))
        sem = semaphores_of(nc, ctx, name + "_")
        U32 = mybir.dt.uint32
        xin = [sb(f"xin{i}", [P, NC, D]) for i in range(2)]
        place = [sb(f"place{i}", [P, 2, NC, top]) for i in range(2)]
        pos = [sb(f"pos{i}", [P, NC, top], U32) for i in range(2)]
        iota = sb("iota", [P, NC, NE])
        cn = sb("cn", [P, NE])
        cni = sb("cni", [P, NE], mybir.dt.int32)
        tiles = sb("tiles", [P, NE])
        cum = sb("cum", [P, NE])
        base = sb("base", [P, NE])
        move = sb("move", [P, NE])
        hot = sb("hot", [P, top, NC, NE])
        add = sb("add", [P, NC, top])
        wts = [sb(f"wts{i}", [P, NC, 2]) for i in range(2)]
        gate = [sb(f"gate{i}", [P, D]) for i in range(2)]
        y = [sb(f"y{i}", [P, NC, top, D]) for i in range(2)]
        acc = sb("acc", [P, NC, D])
        out = [sb(f"out{i}", [P, NC, D]) for i in range(2)]
        loaded, pos_in_s, gathered, stored = ([sem(f"{n}{i}") for i in range(2)]
                                              for n in ("loaded", "pos", "gathered", "stored"))
        chain_s, done, const_in, pos_ready = (sem(n) for n in ("chain", "done", "const_in", "pos_ready"))
        tick = {e: sem("tick_" + e) for e in ("dve", "pool", "sp", "act")}
        LOADS = 16 * (2 + (top == 2))
        with nc.Block() as block:
            @block.sync
            def _(sp):
                def hold(s, v):
                    sp.wait_ge(s, v)
                    sp.sem_inc(tick["sp"], 1)

                sp.dma_start(iota[:], k_iota.unsqueeze(0).to_broadcast([P, NC, NE])).then_inc(const_in, 16)
                sp.dma_start(base[:], k_base.unsqueeze(0).to_broadcast([P, NE])).then_inc(const_in, 16)
                sp.dma_start(cn[:], cnt[0].unsqueeze(0).to_broadcast([P, NE])).then_inc(const_in, 16)
                sp.sem_inc(done, 2)
                with sp.Fori(0, NB // 2) as i:
                    i = sp.snap(i)
                    for par in range(2):
                        b = 2 * i + par
                        hold(done, b + 1)
                        sp.dma_start(place[par][:], pos_in[b]).then_inc(pos_in_s[par], 16)
                        sp.dma_start(xin[par][:], x[b].rearrange("(c p) d -> p c d", p=P)).then_inc(loaded[par], 16)
                        sp.dma_start(gate[par][:], gates[b].unsqueeze(0).to_broadcast([P, D])).then_inc(loaded[par], 16)
                        if top == 2:
                            sp.dma_start(wts[par][:], weight_in[b]).then_inc(loaded[par], 16)

            @block.gpsimd
            def _(pool):
                def hold(s, v):
                    pool.wait_ge(s, v)
                    pool.sem_inc(tick["pool"], 1)

                with pool.Fori(0, NB // 2) as i:
                    i = pool.snap(i)
                    for par in range(2):
                        hold(pos_ready, 2 * i + par + 1)
                        for c in range(NC):
                            for k in range(top):
                                nc.gpsimd.indirect_dma_start(
                                    out=y[par][:, c, k, :], out_offset=None, in_=ys[:, :],
                                    in_offset=bass.IndirectOffsetOnAxis(ap=pos[par][:, c, k:k + 1], axis=0))\
                                    .then_inc(gathered[par], 16)

            @block.vector
            def _(dve):
                def hold(s, v):
                    dve.wait_ge(s, v)
                    dve.sem_inc(tick["dve"], 1)

                chain = Chain(dve, chain_s, tick["dve"])
                for par in range(2):
                    dve.sem_inc(stored[par], 16)
                dve.wait_ge(const_in, 48)
                chain.start(0)
                tiles_before(nc, chain, cn, cni, tiles, cum)
                chain(nc.vector.tensor_tensor(move[:], cum[:], tiles[:], ALU.subtract))
                chain(nc.vector.scalar_tensor_tensor(out=move[:], in0=move[:], scalar=float(TILE), in1=base[:],
                                                     op0=ALU.mult, op1=ALU.subtract))
                setup = chain.count
                CHAIN = 4 + (3 if top == 2 else 1)
                with dve.Fori(0, NB // 2) as i:
                    i = dve.snap(i)
                    for par in range(2):
                        b = 2 * i + par
                        chain.start(CHAIN * b + setup)
                        hold(pos_in_s[par], 16 * i + 16)
                        for k in range(top):
                            last = nc.vector.tensor_tensor(hot[:, k], iota[:], place[par][:, 1, :, k].unsqueeze(2)
                                                           .to_broadcast([P, NC, NE]), ALU.is_equal)
                        chain(last)
                        for k in range(top):
                            last = nc.vector.tensor_tensor(hot[:, k], hot[:, k], move[:].unsqueeze(1)
                                                           .to_broadcast([P, NC, NE]), ALU.mult)
                        chain(last)
                        for k in range(top):
                            last = nc.vector.tensor_reduce(add[:, :, k], hot[:, k], AX.X, ALU.add)
                        chain(last)
                        chain(nc.vector.tensor_tensor(pos[par][:], add[:], place[par][:, 0], ALU.add))
                        dve.sem_inc(pos_ready, 1)
                        hold(loaded[par], LOADS * i + LOADS)
                        hold(gathered[par], 16 * NC * top * (i + 1))
                        src = y[par][:, :, 0, :]
                        if top == 2:
                            for c in range(NC):
                                last = nc.vector.tensor_scalar(acc[:, c, :], y[par][:, c, 0, :], wts[par][:, c, 0:1], None,
                                                               ALU.mult)
                            chain(last)
                            for c in range(NC):
                                last = nc.vector.scalar_tensor_tensor(out=acc[:, c, :], in0=y[par][:, c, 1, :],
                                                                      scalar=wts[par][:, c, 1:2], in1=acc[:, c, :],
                                                                      op0=ALU.mult, op1=ALU.add)
                            chain(last)
                            src = acc[:]
                        hold(stored[par], 16 * i + 16)
                        chain(nc.vector.tensor_tensor(out[par][:], src, gate[par][:].unsqueeze(1).to_broadcast([P, NC, D]),
                                                      ALU.mult))
                        nc.vector.tensor_tensor(out[par][:], out[par][:], xin[par][:], ALU.add).then_inc(done, 1)

            @block.scalar
            def _(act):
                def hold(s, v):
                    act.wait_ge(s, v)
                    act.sem_inc(tick["act"], 1)

                with act.Fori(0, NB // 2) as i:
                    i = act.snap(i)
                    for par in range(2):
                        hold(done, 2 * i + par + 3)
                        act.dma_start(xo[2 * i + par].rearrange("(c p) d -> p c d", p=P), out[par][:])\
                            .then_inc(stored[par], 16)
                for par in range(2):
                    act.wait_ge(stored[par], 16 * (NB // 2 + 1))


WIN = 32
NBLK = S // WIN
UNITS = 8
BPU = NBLK // 2
AHEAD = 3


def window_attention(nc, x, xo, cols, gates, w_qkv, w_out, k_ident, k_head, k_band):
    with ExitStack() as ctx:
        sb = lambda n, s, d=F32: ctx.enter_context(nc.sbuf_tensor("wa_" + n, s, d))
        ps = lambda n, s: ctx.enter_context(nc.psum_tensor("wa_" + n, s, F32))
        sem = semaphores_of(nc, ctx, "wa_")
        ident = sb("ident", [P, P])
        head = sb("head", [P, 4])
        band = sb("band", [P, 2, BPU, 2 * WIN])
        wqkv = sb("wqkv", [P, 3 * D])
        wout = sb("wout", [P, D])
        half = sb("half", [P, NC])
        xin = [sb(f"xin{i}", [P, NC, D]) for i in range(2)]
        xres = [sb(f"xres{i}", [P, NC, D]) for i in range(2)]
        mcol = [sb(f"mcol{i}", [P, 4]) for i in range(2)]
        gate = [sb(f"gate{i}", [P, D]) for i in range(2)]
        stat = sb("stat", [P, NC, 6])
        mv = sb("mv", [P, NC, 2])
        rstd = sb("rstd", [P, NC])
        nmr = sb("nmr", [P, NC])
        xn = sb("xn", [P, NC, D])
        hT = sb("hT", [P, WIN + S])
        qT = sb("qT", [P, S])
        qm = [sb(f"qm{i}", [P, NBLK, D // HD, WIN]) for i in range(2)]
        kT = [sb(f"kT{i}", [P, WIN + S]) for i in range(2)]
        vw = [sb(f"vw{i}", [P, NBLK // 2, 2, D]) for i in range(2)]
        s = [sb(f"s{i}", [P, BPU, 2 * WIN]) for i in range(4)]
        mx = [sb(f"mx{i}", [P, BPU]) for i in range(4)]
        sm = sb("sm", [P, 2, 4, BPU])
        pT = [sb(f"pT{i}", [P, 4, P]) for i in range(2)]
        otok = sb("otok", [P, NC, D])
        oT = sb("oT", [P, S])
        xout = [sb(f"xout{i}", [P, NC, D]) for i in range(2)]
        psc = [ps(f"psc{i}", [P, BPU, 2 * WIN]) for i in range(4)]
        ptr = ps("ptr", [P, 4, P])
        pov = ps("pov", [P, 4, 4, 2, 4 * HD])
        pmisc = ps("pmisc", [P, S])

        names = ("const_in", "cleared", "stats", "rstd_ready", "nmr_ready", "xn_ready", "misc_full", "misc_free",
                 "ht_ready", "kv_ready", "scored", "masked", "lowered", "exped", "summed", "turned", "pT_ready",
                 "weighed", "unpacked", "otok_ready", "oT_ready", "xout_ready", "recip", "gated", "q_ready", "qT_ready")
        (const_in, cleared, stats, rstd_ready, nmr_ready, xn_ready, misc_full, misc_free, ht_ready, kv_ready, scored,
         masked, lowered, exped, summed, turned, pT_ready, weighed, unpacked, otok_ready, oT_ready, xout_ready, recip,
         gated, q_ready, qT_ready) = (sem(n) for n in names)
        loaded = [sem(f"loaded{i}") for i in range(2)]
        kept = [sem(f"kept{i}") for i in range(2)]
        stored = [sem(f"stored{i}") for i in range(2)]
        tick = {e: sem("tick_" + e) for e in ("pe", "dve", "act", "pool", "sp")}

        ORDER = ["T2p", "WOp", "h", "q", "k", "v0", "v1"]
        PRO = ["h", "q", "k", "v0", "v1"]

        class Body:

            def __init__(self, b, half, par, at, prev=True, nxt=True):
                self.b, self.half, self.par, self.at, self.prev, self.nxt = b, half, par, at, prev, nxt
                self.uses = [n for n in ORDER if (prev or n not in ("T2p", "WOp")) and (nxt or n in ("T2p", "WOp"))]

            def nth(self, d):
                return self.half + (self.par + d) // 2

            def use(self, name):
                return self.at + self.uses.index(name)

        def batches(eng, body):
            at1 = 2 * len(PRO)
            body(Body(0, 0, 0, len(PRO), prev=False))
            with eng.Fori(0, (NB - 2) // 2) as i:
                i = eng.snap(i)
                body(Body(2 * i + 1, i, 1, 2 * len(ORDER) * i + at1))
                body(Body(2 * i + 2, i + 1, 0, 2 * len(ORDER) * i + at1 + len(ORDER)))
            at = at1 + (NB - 2) * len(ORDER)
            body(Body(NB - 1, NB // 2 - 1, 1, at, nxt=False))
            return at + 2

        with nc.Block() as block:
            @block.sync
            def _(sp):
                def hold(s_, v):
                    sp.wait_ge(s_, v)
                    sp.sem_inc(tick["sp"], 1)

                for dst, src in ((ident[:], k_ident), (head[:], k_head), (band[:], k_band), (wqkv[:], w_qkv),
                                 (wout[:], w_out)):
                    sp.dma_start(dst, src).then_inc(const_in, 16)

                def load(p, par):
                    if not isinstance(p, int) or p >= 2:
                        hold(ht_ready, p - 1)
                    sp.dma_start(xin[par][:], x[p].rearrange("(c p) d -> p c d", p=P)).then_inc(loaded[par], 16)
                    sp.dma_start(mcol[par][:], cols[p]).then_inc(loaded[par], 16)

                def load_residual(p, par):
                    if not isinstance(p, int) or p >= 2:
                        hold(xout_ready, p - 1)
                    sp.dma_start(xres[par][:], x[p].rearrange("(c p) d -> p c d", p=P)).then_inc(kept[par], 16)
                    sp.dma_start(gate[par][:], gates[p].unsqueeze(0).to_broadcast([P, D])).then_inc(kept[par], 16)

                def store(b, par):
                    hold(xout_ready, b + 1)
                    sp.dma_start(xo[b].rearrange("(c p) d -> p c d", p=P), xout[par][:]).then_inc(stored[par], 16)

                load(0, 0)
                load(1, 1)
                load_residual(0, 0)
                load_residual(1, 1)

                def body(k):
                    if k.prev:
                        if k.nxt:
                            load(k.b + 1, 1 - k.par)
                        store(k.b - 1, 1 - k.par)
                        if k.nxt:
                            load_residual(k.b + 1, 1 - k.par)

                batches(sp, body)
                store(NB - 1, 1)
                for par in range(2):
                    sp.wait_ge(stored[par], 16 * (NB // 2))

            @block.tensor
            def _(pe):
                def hold(s_, v):
                    pe.wait_ge(s_, v)
                    pe.sem_inc(tick["pe"], 1)

                def misc(n):
                    if not isinstance(n, int) or n > 0:
                        hold(misc_free, n)

                def four(src, n):
                    misc(n)
                    for c in range(NC):
                        last = nc.tensor.transpose(pmisc[:, c * P:(c + 1) * P], src[:, c, :], ident[:])
                    last.then_inc(misc_full, 1)

                def turn_x(p, n):
                    hold(xn_ready, p + 1)
                    four(xn, n)

                def project(p, which, n):
                    if which == 0:
                        hold(ht_ready, p + 1)
                    misc(n)
                    nc.tensor.matmul(pmisc[:], wqkv[:, which * D:(which + 1) * D], hT[:, WIN:], start=True, stop=True)\
                        .then_inc(misc_full, 1)

                def values(q, n):
                    misc(n)
                    for m in range(4):
                        for w in range(2):
                            o = WIN * (2 * (4 * q + m) + w)
                            last = nc.tensor.matmul(pmisc[64 * w:64 * w + 64, m * D:(m + 1) * D], hT[:, o:o + 2 * WIN],
                                                    wqkv[:, 2 * D:3 * D], start=True, stop=True, skip_group_check=True)
                    last.then_inc(misc_full, 1)

                def scores(b, par, u):
                    n = UNITS * b + u
                    g, h2 = u % 4, u // 4
                    if u == 0:
                        hold(kv_ready, b + 1)
                    if u < 4:
                        hold(q_ready, 4 * b + u + 1)
                    if not isinstance(n, int) or n >= 4:
                        hold(masked, n - 3)
                    for i in range(BPU):
                        blk = BPU * h2 + i
                        last = nc.tensor.matmul(psc[g][:, i, :], qm[par][:, blk, 4 * g:4 * g + 4].rearrange("p j q -> p (j q)"),
                                                kT[par][:, WIN * blk:WIN * blk + 2 * WIN], start=True, stop=True,
                                                skip_group_check=True)
                    last.then_inc(scored, 1)

                def turn_p(b, u):
                    n = UNITS * b + u
                    hold(exped, n + 1)
                    if not isinstance(n, int) or n >= 1:
                        hold(pT_ready, n)
                    for m in range(4):
                        last = nc.tensor.transpose(ptr[:, m, :], s[u % 4][:, 2 * m:2 * m + 2, :]
                                                   .rearrange("p b k -> p (b k)"), ident[:])
                    last.then_inc(turned, 1)

                def weigh(b, par, u):
                    n = UNITS * b + u
                    g, h2 = u % 4, u // 4
                    hold(pT_ready, n + 1)
                    if g == 0 and (not isinstance(b, int) or 2 * b + h2 >= 1):
                        hold(unpacked, 2 * b + h2)
                    for m in range(4):
                        last = nc.tensor.matmul(pov[:, g, m], pT[u % 2][:, m, :],
                                                vw[par][:, 4 * h2 + m, :, 32 * g:32 * g + 32], start=True, stop=True,
                                                skip_group_check=True)
                    last.then_inc(weighed, 1)

                def project_out(b, n):
                    hold(oT_ready, b + 1)
                    misc(n)
                    for c in range(NC):
                        last = nc.tensor.matmul(pmisc[:, c * P:(c + 1) * P], oT[:, c * P:(c + 1) * P], wout[:],
                                                start=True, stop=True)
                    last.then_inc(misc_full, 1)

                pe.wait_ge(const_in, 80)
                pe.wait_ge(cleared, 2)
                turn_x(0, 0)
                project(0, 0, 1)
                project(0, 1, 2)
                values(0, 3)
                values(1, 4)
                for u in range(AHEAD):
                    scores(0, 0, u)

                def body(k):
                    b, par = k.b, k.par
                    for u in range(UNITS):
                        v = u + AHEAD
                        if v < UNITS:
                            scores(b, par, v)
                        elif k.nxt:
                            scores(b + 1, 1 - par, v - UNITS)
                        turn_p(b, u)
                        if u > 0:
                            weigh(b, par, u - 1)
                        elif k.prev:
                            weigh(b - 1, 1 - par, UNITS - 1)
                        if u == 1:
                            if k.prev:
                                hold(otok_ready, b)
                                four(otok, k.use("T2p"))
                        if u == 2:
                            if k.prev:
                                project_out(b - 1, k.use("WOp"))
                            if k.nxt:
                                turn_x(b + 1, k.use("h"))
                        if k.nxt and u == 3:
                            project(b + 1, 0, k.use("q"))
                            project(b + 1, 1, k.use("k"))
                        if k.nxt and u == 4:
                            values(0, k.use("v0"))
                            values(1, k.use("v1"))

                at = batches(pe, body)
                weigh(NB - 1, 1, UNITS - 1)
                hold(otok_ready, NB)
                four(otok, at)
                project_out(NB - 1, at + 1)

            @block.scalar
            def _(act):
                def hold(s_, v):
                    act.wait_ge(s_, v)
                    act.sem_inc(tick["act"], 1)

                def after(s_from, value, s_to):
                    hold(s_from, value)
                    act.sem_inc(s_to, 1)

                def normalise(p, par):
                    hold(nmr_ready, p + 1)
                    if not isinstance(p, int) or p >= 1:
                        hold(ht_ready, p)
                    for c in range(NC):
                        last = nc.scalar.activation(xn[:, c, :], xin[par][:, c, :], ACT.Identity,
                                                    bias=nmr[:, c:c + 1], scale=rstd[:, c:c + 1])
                    last.then_inc(xn_ready, 1)

                def modulate(p, par, n):
                    hold(misc_full, n + 1)
                    nc.scalar.activation(hT[:, WIN:], pmisc[:], ACT.Identity, bias=mcol[par][:, 0:1],
                                         scale=mcol[par][:, 1:2]).then_inc(misc_free, 1)
                    after(misc_free, n + 1, ht_ready)

                def keep(dst, src, n):
                    hold(misc_full, n + 1)
                    nc.scalar.activation(dst, src, ACT.Copy).then_inc(misc_free, 1)

                def rest(p, par, at):
                    if not isinstance(p, int) or p >= 1:
                        hold(q_ready, 4 * p)
                    hold(misc_full, at + 2)
                    nc.scalar.activation(qT[:], pmisc[:], ACT.Copy).then_inc(misc_free, 1)
                    after(misc_free, at + 2, qT_ready)
                    keep(kT[par][:, WIN:], pmisc[:], at + 2)

                def vals(p, par, at):
                    for q in range(2):
                        hold(misc_full, at + q + 1)
                        for w in range(2):
                            rows = slice(64 * w, 64 * w + 64)
                            last = nc.scalar.activation(vw[par][rows, 4 * q:4 * q + 4, w, :],
                                                        pmisc[rows].rearrange("p (m d) -> p m d", m=4), ACT.Copy)
                        last.then_inc(misc_free, 1)
                    after(misc_free, at + 2, kv_ready)

                def exponentials(b, u):
                    hold(lowered, UNITS * b + u + 1)
                    nc.scalar.activation(s[u % 4][:], s[u % 4][:], ACT.Exp).then_inc(exped, 1)

                def keep_turned(b, u):
                    n = UNITS * b + u
                    hold(turned, n + 1)
                    if not isinstance(n, int) or n >= 2:
                        hold(weighed, n - 1)
                    nc.scalar.activation(pT[u % 2][:], ptr[:], ACT.Copy).then_inc(pT_ready, 1)

                act.wait_ge(const_in, 80)
                act.wait_ge(cleared, 2)
                normalise(0, 0)
                modulate(0, 0, 0)
                rest(0, 0, 0)
                vals(0, 0, 3)
                exponentials(0, 0)

                def body(k):
                    b, par = k.b, k.par
                    for u in range(UNITS):
                        if u + 1 < UNITS:
                            exponentials(b, u + 1)
                        elif k.nxt:
                            exponentials(b + 1, 0)
                        keep_turned(b, u)
                        if u == 0 and k.nxt:
                            normalise(b + 1, 1 - par)
                        if u == 1 and k.prev:
                            keep(oT[:], pmisc[:], k.use("T2p"))
                            after(misc_free, k.use("T2p") + 1, oT_ready)
                        if u == 2 and k.nxt:
                            modulate(b + 1, 1 - par, k.use("h"))
                        if u == 3 and k.nxt:
                            rest(b + 1, 1 - par, k.use("q") - 1)
                        if u == 4 and k.nxt:
                            vals(b + 1, 1 - par, k.use("v0"))

                at = batches(act, body)
                keep(oT[:], pmisc[:], at)
                after(misc_free, at + 1, oT_ready)

            @block.vector
            def _(dve):
                def hold(s_, v):
                    dve.wait_ge(s_, v)
                    dve.sem_inc(tick["dve"], 1)

                nc.vector.memset(half[:], -0.5)
                nc.vector.memset(hT[:, 0:WIN], 0.0)
                for par in range(2):
                    nc.vector.memset(kT[par][:, 0:WIN], 0.0)
                    nc.vector.memset(vw[par][:], 0.0)
                nc.vector.memset(qm[0][:], 0.0).then_inc(cleared, 1)
                dve.wait_ge(const_in, 80)
                dve.wait_ge(cleared, 2)

                def statistics(p, par, nth):
                    hold(loaded[par], 32 * nth + 32)
                    if not isinstance(p, int) or p >= 1:
                        hold(xn_ready, p)
                    for c in range(NC):
                        last = nc.vector.bn_stats(stat[:, c, :], xin[par][:, c, :])
                    last.then_inc(stats, 1)
                    hold(stats, 3 * p + 1)
                    for c in range(NC):
                        last = nc.vector.bn_aggr(mv[:, c, :], stat[:, c, :])
                    last.then_inc(stats, 1)
                    hold(stats, 3 * p + 2)
                    nc.vector.tensor_scalar(mv[:, :, 1], mv[:, :, 1], LN_EPS, None, ALU.add).then_inc(stats, 1)

                def shift(p):
                    hold(rstd_ready, p + 1)
                    nc.vector.scalar_tensor_tensor(out=nmr[:], in0=mv[:, :, 0], scalar=-1.0, in1=rstd[:],
                                                   op0=ALU.mult, op1=ALU.mult).then_inc(nmr_ready, 1)

                def by_head(p, par, g):
                    hold(qT_ready, p + 1)
                    rows = slice(32 * g, 32 * g + 32)
                    for j in range(4):
                        last = nc.vector.tensor_scalar(qm[par][rows, :, 4 * g + j, :],
                                                       qT[rows].rearrange("p (b q) -> p b q", q=WIN),
                                                       head[rows, j:j + 1], None, ALU.mult)
                    last.then_inc(q_ready, 1)

                def mask(b, u):
                    n = UNITS * b + u
                    hold(scored, n + 1)
                    if not isinstance(n, int) or n >= 4:
                        hold(turned, n - 3)
                        hold(summed, n - 3)
                    nc.vector.scalar_tensor_tensor(out=s[u % 4][:], in0=psc[u % 4][:], scalar=1.0 / float(np.sqrt(HD)),
                                                   in1=band[:, u // 4], op0=ALU.mult, op1=ALU.add).then_inc(masked, 1)
                    hold(masked, n + 1)
                    nc.vector.tensor_reduce(mx[u % 4][:], s[u % 4][:], AX.X, ALU.max)\
                        .then_inc(gated, 1)

                def total(b, u):
                    n = UNITS * b + u
                    hold(exped, n + 1)
                    if u % 4 == 0 and (not isinstance(b, int) or b >= 1):
                        hold(unpacked, 2 * b + u // 4 - 1)
                    nc.vector.tensor_reduce(sm[:, u // 4, u % 4, :], s[u % 4][:], AX.X, ALU.add).then_inc(summed, 1)

                def unpack(b, h2):
                    n = 2 * b + h2
                    hold(summed, 4 * n + 4)
                    nc.vector.reciprocal(sm[:, h2], sm[:, h2]).then_inc(recip, 1)
                    hold(recip, n + 1)
                    hold(weighed, 4 * n + 4)
                    if h2 == 0 and (not isinstance(b, int) or b >= 1):
                        hold(oT_ready, b)
                    for j in range(4):
                        src = slice(32 * j, 32 * j + 32)
                        for w in range(2):
                            for m2 in range(2):
                                o = 32 * (2 * m2 + w)
                                last = nc.vector.tensor_tensor(
                                    otok[o:o + 32, 2 * h2:2 * h2 + 2, :].rearrange("p c (g f) -> p g c f", g=4)
                                    [:, :, :, 8 * j:8 * j + 8],
                                    pov[src, :, m2::2, w, 8 * j:8 * j + 8],
                                    sm[src, h2, :, 2 * m2 + w::4].unsqueeze(3).to_broadcast([32, 4, 2, HD]), ALU.mult)
                    last.then_inc(unpacked, 1)
                    if h2 == 1:
                        hold(unpacked, n + 1)
                        dve.sem_inc(otok_ready, 1)

                def residual(b, par, nth, n):
                    hold(misc_full, n + 1)
                    hold(kept[par], 32 * nth + 32)
                    if not isinstance(nth, int) or nth >= 1:
                        hold(stored[par], 16 * nth)
                    nc.vector.tensor_tensor(xout[par][:], pmisc[:].rearrange("p (c d) -> p c d", c=NC),
                                            gate[par][:].unsqueeze(1).to_broadcast([P, NC, D]), ALU.mult)\
                        .then_inc(misc_free, 1)
                    hold(misc_free, n + 1)
                    nc.vector.tensor_tensor(xout[par][:], xout[par][:], xres[par][:], ALU.add).then_inc(xout_ready, 1)

                statistics(0, 0, 0)
                shift(0)
                for g in range(4):
                    by_head(0, 0, g)
                for u in range(AHEAD):
                    mask(0, u)

                def body(k):
                    b, par = k.b, k.par
                    for u in range(UNITS):
                        v = u + AHEAD
                        if k.nxt and u >= 4:
                            by_head(b + 1, 1 - par, u - 4)
                        if v < UNITS:
                            mask(b, v)
                        elif k.nxt:
                            mask(b + 1, v - UNITS)
                        total(b, u)
                        if u == 0 and k.prev:
                            unpack(b - 1, 1)
                        if u == 4:
                            unpack(b, 0)
                        if u == 2 and k.prev:
                            residual(b - 1, 1 - par, k.nth(-1), k.use("WOp"))
                        if u == 0 and k.nxt:
                            statistics(b + 1, 1 - par, k.nth(1))
                            shift(b + 1)

                at = batches(dve, body)
                unpack(NB - 1, 1)
                residual(NB - 1, 1, NB // 2 - 1, at + 1)

            @block.gpsimd
            def _(pool):
                def hold(s_, v):
                    pool.wait_ge(s_, v)
                    pool.sem_inc(tick["pool"], 1)

                def deviation(p):
                    hold(stats, 3 * p + 3)
                    nc.gpsimd.tensor_tensor(rstd[:], mv[:, :, 1], half[:], ALU.pow).then_inc(rstd_ready, 1)

                def lower(b, u):
                    hold(gated, UNITS * b + u + 1)
                    nc.gpsimd.tensor_tensor(s[u % 4][:], s[u % 4][:],
                                            mx[u % 4][:].unsqueeze(2).to_broadcast([P, BPU, 2 * WIN]), ALU.subtract)\
                        .then_inc(lowered, 1)

                nc.gpsimd.memset(qm[1][:], 0.0).then_inc(cleared, 1)
                pool.wait_ge(cleared, 2)
                deviation(0)
                for u in range(AHEAD):
                    lower(0, u)

                def body(k):
                    for u in range(UNITS):
                        v = u + AHEAD
                        if v < UNITS:
                            lower(k.b, v)
                        elif k.nxt:
                            lower(k.b + 1, v - UNITS)
                        if u == 0 and k.nxt:
                            deviation(k.b + 1)

                batches(pool, body)


def program(nc, t, out):
    dram = lambda n, s, d=F32: nc.dram_tensor(n, s, d, kind="Internal").ap()
    cols = [dram(f"cols{l}", (NB, D, 4)) for l in range(2)]
    gates = [dram(f"gates{l}", (2, NB, D)) for l in range(2)]
    shifts = [dram(f"shifts{l}", (NB, 2, D)) for l in range(2)]
    xs = [dram(f"xs{l}", ((NE + 1) * REGION, D)) for l in range(2)]
    ys = [dram(f"ys{l}", (top * NB * S + NE * TILE, D)) for l, top in enumerate((2, 1))]
    cnt = [dram(f"cnt{l}", (1, NE)) for l in range(2)]
    pos = [dram(f"pos{l}", (NB, P, 2, NC, top)) for l, top in enumerate((2, 1))]
    weight = dram("weight", (NB, P, NC, 2))
    xa = dram("xa", (NB, S, D))
    xb = dram("xb", (NB, S, D))
    xc = dram("xc", (NB, S, D))

    modulation(nc, [t["c0T"], t["c1T"]], [t["L0_wmod"], t["L1_wmod"]], cols, gates, shifts)
    decayed_attention(nc, t["L0_attn_x"], xa, cols[0], gates[0][0], t["L0_attn_W_q"], t["L0_attn_W_k"],
                      t["L0_attn_W_v"], t["L0_attn_W_o"], t["L0_attn_W_down_kv"], t["L0_attn_W_up_k"],
                      t["L0_attn_W_up_v"], t["k_rows"], t["k_late"], t["k_ident"])
    route(nc, "r0", xa, shifts[0], t["router0T"], [t["L0_ffn_router_b"], t["L0_ffn_lang_b"]], t["k_ident"],
          t["k_prefix"], t["k_iota"], t["k_base"], t["k_row"], xs[0], pos[0], weight, cnt[0], 2)
    experts(nc, "e0", xs[0], ys[0], cnt[0], t["L0_ffn_w1"], t["b1T0"], t["L0_ffn_w2"], t["L0_ffn_b2"], t["k_ident"],
            t["k_tiles"], False, 2)
    combine(nc, "m0", xa, xb, ys[0], pos[0], weight, cnt[0], gates[0][1], t["k_iota"],
            t["k_base"], 2)
    window_attention(nc, xb, xc, cols[1], gates[1][0], t["L1_attn_w_qkv"], t["L1_attn_w_out"], t["k_ident"],
                     t["k_head"], t["k_band"])
    route(nc, "r1", xc, shifts[1], t["L1_ffn_router_w"], [t["L1_ffn_router_b"]], t["k_ident"], t["k_prefix"],
          t["k_iota"], t["k_base"], t["k_row"], xs[1], pos[1], None, cnt[1], 1)
    experts(nc, "e1", xs[1], ys[1], cnt[1], t["L1_ffn_w1"], t["b1T1"], t["L1_ffn_w2"], t["L1_ffn_b2"], t["k_ident"],
            t["k_tiles"], True, 1)
    combine(nc, "m1", xc, out, ys[1], pos[1], None, cnt[1], gates[1][1], t["k_iota"], t["k_base"], 1)


_OUTS = [((16, 512, 128), 'float32')]


def kernel(**inputs):
    import numpy as _np
    import concourse.bacc as _bacc
    from concourse import mybir as _mybir
    from concourse.bass_utils import run_bass_kernel_spmd as _run

    nc = _bacc.Bacc("TRN2", target_bir_lowering=False, num_devices=1)
    a = {n: _np.asarray(v) for n, v in inputs.items()}
    a["c0T"] = a.pop("L0_c").T
    a["c1T"] = a.pop("L1_c").T
    a["router0T"] = _np.concatenate([a.pop("L0_ffn_router_w"), a.pop("L0_ffn_lang_w")]).T
    for l in range(2):
        b1 = a.pop(f"L{l}_ffn_b1")
        a[f"b1T{l}"] = b1.reshape(b1.shape[0], -1, P).transpose(0, 2, 1)
    a.update(constants())
    arrays = {n: _np.ascontiguousarray(v) for n, v in a.items()}
    t = {n: nc.dram_tensor(n, v.shape, _mybir.dt.from_np(v.dtype), kind="ExternalInput").ap()
         for n, v in arrays.items()}
    out = nc.dram_tensor("out_0_dram", _OUTS[0][0], _mybir.dt.from_np(_np.dtype(_OUTS[0][1])),
                         kind="ExternalOutput").ap()
    program(nc, t, out)
    r = _run(nc, [arrays], core_ids=[0])
    return r.results[0]["out_0_dram"]
```

```python
from contextlib import ExitStack

import numpy as np

import concourse.bass as bass
from concourse import mybir

F32 = mybir.dt.float32
BF16 = mybir.dt.bfloat16
ALU = mybir.AluOpType
ACT = mybir.ActivationFunctionType
AX = mybir.AxisListType

P = 128
NB, S, D = 16, 512, 128
NH, HD = 16, 8
NC = S // P
NU = NH // 4
DL = 32
LN_EPS = 1e-5
GATE_MIN = 0.25
DECAY = 0.01
LOWEST = -3.0e38

PART_Q = (0, 0, 1, 0, 2, 1)
PART_K = (0, 1, 0, 2, 0, 1)
SIDE = 8 * len(PART_Q)
KMAX = 2 * SIDE
KEXP = KMAX + 3
LEAD = 7
STEPS = 4 * NU


def constants():
    i = np.arange(S)
    q_behind = np.exp(-DECAY * (i - S / 2)) / np.sqrt(D)
    q_before = np.exp(DECAY * (i - S / 2)) / np.sqrt(D)
    k_behind = np.exp(DECAY * (i - S / 2))
    k_before = np.exp(-DECAY * (i - S / 2))
    rows = np.stack([q_behind, q_before, k_behind, k_before]).astype(np.float32)
    width = 2 * S - P
    ahead = np.arange(width)[None, :] - np.arange(P)[:, None] - (S - P)
    late = np.exp(-2 * DECAY * np.maximum(ahead, 0)).astype(np.float32)
    ident = np.eye(P, dtype=np.float32)
    prefix = np.triu(np.ones((P, P), np.float32), 1)
    iota = np.tile(np.arange(NE, dtype=np.float32), (NC, 1))
    base = np.arange(NE, dtype=np.float32) * REGION
    row = (np.arange(P)[:, None] + np.array([[0, P]])).astype(np.float32)
    tiles = np.arange(2 * NB * S // TILE + NE, dtype=np.float32)
    head = (np.arange(P)[:, None] // HD % 4 == np.arange(4)[None, :]).astype(np.float32)
    q, k = np.arange(P)[:, None] % WIN, np.arange(2 * WIN)[None, :]
    inside = (k >= q + 1) & (k <= q + WIN)
    band = np.broadcast_to(np.where(inside, 0.0, -1e30)[:, None, None, :], (P, 2, BPU, 2 * WIN)).astype(np.float32)
    band[:, 0, 0, :] = np.where(inside & (k >= WIN), 0.0, -1e30)
    return {"k_head": head, "k_band": band, "k_rows": rows, "k_late": late, "k_ident": ident, "k_prefix": prefix, "k_iota": iota, "k_base": base,
            "k_row": row, "k_tiles": tiles}


def semaphores_of(nc, ctx, prefix):
    taken = []

    def sem(name):
        taken.append(nc.alloc_semaphore(name=prefix + name))
        return taken[-1]

    def give_back():
        nc.clear_and_free_semaphores(taken)
        nc.all_engine_barrier()

    ctx.callback(give_back)
    return sem


def modulation(nc, cT, wmod, cols, gates, shifts):
    with ExitStack() as ctx:
        sb = lambda n, s, d=F32: ctx.enter_context(nc.sbuf_tensor(n, s, d))
        sem = semaphores_of(nc, ctx, "mo_")
        c = sb("mod_c", [P, 2, NB])
        e = sb("mod_e", [P, 2, NB])
        w = sb("mod_w", [P, 2, 6 * D])
        colt = sb("mod_cols", [P, 2, NB, 4])
        g = sb("mod_g", [NB, 2, 2, D])
        sgn = sb("mod_sgn", [NB, 2, 2, D])
        mag = sb("mod_mag", [NB, 2, 2, D])
        sh = sb("mod_sh", [NB, 2, 2, D])
        pc = ctx.enter_context(nc.psum_tensor("mod_pc", [P, 512], F32))
        psh = ctx.enter_context(nc.psum_tensor("mod_psh", [P, 512], F32))
        pg = ctx.enter_context(nc.psum_tensor("mod_pg", [P, 512], F32))
        loaded, expd, dve, mm_cols, mm_gates, stored = (sem("mod_" + n) for n in
                                                        ("loaded", "expd", "dve", "mmc", "mmg", "stored"))
        with nc.Block() as block:
            @block.sync
            def _(sp):
                for l in range(2):
                    sp.dma_start(c[:, l, :], cT[l]).then_inc(loaded, 16)
                    sp.dma_start(w[:, l, :], wmod[l]).then_inc(loaded, 16)
                sp.wait_ge(dve, 7)
                for l in range(2):
                    sp.dma_start(cols[l].rearrange("b f j -> f b j"), colt[:, l]).then_inc(stored, 16)
                    sp.dma_start(gates[l].rearrange("g b f -> b g f"), g[:, l]).then_inc(stored, 16)
                    sp.dma_start(shifts[l], sh[:, l]).then_inc(stored, 16)
                sp.wait_ge(stored, 96)

            @block.scalar
            def _(act):
                act.wait_ge(loaded, 64)
                nc.scalar.activation(e[:], c[:], ACT.Exp, scale=-1.0).then_inc(expd, 1)

            @block.vector
            def _(v):
                v.wait_ge(expd, 1)
                nc.vector.tensor_scalar(e[:], e[:], 1.0, None, ALU.add).then_inc(dve, 1)
                v.wait_ge(dve, 1)
                nc.vector.reciprocal(e[:], e[:]).then_inc(dve, 1)
                v.wait_ge(dve, 2)
                nc.vector.tensor_tensor(c[:], c[:], e[:], ALU.mult).then_inc(dve, 1)
                v.wait_ge(mm_cols, 1)
                v.wait_ge(mm_gates, 1)
                pcv = pc[:, 0:2 * 4 * NB].rearrange("p (l j b) -> p l j b", l=2, j=4)
                for l in range(2):
                    for j in range(4):
                        last = nc.vector.tensor_scalar(colt[:, l, :, j], pcv[:, l, j, :], float(j % 2), None, ALU.add)
                pshv = psh[0:NB, :].rearrange("p (l g f) -> p l g f", l=2, g=2)
                for j in range(2):
                    nc.vector.tensor_scalar(sh[:, :, j, :], pshv[:, :, j, :], float(j), None, ALU.add)
                pgv = pg[0:NB, :].rearrange("p (l g f) -> p l g f", l=2, g=2)
                nc.vector.tensor_copy(g[:], pgv).then_inc(dve, 1)
                v.wait_ge(dve, 4)
                nc.vector.scalar_tensor_tensor(out=mag[:], in0=g[:], scalar=-1.0, in1=g[:], op0=ALU.mult, op1=ALU.max)
                nc.vector.tensor_scalar(sgn[:], g[:], 0.0, 2.0, ALU.is_ge, ALU.mult).then_inc(dve, 1)
                v.wait_ge(dve, 5)
                nc.vector.tensor_scalar(sgn[:], sgn[:], 1.0, None, ALU.subtract).then_inc(dve, 1)
                v.wait_ge(dve, 6)
                nc.vector.scalar_tensor_tensor(out=g[:], in0=mag[:], scalar=GATE_MIN, in1=sgn[:], op0=ALU.max,
                                               op1=ALU.mult).then_inc(dve, 1)

            @block.tensor
            def _(pe):
                pe.wait_ge(dve, 3)
                for l in range(2):
                    for j, part in enumerate((0, 1, 3, 4)):
                        o = (4 * l + j) * NB
                        last = nc.tensor.matmul(pc[:, o:o + NB], w[:, l, part * D:part * D + D], c[:, l, :],
                                                start=True, stop=True)
                last.then_inc(mm_cols, 1)
                for l in range(2):
                    for j, (dst, part) in enumerate(((pg, 2), (pg, 5), (psh, 3), (psh, 4))):
                        o = (2 * l + j % 2) * D
                        last = nc.tensor.matmul(dst[0:NB, o:o + D], c[:, l, :], w[:, l, part * D:part * D + D],
                                                start=True, stop=True)
                last.then_inc(mm_gates, 1)


def decayed_attention(nc, x, xo, cols, gates, w_q, w_k, w_v, w_o, w_down, w_up_k, w_up_v, k_rows, k_late, k_ident):
    with ExitStack() as ctx:
        sb = lambda n, s, d=F32: ctx.enter_context(nc.sbuf_tensor(n, s, d))
        ps = lambda n, s: ctx.enter_context(nc.psum_tensor(n, s, F32))
        sem = semaphores_of(nc, ctx, "da_")

        ident = sb("ident", [P, P])
        identb = sb("identb", [P, P], BF16)
        late = sb("late", [P, 2 * S - P])
        rows = sb("rows", [P, 4, S])
        wq, wk, wv, wo = (sb("w" + n, [P, D]) for n in "qkvo")
        wdown = sb("wdown", [P, DL])
        wup = sb("wup", [DL, 2, D])
        wq_turned = sb("wq_turned", [P, D])
        wup_turned = sb("wup_turned", [DL, D])
        xin = [sb(f"xin{i}", [P, NC, D]) for i in range(2)]
        mcol = [sb(f"mcol{i}", [P, 4]) for i in range(2)]
        xres = [sb(f"xres{i}", [P, NC, D]) for i in range(2)]
        gate = [sb(f"gate{i}", [P, D]) for i in range(2)]
        stack_q = [sb(f"stack_q{i}", [P, NH, S], BF16) for i in range(2)]
        stack_kb = [sb(f"stack_kb{i}", [P, NH, S], BF16) for i in range(2)]
        stack_ka = [sb(f"stack_ka{i}", [P, NH, S], BF16) for i in range(2)]
        vx = [sb(f"vx{i}", [P, NC, NH, 16]) for i in range(2)]
        stat = sb("stat", [P, NC, 6])
        mv = sb("mv", [P, NC, 2])
        rstd = sb("rstd", [P, NC])
        half = sb("half", [P, NC])
        nmr = sb("nmr", [P, NC])
        xn = sb("xn", [P, NC, D])
        hT = sb("hT", [P, S])
        kvT = hT
        latT = sb("latT", [DL, S])
        full = sb("full", [P, 2, S])
        rest = sb("rest", [P, 2, S])
        parts = [sb(f"parts{n}", [P, 2, 3, S], BF16) for n in "qk"]
        sd = [sb(f"sd{i}", [P, S]) for i in range(5)]
        sdc = sb("sdc", [P, 8, 4, P])
        cmax = sb("cmax", [P, 2, NC, 4])
        cpart = sb("cpart", [P, 2, NC, 3, 4], BF16)
        crest = sb("crest", [P, NC, 4])
        cT = [sb(f"cT{i}", [12, S], BF16) for i in range(2)]
        pt = [sb(f"pt{i}", [P, 4, S]) for i in range(2)]
        oTs = sb("oTs", [P, S])
        rsum = sb("rsum", [P, NC, 4])
        otok = sb("otok", [P, NC, D])
        oT = sb("oT", [P, S])
        xout = oT[:].rearrange("p (c d) -> p c d", c=NC)

        pmax = [ps(f"pmax{i}", [P, S]) for i in range(2)]
        pst = [ps(f"pst{i}", [P, 2, S]) for i in range(2)]
        pot = ps("pot", [P, S])
        pmisc = ps("pmisc", [P, S])

        const_in = sem("const_in")
        turned = sem("turned")
        cleared = sem("cleared")
        x_in = [sem(f"x_in{i}") for i in range(2)]
        res_in = [sem(f"res_in{i}") for i in range(2)]
        stack_in = sem("stack_in")
        c_in = [sem(f"c_in{i}") for i in range(2)]
        out_done = sem("out_done")
        stats = sem("stats")
        rstd_ready = sem("rstd_ready")
        nmr_ready = sem("nmr_ready")
        xn_ready = sem("xn_ready")
        ht_ready = sem("ht_ready")
        kv_ready = sem("kv_ready")
        lat_ready = sem("lat_ready")
        full_ready = sem("full_ready")
        hi_ready = sem("hi_ready")
        rest_ready = sem("rest_ready")
        mid_ready = sem("mid_ready")
        low_ready = sem("low_ready")
        v_ready = sem("v_ready")
        misc_full = sem("misc_full")
        misc_free = sem("misc_free")
        max_scored = sem("max_scored")
        max_taken = sem("max_taken")
        diag_ready = sem("diag_ready")
        csplit = sem("csplit")
        cT_ready = sem("cT_ready")
        s_ready = sem("s_ready")
        p_ready = sem("p_ready")
        pv_done = sem("pv_done")
        ot_free = sem("ot_free")
        oTs_ready = sem("oTs_ready")
        recip = sem("recip")
        otok_ready = sem("otok_ready")
        oT_ready = sem("oT_ready")
        gated = sem("gated")
        xout_ready = sem("xout_ready")
        tick = {e: sem("tick_" + e) for e in ("pe", "dve", "act", "pool", "sp")}

        ORDER = ["V", "O3p", "c1", "T2p", "WOp", "O0", "c2", "h", "q", "kv", "O1", "c3", "lat", "k", "O2", "c0n"]
        PREV = ("O3p", "T2p", "WOp")
        PROLOGUE = ["h", "q", "kv", "lat", "k", "V", "h1", "q1", "kv1", "lat1", "k1", "c0"]

        def body_uses(prev, next_v, next_p, next_m):
            skip = set() if prev else set(PREV)
            skip |= set() if next_v else {"V"}
            skip |= set() if next_p else {"h", "q", "kv", "lat", "k"}
            skip |= set() if next_m else {"c0n"}
            return [n for n in ORDER if n not in skip]

        FIRST = body_uses(False, True, True, True)
        FULL = body_uses(True, True, True, True)

        class Body:

            def __init__(self, b, half, par, at, prev=True, next_v=True, next_p=True, next_m=True):
                self.b, self.half, self.par, self.at = b, half, par, at
                self.prev, self.next_v, self.next_p, self.next_m = prev, next_v, next_p, next_m
                self.uses = body_uses(prev, next_v, next_p, next_m)

            def nth(self, d):
                return self.half + (self.par + d) // 2

            def use(self, name):
                return self.at + self.uses.index(name)

        def batches(eng, body):
            at1 = len(PROLOGUE) + len(FIRST)
            body(Body(0, 0, 0, len(PROLOGUE), prev=False))
            with eng.Fori(0, (NB - 4) // 2) as i:
                i = eng.snap(i)
                body(Body(2 * i + 1, i, 1, 2 * len(FULL) * i + at1))
                body(Body(2 * i + 2, i + 1, 0, 2 * len(FULL) * i + at1 + len(FULL)))
            at = at1 + (NB - 4) * len(FULL)
            body(Body(NB - 3, NB // 2 - 2, 1, at))
            at += len(FULL)
            last2 = Body(NB - 2, NB // 2 - 1, 0, at, next_p=False)
            body(last2)
            last1 = Body(NB - 1, NB // 2 - 1, 1, at + len(last2.uses), next_v=False, next_p=False, next_m=False)
            body(last1)
            return last1.at + len(last1.uses)

        def sd_of(m, j):
            return 4 * (m % 2) if j == 0 else j

        def fill(eng, stack):
            pairs_of = stack[:].rearrange("p h s -> p (h s)").bitcast(F32)
            eng.memset(pairs_of[0:KMAX, :], 0.0)
            return eng.memset(pairs_of[KMAX:P, :], float(np.array([0x3F803F80], np.uint32).view(np.float32)[0]))

        with nc.Block() as block:
            @block.sync
            def _(sp):
                for dst, src in ((ident[:], k_ident), (late[:], k_late), (wq[:], w_q), (wk[:], w_k), (wv[:], w_v),
                                 (wo[:], w_o), (wdown[:], w_down), (wup[:, 0, :], w_up_k), (wup[:, 1, :], w_up_v)):
                    sp.dma_start(dst, src).then_inc(const_in, 16)
                sp.dma_start(rows[:], k_rows[None, :, :].to_broadcast([P, 4, S])).then_inc(const_in, 16)

                def hold(s, v):
                    sp.wait_ge(s, v)
                    sp.sem_inc(tick["sp"], 1)

                def load_x(p, par):
                    if not isinstance(p, int) or p >= 2:
                        hold(ht_ready, p - 1)
                    sp.dma_start(xin[par][:], x[p].rearrange("(c p) d -> p c d", p=P)).then_inc(x_in[par], 16)
                    sp.dma_start(mcol[par][:], cols[p]).then_inc(x_in[par], 16)

                def load_stacks(p, par, side):
                    if side == 0:
                        hold(low_ready, 2 * p + 2)
                        if not isinstance(p, int) or p >= 2:
                            hold(s_ready, 2 * STEPS * (p - 1))
                    stack_k = (stack_kb, stack_ka)[side][par]
                    for r in range(len(PART_Q)):
                        o = SIDE * side + HD * r
                        for dst, src in ((stack_q[par], parts[0][:, side, PART_Q[r], :]),
                                         (stack_k, parts[1][:, side, PART_K[r], :])):
                            sp.dma_start(dst[o:o + HD, :, :], src).then_inc(stack_in, 16)

                def load_residual(b, par):
                    sp.dma_start(xres[par][:], x[b].rearrange("(c p) d -> p c d", p=P)).then_inc(res_in[par], 16)
                    sp.dma_start(gate[par][:], gates[b].unsqueeze(0).to_broadcast([P, D])).then_inc(res_in[par], 16)

                def store_maxima(unit, par, u):
                    hold(cT_ready, unit + 1)
                    sp.dma_start(stack_q[par][KMAX:KEXP, 4 * u:4 * u + 4, :], cT[u % 2][:]).then_inc(c_in[u % 2], 16)

                def store_out(b):
                    hold(xout_ready, b + 1)
                    sp.dma_start(xo[b].rearrange("(c p) d -> p c d", p=P), xout).then_inc(out_done, 16)

                sp.sem_inc(out_done, 16)
                load_x(0, 0)
                load_x(1, 1)
                sp.wait_ge(cleared, 7)
                load_stacks(0, 0, 0)
                load_stacks(0, 0, 1)
                store_maxima(0, 0, 0)

                def body(k):
                    b, par = k.b, k.par
                    if k.next_p:
                        load_x(b + 2, par)
                    if k.next_v:
                        load_stacks(b + 1, 1 - par, 0)
                    store_maxima(NU * b + 1, par, 1)
                    if k.next_v:
                        load_stacks(b + 1, 1 - par, 1)
                    if k.prev:
                        store_out(b - 1)
                    load_residual(b, par)
                    store_maxima(NU * b + 2, par, 2)
                    store_maxima(NU * b + 3, par, 3)
                    if k.next_m:
                        store_maxima(NU * b + 4, 1 - par, 0)

                batches(sp, body)
                store_out(NB - 1)
                sp.wait_ge(out_done, 16 * (NB + 1))

            @block.tensor
            def _(pe):
                def hold(s, v):
                    pe.wait_ge(s, v)
                    pe.sem_inc(tick["pe"], 1)

                def misc(n):
                    if not isinstance(n, int) or n > 0:
                        hold(misc_free, n)

                def project(p, uses):
                    misc(uses("h"))
                    hold(xn_ready, p + 1)
                    for c in range(NC):
                        last = nc.tensor.transpose(pmisc[:, c * P:(c + 1) * P], xn[:, c, :], ident[:])
                    last.then_inc(misc_full, 1)

                def project_q(p, n):
                    misc(n)
                    hold(ht_ready, p + 1)
                    nc.tensor.matmul(pmisc[:], wq_turned[:], hT[:], start=True, stop=True).then_inc(misc_full, 1)

                def project_kv(n):
                    misc(n)
                    nc.tensor.matmul(pmisc[:], wk[:], hT[:], start=True, stop=False)
                    nc.tensor.matmul(pmisc[:], wv[:], hT[:], start=False, stop=True).then_inc(misc_full, 1)

                def project_lat(p, n):
                    misc(n)
                    hold(kv_ready, p + 1)
                    nc.tensor.matmul(pmisc[0:DL, :], wdown[:], kvT[:], start=True, stop=True).then_inc(misc_full, 1)

                def project_k(p, n):
                    misc(n)
                    hold(lat_ready, p + 1)
                    nc.tensor.matmul(pmisc[:], wup_turned[:], latT[:], start=True, stop=True).then_inc(misc_full, 1)

                def project_v(n):
                    misc(n)
                    for c in range(NC):
                        last = nc.tensor.matmul(pmisc[:, c * P:(c + 1) * P], latT[:, c * P:(c + 1) * P], wup[:, 1, :],
                                                start=True, stop=True)
                    last.then_inc(misc_full, 1)

                def score_for_max(b, par, m, j):
                    n = 4 * (STEPS * b + m) + j
                    h, c = 4 * (m // NC) + j, m % NC
                    if not isinstance(n, int) or n >= 2:
                        hold(max_taken, n - 1)
                    nc.tensor.matmul(pmax[j % 2][:], stack_q[par][0:KMAX, h, c * P:(c + 1) * P],
                                     stack_kb[par][0:KMAX, h, :], start=True, stop=True).then_inc(max_scored, 1)

                def transpose_maxima(unit, u, n):
                    misc(n)
                    hold(csplit, 4 * unit + 4)
                    out = pmisc[0:12, :].bitcast(BF16)
                    for c in range(NC):
                        last = nc.tensor.transpose(out[:, c * P:(c + 1) * P],
                                                   cpart[:, u % 2, c].rearrange("p a b -> p (a b)"), identb[:])
                    last.then_inc(misc_full, 1)

                def scores(b, par, f, pair, between):
                    e = 2 * (STEPS * b + f) + pair
                    u, c = f // NC, f % NC
                    if not isinstance(e, int) or e >= 2:
                        hold(p_ready, e - 1)
                    if c == 0 and pair == 0:
                        hold(c_in[u % 2], 16 * (2 * b + u // 2 + 1))
                    hold(diag_ready, 4 * (STEPS * b + f) + 2 * pair + 2)
                    keys = slice(c * P, (c + 1) * P)
                    for k in range(2):
                        h = 4 * u + 2 * pair + k
                        out = pst[pair][:, k, :]
                        if c < NC - 1:
                            behind = slice((c + 1) * P, S)
                            nc.tensor.matmul(out[:, behind], stack_kb[par][0:KEXP, h, keys],
                                             stack_q[par][0:KEXP, h, behind], start=True, stop=True)
                        if c > 0:
                            ahead = slice(0, c * P)
                            nc.tensor.matmul(out[:, ahead], stack_ka[par][0:KEXP, h, keys],
                                             stack_q[par][0:KEXP, h, ahead], start=True, stop=True)
                        last = nc.tensor.transpose(out[:, keys], sdc[:, f % 8, 2 * pair + k, :], ident[:])
                        if k == 1:
                            last.then_inc(s_ready, 1)
                        between(2 * pair + k)

                def weigh(b, par, f):
                    u, c = f // NC, f % NC
                    hold(p_ready, 2 * (STEPS * b + f) + 2)
                    if c == 0:
                        hold(v_ready, b + 1)
                        if not isinstance(b, int) or NU * b + u > 0:
                            hold(ot_free, NU * b + u)
                    for j in range(4):
                        last = nc.tensor.matmul(pot[32 * j:32 * j + 16, :], vx[par][:, c, 4 * u + j, :], pt[f % 2][:, j, :],
                                                start=(c == 0), stop=(c == NC - 1), skip_group_check=True)
                    last.then_inc(pv_done, 1)

                def turn_heads(unit, n):
                    misc(n)
                    hold(oTs_ready, unit + 1)
                    for c in range(NC):
                        last = nc.tensor.transpose(pmisc[:, c * P:(c + 1) * P], oTs[:, c * P:(c + 1) * P], ident[:])
                    last.then_inc(misc_full, 1)

                def turn_tokens(b, n):
                    misc(n)
                    hold(otok_ready, NU * b + NU)
                    for c in range(NC):
                        last = nc.tensor.transpose(pmisc[:, c * P:(c + 1) * P], otok[:, c, :], ident[:])
                    last.then_inc(misc_full, 1)

                def project_out(b, n):
                    misc(n)
                    hold(oT_ready, b + 1)
                    for c in range(NC):
                        last = nc.tensor.matmul(pmisc[:, c * P:(c + 1) * P], oT[:, c * P:(c + 1) * P], wo[:],
                                                start=True, stop=True)
                    last.then_inc(misc_full, 1)

                pe.wait_ge(const_in, 160)
                pe.wait_ge(cleared, 7)
                pe.wait_ge(turned, 3)
                for p in range(2):
                    at = 6 * p
                    project(p, lambda n: at)
                    project_q(p, at + 1)
                    project_kv(at + 2)
                    project_lat(p, at + 3)
                    project_k(p, at + 4)
                    if p == 0:
                        project_v(5)
                pe.wait_ge(stack_in, 24 * 16)
                for m in range(LEAD):
                    for j in range(4):
                        score_for_max(0, 0, m, j)
                    if m == 4:
                        transpose_maxima(0, 0, 11)

                def body(k):
                    b, par = k.b, k.par
                    for f in range(STEPS):
                        m = f + LEAD
                        if m < STEPS:
                            mb, mpar, mm = b, par, m
                        else:
                            mb, mpar, mm = b + 1, 1 - par, m - STEPS
                        if m == STEPS and k.next_m:
                            hold(stack_in, 24 * 16 * (b + 2))

                        def between(j):
                            if m < STEPS or k.next_m:
                                score_for_max(mb, mpar, mm, j)

                        for pair in range(2):
                            scores(b, par, f, pair, between)
                        if f > 0:
                            weigh(b, par, f - 1)
                        elif k.prev:
                            weigh(b - 1, 1 - par, STEPS - 1)
                        if f == 0 and k.next_v:
                            project_v(k.use("V"))
                        if f == 2:
                            transpose_maxima(NU * b + 1, 1, k.use("c1"))
                        if k.prev:
                            if f == 1:
                                turn_heads(NU * b - 1, k.use("O3p"))
                            if f == 3:
                                turn_tokens(b - 1, k.use("T2p"))
                            if f == 4:
                                project_out(b - 1, k.use("WOp"))
                        if f == 5:
                            turn_heads(NU * b, k.use("O0"))
                        if f == 6:
                            transpose_maxima(NU * b + 2, 0, k.use("c2"))
                        if f == 9:
                            if k.next_p:
                                project_kv(k.use("kv"))
                            turn_heads(NU * b + 1, k.use("O1"))
                        if f == 10:
                            transpose_maxima(NU * b + 3, 1, k.use("c3"))
                        if k.next_p:
                            if f == 7:
                                project(b + 2, k.use)
                            if f == 8:
                                project_q(b + 2, k.use("q"))
                            if f == 11:
                                project_lat(b + 2, k.use("lat"))
                            if f == 12:
                                project_k(b + 2, k.use("k"))
                        if f == 13:
                            turn_heads(NU * b + 2, k.use("O2"))
                        if f == 14 and k.next_m:
                            transpose_maxima(NU * b + 4, 0, k.use("c0n"))

                at = batches(pe, body)
                weigh(NB - 1, 1, STEPS - 1)
                turn_heads(NU * NB - 1, at)
                turn_tokens(NB - 1, at + 1)
                project_out(NB - 1, at + 2)

            @block.scalar
            def _(act):
                def hold(s, v):
                    act.wait_ge(s, v)
                    act.sem_inc(tick["act"], 1)

                def normalise(p, par):
                    hold(nmr_ready, p + 1)
                    if not isinstance(p, int) or p >= 1:
                        hold(ht_ready, p)
                    for c in range(NC):
                        last = nc.scalar.activation(xn[:, c, :], xin[par][:, c, :], ACT.Identity,
                                                    bias=nmr[:, c:c + 1], scale=rstd[:, c:c + 1])
                    last.then_inc(xn_ready, 1)

                def modulate(p, par, n):
                    hold(misc_full, n + 1)
                    nc.scalar.activation(hT[:], pmisc[:], ACT.Identity, bias=mcol[par][:, 0:1],
                                         scale=mcol[par][:, 1:2]).then_inc(misc_free, 1)

                def keep(dst, src, n, ready):
                    hold(misc_full, n + 1)
                    nc.scalar.activation(dst, src, ACT.Copy).then_inc(misc_free, 1)

                def high(p, which):
                    i = 2 * p + which
                    hold(full_ready, i + 1)
                    if not isinstance(p, int) or p >= 1:
                        hold(stack_in, 24 * 16 * p)
                    nc.scalar.activation(parts[which][:, :, 0, :], full[:], ACT.Copy).then_inc(hi_ready, 1)

                def middle(p, which):
                    i = 2 * p + which
                    hold(rest_ready, i + 1)
                    nc.scalar.activation(parts[which][:, :, 1, :], rest[:], ACT.Copy).then_inc(mid_ready, 1)

                def keep_maxima(nth, u, n):
                    hold(misc_full, n + 1)
                    if not isinstance(nth, int) or nth >= 1:
                        hold(c_in[u % 2], 16 * nth)
                    nc.scalar.activation(cT[u % 2][:], pmisc[0:12, :].bitcast(BF16)[:, 0:S], ACT.Copy)\
                        .then_inc(misc_free, 1)
                    hold(misc_free, n + 1)
                    act.sem_inc(cT_ready, 1)

                def keep_turned(b, n):
                    hold(out_done, 16 * (b + 1))
                    keep(oT[:], pmisc[:], n, oT_ready)
                    after(misc_free, n + 1, oT_ready)

                def exponentials(b, f, pair):
                    e = 2 * (STEPS * b + f) + pair
                    hold(s_ready, e + 1)
                    if pair == 0 and (not isinstance(b, int) or b > 0 or f >= 2):
                        hold(pv_done, STEPS * b + f - 1)
                    nc.scalar.activation(pt[f % 2][:, 2 * pair:2 * pair + 2, :], pst[pair][:], ACT.Exp)\
                        .then_inc(p_ready, 1)

                def keep_unit(unit):
                    hold(pv_done, NC * (unit + 1))
                    if not isinstance(unit, int) or unit >= 1:
                        hold(otok_ready, unit)
                    nc.scalar.activation(oTs[:], pot[:], ACT.Copy).then_inc(ot_free, 1)
                    hold(ot_free, unit + 1)
                    act.sem_inc(oTs_ready, 1)

                act.wait_ge(const_in, 160)
                nc.scalar.activation(identb[:], ident[:], ACT.Copy).then_inc(turned, 1)
                nc.scalar.activation(wq_turned[:].rearrange("p (d h) -> p d h", d=HD),
                                     wq[:].rearrange("p (h d) -> p d h", d=HD), ACT.Copy).then_inc(turned, 1)
                nc.scalar.activation(wup_turned[:].rearrange("p (d h) -> p d h", d=HD),
                                     wup[:, 0, :].rearrange("p (h d) -> p d h", d=HD), ACT.Copy).then_inc(turned, 1)

                def after(s_from, value, s_to):
                    hold(s_from, value)
                    act.sem_inc(s_to, 1)

                def ht(p, par, n):
                    modulate(p, par, n)
                    after(misc_free, n + 1, ht_ready)

                def kv(p, n):
                    keep(kvT[:], pmisc[:], n, kv_ready)
                    after(misc_free, n + 1, kv_ready)

                def lat(p, n):
                    keep(latT[:], pmisc[0:DL, :], n, lat_ready)
                    after(misc_free, n + 1, lat_ready)

                def values(b, par, n):
                    hold(misc_full, n + 1)
                    nc.scalar.activation(vx[par][:, :, :, 0:HD], pmisc[:].rearrange("p (c h d) -> p c h d", c=NC, h=NH),
                                         ACT.Copy).then_inc(misc_free, 1)
                    after(misc_free, n + 1, v_ready)

                for p in range(2):
                    at = 6 * p
                    normalise(p, p)
                    ht(p, p, at)
                    high(p, 0)
                    kv(p, at + 2)
                    middle(p, 0)
                    lat(p, at + 3)
                    high(p, 1)
                    if p == 0:
                        values(0, 0, 5)
                    middle(p, 1)
                keep_maxima(0, 0, 11)

                def body(k):
                    b, par = k.b, k.par
                    for f in range(STEPS):
                        exponentials(b, f, 0)
                        exponentials(b, f, 1)
                        if f == 0:
                            if k.prev:
                                keep_unit(NU * b - 1)
                            if k.next_v:
                                values(b + 1, 1 - par, k.use("V"))
                        if f == 2:
                            keep_maxima(2 * b, 1, k.use("c1"))
                        if f == 3 and k.prev:
                            keep_turned(b - 1, k.use("T2p"))
                        if f in (4, 8, 12):
                            keep_unit(NU * b + f // 4 - 1)
                        if f == 6:
                            keep_maxima(2 * b + 1, 0, k.use("c2"))
                        if f == 10:
                            keep_maxima(2 * b + 1, 1, k.use("c3"))
                        if f == 14 and k.next_m:
                            keep_maxima(2 * b + 2, 0, k.use("c0n"))
                        if k.next_p:
                            if f == 6:
                                normalise(b + 2, par)
                            if f == 7:
                                ht(b + 2, par, k.use("h"))
                            if f == 9:
                                kv(b + 2, k.use("kv"))
                                high(b + 2, 0)
                            if f == 10:
                                middle(b + 2, 0)
                            if f == 11:
                                lat(b + 2, k.use("lat"))
                            if f == 13:
                                high(b + 2, 1)
                            if f == 14:
                                middle(b + 2, 1)

                at = batches(act, body)
                keep_unit(NU * NB - 1)
                keep_turned(NB - 1, at + 1)

            @block.vector
            def _(dve):
                def hold(s, v):
                    dve.wait_ge(s, v)
                    dve.sem_inc(tick["dve"], 1)

                for par in range(2):
                    nc.vector.memset(vx[par][:, :, :, HD:HD + 1], 1.0).then_inc(cleared, 1)
                    nc.vector.memset(vx[par][:, :, :, HD + 1:], 0.0)
                    fill(nc.vector, stack_kb[par]).then_inc(cleared, 1)
                nc.vector.memset(half[:], -0.5)
                nc.vector.memset(pot[:], 0.0).then_inc(cleared, 1)
                dve.wait_ge(const_in, 160)

                def statistics(p, par, nth):
                    hold(x_in[par], 32 * nth + 32)
                    if not isinstance(p, int) or p >= 1:
                        hold(xn_ready, p)
                    for c in range(NC):
                        last = nc.vector.bn_stats(stat[:, c, :], xin[par][:, c, :])
                    last.then_inc(stats, 1)
                    hold(stats, 3 * p + 1)
                    for c in range(NC):
                        last = nc.vector.bn_aggr(mv[:, c, :], stat[:, c, :])
                    last.then_inc(stats, 1)
                    hold(stats, 3 * p + 2)
                    nc.vector.tensor_scalar(mv[:, :, 1], mv[:, :, 1], LN_EPS, None, ALU.add).then_inc(stats, 1)

                def shift(p):
                    hold(rstd_ready, p + 1)
                    nc.vector.scalar_tensor_tensor(out=nmr[:], in0=mv[:, :, 0], scalar=-1.0, in1=rstd[:],
                                                   op0=ALU.mult, op1=ALU.mult).then_inc(nmr_ready, 1)

                def decay(p, which, n, piece):
                    if piece == 0:
                        hold(misc_full, n + 1)
                        i = 2 * p + which
                        if not isinstance(i, int) or i >= 1:
                            hold(rest_ready, i)
                            hold(hi_ready, i)
                        nc.vector.tensor_tensor(full[:, 0, :], pmisc[:], rows[:, 2 * which, :], ALU.mult)
                    if piece == 1:
                        nc.vector.tensor_tensor(full[:, 1, :], pmisc[:], rows[:, 2 * which + 1, :], ALU.mult)\
                            .then_inc(misc_free, 1)
                        hold(misc_free, n + 1)
                        dve.sem_inc(full_ready, 1)

                def maxima(b, m, j):
                    n = 4 * (STEPS * b + m) + j
                    c = m % NC
                    hold(max_scored, n + 1)
                    ago = 8 if j == 0 else 4
                    if not isinstance(n, int) or n >= ago:
                        hold(diag_ready, n - ago + 1)
                    o = S - P - c * P
                    nc.vector.tensor_tensor_reduce(out=sd[sd_of(m, j)][:], in0=pmax[j % 2][:], in1=late[:, o:o + S], scale=1.0,
                                                   scalar=LOWEST, op0=ALU.mult, op1=ALU.max,
                                                   accum_out=cmax[:, (m // NC) % 2, c, j:j + 1]).then_inc(max_taken, 1)

                def split_maxima(unit, u, piece):
                    par = u % 2
                    c = cmax[:, par].rearrange("p c j -> p c j")
                    if piece == 0:
                        hold(max_taken, 16 * (unit + 1))
                        nc.vector.tensor_scalar(cpart[:, par, :, 0, :], c, -1.0, None, ALU.mult).then_inc(csplit, 1)
                    if piece == 1:
                        hold(csplit, 4 * unit + 1)
                        nc.vector.scalar_tensor_tensor(out=crest[:], in0=c, scalar=-1.0, in1=cpart[:, par, :, 0, :],
                                                       op0=ALU.mult, op1=ALU.subtract).then_inc(csplit, 1)
                    if piece == 2:
                        hold(csplit, 4 * unit + 2)
                        nc.vector.tensor_copy(cpart[:, par, :, 1, :], crest[:]).then_inc(csplit, 1)
                    if piece == 3:
                        hold(csplit, 4 * unit + 3)
                        nc.vector.tensor_tensor(cpart[:, par, :, 2, :], crest[:], cpart[:, par, :, 1, :], ALU.subtract)\
                            .then_inc(csplit, 1)

                def normalise_heads(b, unit, u, n, piece):
                    t = pmisc[:].rearrange("p (c j r) -> p c j r", c=NC, j=4)
                    if piece == 0:
                        hold(misc_full, n + 1)
                        if u == 0 and (not isinstance(b, int) or b > 0):
                            hold(oT_ready, b)
                        nc.vector.reciprocal(rsum[:], t[:, :, :, HD]).then_inc(recip, 1)
                    if piece == 1:
                        hold(recip, unit + 1)
                        nc.vector.tensor_tensor(otok[:, :, 32 * u:32 * u + 32].rearrange("p c (j d) -> p c j d", j=4),
                                                t[:, :, :, 0:HD],
                                                rsum[:].unsqueeze(3).to_broadcast([P, NC, 4, HD]),
                                                ALU.mult).then_inc(misc_free, 1)
                        hold(misc_free, n + 1)
                        dve.sem_inc(otok_ready, 1)

                def add_residual(b, par, nth, n, piece):
                    if piece == 0:
                        hold(misc_full, n + 1)
                        hold(res_in[par], 32 * (nth + 1))
                        nc.vector.tensor_tensor(xout, pmisc[:].rearrange("p (c d) -> p c d", c=NC),
                                                gate[par][:].unsqueeze(1).to_broadcast([P, NC, D]), ALU.mult)\
                            .then_inc(misc_free, 1)
                    if piece == 1:
                        hold(misc_free, n + 1)
                        nc.vector.tensor_tensor(xout, xout, xres[par][:], ALU.add).then_inc(xout_ready, 1)

                for p in range(2):
                    at = 6 * p
                    statistics(p, p, 0)
                    shift(p)
                    for piece in range(2):
                        decay(p, 0, at + 1, piece)
                    for piece in range(2):
                        decay(p, 1, at + 4, piece)
                for m in range(LEAD):
                    for j in range(4):
                        maxima(0, m, j)
                    if m == 3:
                        for piece in range(4):
                            split_maxima(0, 0, piece)

                def body(k):
                    b, par = k.b, k.par
                    for f in range(STEPS):
                        m = f + LEAD
                        for j in range(4):
                            if m < STEPS:
                                maxima(b, m, j)
                            elif k.next_m:
                                maxima(b + 1, m - STEPS, j)
                            if f in (1, 5, 9):
                                split_maxima(NU * b + f // 4 + 1, (f // 4 + 1) % 2, j)
                            if f == 13 and k.next_m:
                                split_maxima(NU * b + 4, 0, j)
                            if f == 2 and k.prev:
                                normalise_heads(b - 1, NU * b - 1, 3, k.use("O3p"), j)
                            if f in (6, 10, 14):
                                u = (f - 6) // 4
                                normalise_heads(b, NU * b + u, u, k.use(f"O{u}"), j)
                            if f == 5 and k.prev:
                                add_residual(b - 1, 1 - par, k.nth(-1), k.use("WOp"), j)
                            if f == 9 and k.next_p:
                                decay(b + 2, 0, k.use("q"), j)
                            if f == 13 and k.next_p:
                                decay(b + 2, 1, k.use("k"), j)
                        if k.next_p:
                            if f == 4:
                                statistics(b + 2, par, k.nth(2))
                            if f == 5:
                                shift(b + 2)

                at = batches(dve, body)
                for piece in range(2):
                    normalise_heads(NB - 1, NU * NB - 1, 3, at, piece)
                for piece in range(2):
                    add_residual(NB - 1, 1, NB // 2 - 1, at + 2, piece)

            @block.gpsimd
            def _(pool):
                def hold(s, v):
                    pool.wait_ge(s, v)
                    pool.sem_inc(tick["pool"], 1)

                def deviation(p):
                    hold(stats, 3 * p + 3)
                    nc.gpsimd.tensor_tensor(rstd[:], mv[:, :, 1], half[:], ALU.pow).then_inc(rstd_ready, 1)

                def remainder(p, which):
                    hold(hi_ready, 2 * p + which + 1)
                    if not isinstance(p, int) or p + which >= 1:
                        hold(low_ready, 2 * p + which)
                    nc.gpsimd.tensor_tensor(rest[:], full[:], parts[which][:, :, 0, :], ALU.subtract)\
                        .then_inc(rest_ready, 1)

                def low(p, which):
                    hold(mid_ready, 2 * p + which + 1)
                    nc.gpsimd.tensor_tensor(parts[which][:, :, 2, :], rest[:], parts[which][:, :, 1, :], ALU.subtract)\
                        .then_inc(low_ready, 1)

                def diagonal(b, m, j):
                    n = 4 * (STEPS * b + m) + j
                    hold(max_taken, n + 1)
                    if j == 0 and (not isinstance(b, int) or STEPS * b + m >= 8):
                        hold(s_ready, 2 * (STEPS * b + m - 8) + 2)
                    c = m % NC
                    nc.gpsimd.tensor_scalar(sdc[:, m % 8, j, :], sd[sd_of(m, j)][:, c * P:(c + 1) * P],
                                            cmax[:, (m // NC) % 2, c, j:j + 1], None, ALU.subtract)\
                        .then_inc(diag_ready, 1)

                for par in range(2):
                    fill(nc.gpsimd, stack_ka[par]).then_inc(cleared, 1)
                pool.wait_ge(cleared, 7)
                for p in range(2):
                    deviation(p)
                    for which in range(2):
                        remainder(p, which)
                        low(p, which)
                for m in range(LEAD):
                    for j in range(4):
                        diagonal(0, m, j)

                def body(k):
                    b = k.b
                    for f in range(STEPS):
                        m = f + LEAD
                        for j in range(4):
                            if m < STEPS:
                                diagonal(b, m, j)
                            elif k.next_m:
                                diagonal(b + 1, m - STEPS, j)
                        if k.next_p:
                            if f == 4:
                                deviation(b + 2)
                            if f == 10:
                                remainder(b + 2, 0)
                            if f == 11:
                                low(b + 2, 0)
                            if f == 13:
                                remainder(b + 2, 1)
                            if f == 15:
                                low(b + 2, 1)

                batches(pool, body)


TILE = 256
NE = 8
DEEP = 4
HID = 512
REGION = NB * S + TILE


class Chain:

    def __init__(self, eng, sem, tick):
        self.eng, self.sem, self.tick, self.base, self.count = eng, sem, tick, 0, 0

    def start(self, base):
        self.base, self.count = base, 0

    def __call__(self, ins):
        ins.then_inc(self.sem, 1)
        self.count += 1
        self.eng.wait_ge(self.sem, self.base + self.count)
        self.eng.sem_inc(self.tick, 1)


def pairs(eng, body, n):
    body(0)
    with eng.Fori(1, n) as i:
        body(eng.snap(i))


def later(i):
    return not isinstance(i, int) or i > 0


W = 2
NS = NB // W
GC = W * NC


def route(nc, name, x, shifts, w_router, biases, k_ident, k_prefix, k_iota, k_base, k_row, xs, pos_out, weight_out, cnt_out,
          top):
    nl = w_router.shape[1]
    with ExitStack() as ctx:
        sb = lambda n, s, d=F32: ctx.enter_context(nc.sbuf_tensor(f"{name}_{n}", s, d))
        ps = lambda n, s: ctx.enter_context(nc.psum_tensor(f"{name}_{n}", s, F32))
        sem = semaphores_of(nc, ctx, name + "_")
        U32 = mybir.dt.uint32
        BF16 = mybir.dt.bfloat16
        ident = sb("ident", [P, P])
        before = sb("before", [P, P])
        before16 = sb("before16", [P, P], BF16)
        ones16 = sb("ones16", [P, P], BF16)
        wr = sb("wr", [P, nl])
        bias = sb("bias", [P, nl])
        iota = sb("iota", [P, NE])
        base0 = sb("base0", [P, NE])
        half = sb("half", [P, GC])
        zero = sb("zero", [P, D])
        row = sb("row", [P, 2])
        xin = [sb(f"xin{i}", [P, W, NC, D]) for i in range(2)]
        shift = [sb(f"shift{i}", [P, W, 2, D]) for i in range(2)]
        stat = sb("stat", [P, GC, 6])
        mv = [sb(f"mv{i}", [P, GC, 2]) for i in range(2)]
        rstd = [sb(f"rstd{i}", [P, GC]) for i in range(2)]
        h = [sb(f"h{i}", [P, W, NC, D]) for i in range(2)]
        hT = sb("hT", [P, GC * P])
        lang = sb("lang", [P, GC, 5])
        ew = sb("ew", [P, GC, 4])
        m = sb("m", [P, GC])
        prob = sb("prob", [P, GC, NE])
        best = sb("best", [P, GC, 8])
        bidx = sb("bidx", [P, GC, 8], U32)
        idxf = sb("idxf", [P, GC, 2])
        hot = sb("hot", [P, 2, GC, NE])
        both = sb("both", [P, GC + 1, NE], BF16)
        wts = [sb(f"wts{i}", [P, GC, 2]) for i in range(2)]
        rank = sb("rank", [P, GC, NE])
        picked = sb("picked", [P, 2, GC, NE])
        place = [sb(f"place{i}", [P, 2, GC, top]) for i in range(2)]
        pos = [sb(f"pos{i}", [P, GC, top], U32) for i in range(2)]
        base = sb("base", [P, NE])
        tail = sb("tail", [P, NE])
        tails = sb("tails", [P, 2, NE], U32)
        ph = [ps(f"ph{i}", [P, S]) for i in range(W)]
        plog = ps("plog", [P, 512])
        ppre = ps("ppre", [P, 512])
        const_in, cleared, x_used, h_ready, hT_full, hT_ready, log_full, exp_in, exp_out, hot_ready, pre_full, \
            pos_ready, stats, rstd_ready, chain_s, tail_ready, cnt_saved, zeroed, tails_zeroed = (
                sem(n) for n in ("const_in", "cleared", "x_used", "h_ready", "hT_full", "hT_ready",
                                 "log_full", "exp_in", "exp_out", "hot_ready", "pre_full", "pos_ready",
                                 "stats", "rstd_ready", "chain", "tail_ready", "cnt_saved", "zeroed", "tails_zeroed"))
        x_in, scattered, saved = ([sem(f"{n}{i}") for i in range(2)] for n in ("x_in", "scattered", "saved"))
        tick = {e: sem("tick_" + e) for e in ("pe", "dve", "act", "pool", "sp")}
        nexp = 2 if top == 2 else 1
        x_steps = x.rearrange("(n w) (c p) d -> n p w c d", w=W, p=P)
        shift_steps = shifts.rearrange("(n w) t d -> n w t d", w=W)

        with nc.Block() as block:
            @block.sync
            def _(sp):
                def hold(s, v):
                    sp.wait_ge(s, v)
                    sp.sem_inc(tick["sp"], 1)

                for dst, src in ((ident[:], k_ident), (before[:], k_prefix), (wr[:], w_router),
                                 (row[:], k_row),
                                 (iota[:], k_iota[0:1, :].to_broadcast([P, NE])),
                                 (base0[:], k_base.unsqueeze(0).to_broadcast([P, NE]))):
                    sp.dma_start(dst, src).then_inc(const_in, 16)
                o = 0
                for bvec in biases:
                    n = bvec.shape[0]
                    sp.dma_start(bias[:, o:o + n], bvec.unsqueeze(0).to_broadcast([P, n])).then_inc(const_in, 16)
                    o += n
                sp.wait_ge(cleared, 1)
                for r in range(NE * TILE // P):
                    sp.dma_start(xs[NE * REGION + r * P:NE * REGION + (r + 1) * P, :], zero[:]).then_inc(zeroed, 16)
                sp.sem_inc(x_used, 2)
                with sp.Fori(0, NS // 2) as i:
                    i = sp.snap(i)
                    for par in range(2):
                        b = 2 * i + par
                        hold(x_used, b + 1)
                        sp.dma_start(xin[par][:], x_steps[b]).then_inc(x_in[par], 16)
                        sp.dma_start(shift[par][:], shift_steps[b].unsqueeze(0).to_broadcast([P, W, 2, D]))\
                            .then_inc(x_in[par], 16)
                sp.wait_ge(tail_ready, 1)
                sp.dma_start(cnt_out, tail[0:1, :]).then_inc(cnt_saved, 16)
                sp.wait_ge(cnt_saved, 16)
                sp.wait_ge(zeroed, 16 * (NE * TILE // P))

            @block.tensor
            def _(pe):
                def hold(s, v):
                    pe.wait_ge(s, v)
                    pe.sem_inc(tick["pe"], 1)

                pe.wait_ge(const_in, 16 * (6 + len(biases)))
                pe.wait_ge(cleared, 2)

                def logits(b, par):
                    hold(h_ready, b + 1)
                    for w in range(W):
                        for c in range(NC):
                            last = nc.tensor.transpose(ph[w][:, c * P:(c + 1) * P], h[par][:, w, c, :], ident[:])
                        last.then_inc(hT_full, 1)
                    for w in range(W):
                        hold(hT_ready, W * b + w + 1)
                        for c in range(w * NC, (w + 1) * NC):
                            last = nc.tensor.matmul(plog[:, c * nl:(c + 1) * nl], hT[:, c * P:(c + 1) * P], wr[:],
                                                    start=True, stop=True, skip_group_check=True)
                    last.then_inc(log_full, 1)

                def ranks(b):
                    hold(hot_ready, b + 1)
                    nc.tensor.matmul(ppre[:, 0:(GC + 1) * NE], before16[:], both[:].rearrange("p c e -> p (c e)"),
                                     start=True, stop=False, skip_group_check=True)
                    for d in range(1, GC + 1):
                        last = nc.tensor.matmul(ppre[:, d * NE:(GC + 1) * NE], ones16[:],
                                                both[:, 0:GC + 1 - d, :].rearrange("p c e -> p (c e)"),
                                                start=False, stop=(d == GC), skip_group_check=True)
                    last.then_inc(pre_full, 1)

                logits(0, 0)
                with pe.Fori(0, NS // 2 - 1) as i:
                    i = pe.snap(i)
                    for par in range(2):
                        ranks(2 * i + par)
                        logits(2 * i + par + 1, 1 - par)
                ranks(NS - 2)
                logits(NS - 1, 1)
                ranks(NS - 1)

            @block.scalar
            def _(act):
                def hold(s, v):
                    act.wait_ge(s, v)
                    act.sem_inc(tick["act"], 1)

                def keep_turned(b):
                    for w in range(W):
                        hold(hT_full, W * b + w + 1)
                        nc.scalar.activation(hT[:, w * S:(w + 1) * S], ph[w][:], ACT.Copy).then_inc(hT_ready, 1)

                def exponentials(b):
                    if top == 2:
                        hold(exp_in, nexp * b + 1)
                        nc.scalar.activation(lang[:, :, 0:4], lang[:, :, 0:4], ACT.Exp).then_inc(exp_out, 1)
                    hold(exp_in, nexp * b + nexp)
                    nc.scalar.activation(prob[:], prob[:], ACT.Exp).then_inc(exp_out, 1)

                def save(b, par):
                    hold(pos_ready, b + 1)
                    for w in range(W):
                        cs = slice(w * NC, (w + 1) * NC)
                        act.dma_start(pos_out[W * b + w], place[par][:, :, cs, :]).then_inc(saved[par], 16)
                        if top == 2:
                            act.dma_start(weight_out[W * b + w], wts[par][:, cs, :]).then_inc(saved[par], 16)

                keep_turned(0)
                with act.Fori(0, NS // 2 - 1) as i:
                    i = act.snap(i)
                    for par in range(2):
                        exponentials(2 * i + par)
                        keep_turned(2 * i + par + 1)
                        save(2 * i + par, par)
                exponentials(NS - 2)
                keep_turned(NS - 1)
                save(NS - 2, 0)
                exponentials(NS - 1)
                save(NS - 1, 1)
                for par in range(2):
                    act.wait_ge(saved[par], 16 * W * top * (NS // 2))

            @block.vector
            def _(dve):
                def hold(s, v):
                    dve.wait_ge(s, v)
                    dve.sem_inc(tick["dve"], 1)

                chain = Chain(dve, chain_s, tick["dve"])
                nc.vector.memset(zero[:], 0.0)
                nc.vector.memset(ones16[:], 1.0)
                nc.vector.memset(both[:, GC], 0.0)
                nc.vector.memset(lang[:], 0.0)
                nc.vector.memset(half[:], -0.5).then_inc(cleared, 1)
                dve.wait_ge(const_in, 16 * (6 + len(biases)))
                chain.start(0)
                nc.vector.tensor_copy(before16[:], before[:]).then_inc(cleared, 1)
                chain(nc.vector.tensor_copy(base[:], base0[:]))

                def per_token(v, n):
                    return v.unsqueeze(2).to_broadcast([P, GC, n])

                def softmax(v, n, e):
                    chain(nc.vector.tensor_reduce(m[:], v, AX.X, ALU.max))
                    chain(nc.vector.tensor_tensor(v, v, per_token(m[:], n), ALU.subtract))
                    dve.sem_inc(exp_in, 1)
                    hold(exp_out, e)
                    chain(nc.vector.tensor_reduce(m[:], v, AX.X, ALU.add))
                    chain(nc.vector.reciprocal(m[:], m[:]))
                    chain(nc.vector.tensor_tensor(v, v, per_token(m[:], n), ALU.mult))

                def statistics(p, i, par):
                    hold(x_in[par], 32 * i + 32)
                    for c in range(GC):
                        last = nc.vector.bn_stats(stat[:, c, :], xin[par][:, c // NC, c % NC, :])
                    chain(last)
                    for c in range(GC):
                        last = nc.vector.bn_aggr(mv[par][:, c, :], stat[:, c, :])
                    chain(last)
                    nc.vector.tensor_scalar(mv[par][:, :, 1], mv[par][:, :, 1], LN_EPS, None, ALU.add)\
                        .then_inc(stats, 1)

                def normalise(p, i, par):
                    hold(rstd_ready, p + 1)
                    for c in range(GC):
                        o = xin[par][:, c // NC, c % NC, :]
                        last = nc.vector.tensor_scalar(o, o, mv[par][:, c, 0:1], rstd[par][:, c:c + 1],
                                                       ALU.subtract, ALU.mult)
                    chain(last)
                    chain(nc.vector.tensor_tensor(xin[par][:], xin[par][:],
                                                  shift[par][:, :, 1, :].unsqueeze(2).to_broadcast([P, W, NC, D]),
                                                  ALU.mult))
                    if later(i):
                        hold(scattered[par], 16 * GC * top * i)
                    chain(nc.vector.tensor_tensor(h[par][:], xin[par][:],
                                                  shift[par][:, :, 0, :].unsqueeze(2).to_broadcast([P, W, NC, D]),
                                                  ALU.add))
                    dve.sem_inc(x_used, 1)
                    dve.sem_inc(h_ready, 1)

                def step(b, i, par, more=2):
                    hold(log_full, b + 1)
                    lgv = plog[:, 0:GC * nl].rearrange("p (c n) -> p c n", c=GC)
                    if top == 2:
                        nc.vector.tensor_tensor(lang[:, :, 0:4], lgv[:, :, NE:nl],
                                                bias[:, NE:nl].unsqueeze(1).to_broadcast([P, GC, 4]), ALU.add)
                    chain(nc.vector.tensor_tensor(prob[:], lgv[:, :, 0:NE],
                                                  bias[:, 0:NE].unsqueeze(1).to_broadcast([P, GC, NE]), ALU.add))
                    if top == 2:
                        softmax(lang[:, :, 0:4], 4, 2 * b + 1)
                        chain(nc.vector.tensor_tensor(ew[:], lang[:, :, 0:4], lang[:, :, 1:5], ALU.add))
                        for q in range(2):
                            o = prob[:, :, 4 * q:4 * q + 4]
                            last = nc.vector.scalar_tensor_tensor(out=o, in0=ew[:], scalar=0.1, in1=o, op0=ALU.mult,
                                                                  op1=ALU.add)
                        chain(last)
                    softmax(prob[:], NE, nexp * b + nexp)
                    for c in range(GC):
                        last = nc.vector.max(best[:, c, :], prob[:, c, :])
                    chain(last)
                    for c in range(GC):
                        last = nc.vector.max_index(bidx[:, c, :], best[:, c, :], prob[:, c, :])
                    chain(last)
                    if later(i):
                        hold(saved[par], 16 * W * top * i)
                    nc.vector.tensor_copy(place[par][:, 1], bidx[:, :, 0:top])
                    chain(nc.vector.tensor_copy(idxf[:], bidx[:, :, 0:2]))
                    for k in range(top):
                        last = nc.vector.tensor_tensor(hot[:, k], iota[:].unsqueeze(1).to_broadcast([P, GC, NE]), per_token(idxf[:, :, k], NE), ALU.is_equal)
                    chain(last)
                    if top == 2:
                        chain(nc.vector.tensor_tensor(both[:, 0:GC], hot[:, 0], hot[:, 1], ALU.add))
                        chain(nc.vector.tensor_tensor(m[:], best[:, :, 0], best[:, :, 1], ALU.add))
                        chain(nc.vector.reciprocal(m[:], m[:]))
                        chain(nc.vector.tensor_tensor(wts[par][:], best[:, :, 0:2], per_token(m[:], 2), ALU.mult))
                    else:
                        chain(nc.vector.tensor_copy(both[:, 0:GC], hot[:, 0]))
                    dve.sem_inc(hot_ready, 1)
                    if more >= 1:
                        normalise(b + 1, i + par, 1 - par)
                    if more >= 2:
                        statistics(b + 2, i + 1, par)
                    hold(pre_full, b + 1)
                    chain(nc.vector.tensor_tensor(rank[:], ppre[:, 0:GC * NE].rearrange("p (c e) -> p c e", c=GC),
                                                  base[:].unsqueeze(1).to_broadcast([P, GC, NE]), ALU.add))
                    for k in range(top):
                        last = nc.vector.tensor_tensor(picked[:, k], rank[:], hot[:, k], ALU.mult)
                    chain(last)
                    for k in range(top):
                        last = nc.vector.tensor_reduce(place[par][:, 0, :, k], picked[:, k], AX.X, ALU.add)
                    chain(last)
                    nc.vector.tensor_copy(pos[par][:], place[par][:, 0]).then_inc(pos_ready, 1)
                    chain(nc.vector.tensor_tensor(base[:], ppre[:, GC * NE:(GC + 1) * NE], base[:], ALU.add))

                CHAIN = 2 + 3 + 1 + 5 * nexp + (2 if top == 2 else 0) + 4 + (4 if top == 2 else 1) + 4
                statistics(0, 0, 0)
                normalise(0, 0, 0)
                statistics(1, 0, 1)
                start = chain.count

                def pair(i):
                    for par in range(2):
                        chain.start(start + CHAIN * (2 * i + par))
                        step(2 * i + par, i, par)
                        assert chain.count == CHAIN, (chain.count, CHAIN)

                pairs(dve, pair, NS // 2 - 1)
                chain.start(start + CHAIN * (NS - 2))
                step(NS - 2, NS // 2 - 1, 0, more=1)
                step(NS - 1, NS // 2 - 1, 1, more=0)
                for q in range(2):
                    last = nc.vector.tensor_scalar(picked[:, q, 0, :], base[:], row[:, q:q + 1], None, ALU.add)
                chain(last)
                nc.vector.tensor_tensor(tail[:], base[:], base0[:], ALU.subtract)
                nc.vector.tensor_copy(tails[:], picked[:, :, 0, :]).then_inc(tail_ready, 1)

            @block.gpsimd
            def _(pool):
                def hold(s, v):
                    pool.wait_ge(s, v)
                    pool.sem_inc(tick["pool"], 1)

                pool.wait_ge(cleared, 1)

                def deviation(p, par):
                    hold(stats, p + 1)
                    nc.gpsimd.tensor_tensor(rstd[par][:], mv[par][:, :, 1], half[:], ALU.pow).then_inc(rstd_ready, 1)

                def scatter(b, par):
                    hold(pos_ready, b + 1)
                    for c in range(GC):
                        for k in range(top):
                            nc.gpsimd.indirect_dma_start(
                                out=xs[:, :], out_offset=bass.IndirectOffsetOnAxis(ap=pos[par][:, c, k:k + 1], axis=0),
                                in_=h[par][:, c // NC, c % NC, :], in_offset=None).then_inc(scattered[par], 16)

                deviation(0, 0)
                deviation(1, 1)
                with pool.Fori(0, NS // 2 - 1) as i:
                    i = pool.snap(i)
                    for par in range(2):
                        deviation(2 * i + par + 2, par)
                        scatter(2 * i + par, par)
                for par in range(2):
                    scatter(NS - 2 + par, par)
                pool.wait_ge(tail_ready, 1)
                for e in range(NE):
                    for q in range(TILE // P):
                        nc.gpsimd.indirect_dma_start(
                            out=xs[:, :], out_offset=bass.IndirectOffsetOnAxis(ap=tails[:, q, e:e + 1], axis=0),
                            in_=zero[:], in_offset=None).then_inc(tails_zeroed, 16)
                for par in range(2):
                    pool.wait_ge(scattered[par], 16 * GC * top * (NS // 2))
                pool.wait_ge(tails_zeroed, 16 * NE * (TILE // P))


def tiles_before(nc, chain, cn, cni, tiles, cum):
    chain(nc.vector.tensor_scalar(cni[:], cn[:], float(TILE - 1), None, ALU.add))
    chain(nc.vector.tensor_single_scalar(cni[:], cni[:], int(np.log2(TILE)), ALU.logical_shift_right))
    chain(nc.vector.tensor_copy(tiles[:], cni[:]))
    chain(nc.vector.tensor_copy(cum[:], tiles[:]))
    for e in range(1, NE):
        chain(nc.vector.tensor_tensor(cum[:, e:e + 1], cum[:, e - 1:e], tiles[:, e:e + 1], ALU.add))


def experts(nc, name, xs, ys, cnt, w1, b1T, w2, b2, k_ident, k_tiles, glu, top):
    NT = top * NB * S // TILE + NE
    NJ = HID // P
    with ExitStack() as ctx:
        sb = lambda n, s, d=F32: ctx.enter_context(nc.sbuf_tensor(f"{name}_{n}", s, d))
        ps = lambda n, s: ctx.enter_context(nc.psum_tensor(f"{name}_{n}", s, F32))
        sem = semaphores_of(nc, ctx, name + "_")
        I32 = mybir.dt.int32
        ident = sb("ident", [P, P])
        ids = sb("ids", [1, NT])
        cn = sb("cn", [1, NE])
        cni = sb("cni", [1, NE], I32)
        cnt_t = sb("cnt_t", [1, NE])
        cum = sb("cum", [1, NE])
        hit = sb("hit", [1, 2, NE, NT])
        who = sb("who", [1, NT])
        first = sb("first", [1, NT])
        rowf = sb("rowf", [1, NT])
        plan = sb("plan", [1, 2, NT], I32)
        xt = [sb(f"xt{i}", [P, 2, D]) for i in range(DEEP)]
        w1s = [sb(f"w1s{i}", [P, HID * (2 if glu else 1)]) for i in range(DEEP)]
        w2s = [sb(f"w2s{i}", [P, NJ, D]) for i in range(DEEP)]
        b1s = [sb(f"b1s{i}", [P, NJ * (2 if glu else 1)]) for i in range(DEEP)]
        b2s = [sb(f"b2s{i}", [P, D]) for i in range(DEEP)]
        xT = [sb(f"xT{i}", [P, TILE]) for i in range(2)]
        act_out = [sb(f"act_out{i}", [P, NJ, TILE]) for i in range(2)]
        sig = [sb(f"sig{i}", [P, NJ, TILE]) for i in range(2)] if glu else None
        ysb = [sb(f"ysb{i}", [P, 2, D]) for i in range(2)]
        pT = [ps(f"pT{i}", [P, 512]) for i in range(2)]
        phid = [ps(f"phid{j}", [P, 2, TILE]) for j in range(NJ)]
        py = [ps(f"py{i}", [P, 512]) for i in range(2)]
        const_in, planned, chain_s, turned, xT_ready, hidden, sig_ready, act_ready, y_full, y_ready = (
            sem(n) for n in ("const_in", "planned", "chain", "turned", "xT_ready", "hidden", "sig_ready",
                             "act_ready", "y_full", "y_ready"))
        loaded = [sem(f"loaded{i}") for i in range(DEEP)]
        stored = [sem(f"stored{i}") for i in range(2)]
        tick = {e: sem("tick_" + e) for e in ("pe", "dve", "act", "pool", "sp")}
        LOADS = 16 * 5

        with nc.Block() as block:
            @block.sync
            def _(sp):
                def hold(s, v):
                    sp.wait_ge(s, v)
                    sp.sem_inc(tick["sp"], 1)

                sp.dma_start(ident[:], k_ident).then_inc(const_in, 16)
                sp.dma_start(ids[:], k_tiles[0:NT].unsqueeze(0)).then_inc(const_in, 16)
                sp.dma_start(cn[:], cnt).then_inc(const_in, 16)
                sp.wait_ge(planned, 1)
                sp.sem_inc(y_ready, DEEP)
                with sp.Fori(0, NT // DEEP) as i:
                    i = sp.snap(i)
                    for par in range(DEEP):
                        t = DEEP * i + par
                        row = sp.value_load(plan[0:1, 0, bass.ds(t, 1)], min_val=0, max_val=(NE + 1) * REGION - TILE)
                        ex = sp.value_load(plan[0:1, 1, bass.ds(t, 1)], min_val=0, max_val=NE - 1)
                        hold(y_ready, t + 1)
                        sp.dma_start(xt[par][:], xs[bass.ds(row, TILE), :].rearrange("(c p) d -> p c d", p=P))\
                            .then_inc(loaded[par], 16)
                        sp.dma_start(w1s[par][:], w1[ex]).then_inc(loaded[par], 16)
                        sp.dma_start(b1s[par][:], b1T[ex]).then_inc(loaded[par], 16)
                        sp.dma_start(w2s[par][:], w2[ex].rearrange("(j p) d -> p j d", p=P)).then_inc(loaded[par], 16)
                        sp.dma_start(b2s[par][:], b2[ex].unsqueeze(0).to_broadcast([P, D])).then_inc(loaded[par], 16)

            @block.tensor
            def _(pe):
                def hold(s, v):
                    pe.wait_ge(s, v)
                    pe.sem_inc(tick["pe"], 1)

                pe.wait_ge(const_in, 48)
                pe.sem_inc(act_ready, NJ * 2)

                def turn(i, t, q):
                    hold(loaded[q % DEEP], LOADS * (i + q // DEEP + 1))
                    for c in range(2):
                        last = nc.tensor.transpose(pT[q % 2][:, c * P:(c + 1) * P], xt[q % DEEP][:, c, :], ident[:])
                    last.then_inc(turned, 1)

                def up(t, q):
                    hold(xT_ready, t + 1)
                    w = w1s[q % DEEP]
                    for j in range(NJ):
                        hold(act_ready, NJ * (t + 1) + j + 1)
                        last = nc.tensor.matmul(phid[j][:, 0, :], w[:, j * P:(j + 1) * P], xT[q % 2][:],
                                                start=True, stop=True, skip_group_check=True)
                        if glu:
                            o = HID + j * P
                            last = nc.tensor.matmul(phid[j][:, 1, :], w[:, o:o + P], xT[q % 2][:],
                                                    start=True, stop=True, skip_group_check=True)
                        last.then_inc(hidden, 1)

                def down(t, q):
                    hold(y_ready, DEEP + t - 1)
                    for j in range(NJ):
                        hold(act_ready, NJ * (t + 2) + j + 1)
                        for c in range(2):
                            last = nc.tensor.matmul(py[q % 2][:, c * D:(c + 1) * D],
                                                    act_out[q % 2][:, j, c * P:(c + 1) * P],
                                                    w2s[q % DEEP][:, j, :], start=(j == 0 and c == 0), stop=(j == NJ - 1),
                                                    skip_group_check=True)
                    last.then_inc(y_full, 1)

                def steps(i, end=False):
                    for q in range(DEEP):
                        t = DEEP * i + q
                        if not end or q + 2 < DEEP:
                            turn(i, t + 2, q + 2)
                        if not end or q + 1 < DEEP:
                            up(t + 1, q + 1)
                        down(t, q)

                turn(0, 0, 0)
                up(0, 0)
                turn(0, 1, 1)
                with pe.Fori(0, NT // DEEP - 1) as i:
                    steps(pe.snap(i))
                steps(NT // DEEP - 1, True)

            @block.scalar
            def _(act):
                def hold(s, v):
                    act.wait_ge(s, v)
                    act.sem_inc(tick["act"], 1)

                with act.Fori(0, NT // DEEP) as i:
                    i = act.snap(i)
                    for q in range(DEEP):
                        t, par = DEEP * i + q, q % 2
                        for j in range(NJ):
                            hold(hidden, NJ * t + j + 1)
                            if glu:
                                nc.scalar.activation(sig[par][:, j, :], phid[j][:, 1, :], ACT.Sigmoid,
                                                     bias=b1s[q][:, NJ + j:NJ + j + 1]).then_inc(sig_ready, 1)
                            else:
                                nc.scalar.activation(act_out[par][:, j, :], phid[j][:, 0, :], ACT.Gelu,
                                                     bias=b1s[q][:, j:j + 1]).then_inc(act_ready, 1)

            @block.vector
            def _(dve):
                def hold(s, v):
                    dve.wait_ge(s, v)
                    dve.sem_inc(tick["dve"], 1)

                chain = Chain(dve, chain_s, tick["dve"])
                chain.start(0)
                dve.wait_ge(const_in, 48)
                tiles_before(nc, chain, cn, cni, cnt_t, cum)
                for e in range(NE):
                    nc.vector.tensor_scalar(hit[:, 0, e, :], ids[:], cum[:, e:e + 1], None, ALU.is_ge)
                    last = nc.vector.tensor_scalar(hit[:, 1, e, :], ids[:], cum[:, e:e + 1], cnt_t[:, e:e + 1], ALU.is_ge,
                                                   ALU.mult)
                chain(last)
                nc.vector.tensor_reduce(who[:], hit[:, 0].rearrange("p e t -> p t e"), AX.X, ALU.add)
                chain(nc.vector.tensor_reduce(first[:], hit[:, 1].rearrange("p e t -> p t e"), AX.X, ALU.add))
                chain(nc.vector.tensor_tensor(rowf[:], ids[:], first[:], ALU.subtract))
                chain(nc.vector.tensor_scalar(rowf[:], rowf[:], float(TILE), None, ALU.mult))
                chain(nc.vector.scalar_tensor_tensor(out=rowf[:], in0=who[:], scalar=float(REGION), in1=rowf[:],
                                                     op0=ALU.mult, op1=ALU.add))
                nc.vector.tensor_copy(plan[:, 0, :], rowf[:])
                nc.vector.tensor_scalar(plan[:, 1, :], who[:], float(NE - 1), None, ALU.min).then_inc(planned, 1)

                def turn(t, q):
                    hold(turned, t + 1)
                    nc.vector.tensor_copy(xT[q % 2][:], pT[q % 2][:, 0:TILE]).then_inc(xT_ready, 1)

                def up(t, q):
                    for j in range(NJ if glu else 0):
                        hold(sig_ready, NJ * t + j + 1)
                        nc.vector.scalar_tensor_tensor(out=act_out[q % 2][:, j, :], in0=phid[j][:, 0, :],
                                                       scalar=b1s[q % DEEP][:, j:j + 1], in1=sig[q % 2][:, j, :],
                                                       op0=ALU.add, op1=ALU.mult).then_inc(act_ready, 1)

                def down(i, t, q):
                    hold(y_full, t + 1)
                    if later(i) or q >= 2:
                        hold(stored[q % 2], 16 * (DEEP // 2 * i + q // 2))
                    nc.vector.tensor_tensor(ysb[q % 2][:], py[q % 2][:, 0:2 * D].rearrange("p (c d) -> p c d", c=2),
                                            b2s[q][:].unsqueeze(1).to_broadcast([P, 2, D]), ALU.add)\
                        .then_inc(y_ready, 1)

                def steps(i, end=False):
                    for q in range(DEEP):
                        t = DEEP * i + q
                        if not end or q + 2 < DEEP:
                            turn(t + 2, q + 2)
                        if not end or q + 1 < DEEP:
                            up(t + 1, q + 1)
                        down(i, t, q)

                turn(0, 0)
                up(0, 0)
                turn(1, 1)
                steps(0)
                with dve.Fori(1, NT // DEEP - 1) as i:
                    steps(dve.snap(i))
                steps(NT // DEEP - 1, True)

            @block.gpsimd
            def _(pool):
                def hold(s, v):
                    pool.wait_ge(s, v)
                    pool.sem_inc(tick["pool"], 1)

                pool.wait_ge(planned, 1)
                with pool.Fori(0, NT // 2) as i:
                    i = pool.snap(i)
                    for par in range(2):
                        t = 2 * i + par
                        hold(y_ready, DEEP + t + 1)
                        pool.dma_start(ys[bass.ds(t * TILE, TILE), :].rearrange("(c p) d -> p c d", p=P), ysb[par][:])\
                            .then_inc(stored[par], 16)
                for par in range(2):
                    pool.wait_ge(stored[par], 16 * (NT // 2))


def combine(nc, name, x, xo, ys, pos_in, weight_in, cnt, gates, k_iota, k_base, top):
    with ExitStack() as ctx:
        sb = lambda n, s, d=F32: ctx.enter_context(nc.sbuf_tensor(f"{name}_{n}", s, d))
        sem = semaphores_of(nc, ctx, name + "_")
        U32 = mybir.dt.uint32
        xin = [sb(f"xin{i}", [P, NC, D]) for i in range(2)]
        place = [sb(f"place{i}", [P, 2, NC, top]) for i in range(2)]
        pos = [sb(f"pos{i}", [P, NC, top], U32) for i in range(2)]
        iota = sb("iota", [P, NC, NE])
        cn = sb("cn", [P, NE])
        cni = sb("cni", [P, NE], mybir.dt.int32)
        tiles = sb("tiles", [P, NE])
        cum = sb("cum", [P, NE])
        base = sb("base", [P, NE])
        move = sb("move", [P, NE])
        hot = sb("hot", [P, top, NC, NE])
        add = sb("add", [P, NC, top])
        wts = [sb(f"wts{i}", [P, NC, 2]) for i in range(2)]
        gate = [sb(f"gate{i}", [P, D]) for i in range(2)]
        y = [sb(f"y{i}", [P, NC, top, D]) for i in range(2)]
        acc = sb("acc", [P, NC, D])
        out = [sb(f"out{i}", [P, NC, D]) for i in range(2)]
        loaded, pos_in_s, gathered, stored = ([sem(f"{n}{i}") for i in range(2)]
                                              for n in ("loaded", "pos", "gathered", "stored"))
        chain_s, done, const_in, pos_ready = (sem(n) for n in ("chain", "done", "const_in", "pos_ready"))
        tick = {e: sem("tick_" + e) for e in ("dve", "pool", "sp", "act")}
        LOADS = 16 * (2 + (top == 2))
        with nc.Block() as block:
            @block.sync
            def _(sp):
                def hold(s, v):
                    sp.wait_ge(s, v)
                    sp.sem_inc(tick["sp"], 1)

                sp.dma_start(iota[:], k_iota.unsqueeze(0).to_broadcast([P, NC, NE])).then_inc(const_in, 16)
                sp.dma_start(base[:], k_base.unsqueeze(0).to_broadcast([P, NE])).then_inc(const_in, 16)
                sp.dma_start(cn[:], cnt[0].unsqueeze(0).to_broadcast([P, NE])).then_inc(const_in, 16)
                sp.sem_inc(done, 2)
                with sp.Fori(0, NB // 2) as i:
                    i = sp.snap(i)
                    for par in range(2):
                        b = 2 * i + par
                        hold(pos_ready, b + 1)
                        sp.dma_start(place[par][:], pos_in[b]).then_inc(pos_in_s[par], 16)
                        hold(done, b + 1)
                        sp.dma_start(xin[par][:], x[b].rearrange("(c p) d -> p c d", p=P)).then_inc(loaded[par], 16)
                        sp.dma_start(gate[par][:], gates[b].unsqueeze(0).to_broadcast([P, D])).then_inc(loaded[par], 16)
                        if top == 2:
                            sp.dma_start(wts[par][:], weight_in[b]).then_inc(loaded[par], 16)

            @block.gpsimd
            def _(pool):
                def hold(s, v):
                    pool.wait_ge(s, v)
                    pool.sem_inc(tick["pool"], 1)

                with pool.Fori(0, NB // 2) as i:
                    i = pool.snap(i)
                    for par in range(2):
                        hold(pos_ready, 2 * i + par + 3)
                        for c in range(NC):
                            for k in range(top):
                                nc.gpsimd.indirect_dma_start(
                                    out=y[par][:, c, k, :], out_offset=None, in_=ys[:, :],
                                    in_offset=bass.IndirectOffsetOnAxis(ap=pos[par][:, c, k:k + 1], axis=0))\
                                    .then_inc(gathered[par], 16)

            @block.vector
            def _(dve):
                def hold(s, v):
                    dve.wait_ge(s, v)
                    dve.sem_inc(tick["dve"], 1)

                chain = Chain(dve, chain_s, tick["dve"])
                dve.sem_inc(pos_ready, 2)
                for par in range(2):
                    dve.sem_inc(stored[par], 16)
                dve.wait_ge(const_in, 48)
                chain.start(0)
                tiles_before(nc, chain, cn, cni, tiles, cum)
                chain(nc.vector.tensor_tensor(move[:], cum[:], tiles[:], ALU.subtract))
                chain(nc.vector.scalar_tensor_tensor(out=move[:], in0=move[:], scalar=float(TILE), in1=base[:],
                                                     op0=ALU.mult, op1=ALU.subtract))
                setup = chain.count
                FIND = 4
                CHAIN = FIND + (3 if top == 2 else 1)

                def find(b, i, par):
                    chain.start(setup if isinstance(b, int) and b == 0 else setup + FIND + CHAIN * (b - 1))
                    hold(pos_in_s[par], 16 * i + 16)
                    for k in range(top):
                        last = nc.vector.tensor_tensor(hot[:, k], iota[:], place[par][:, 1, :, k].unsqueeze(2)
                                                       .to_broadcast([P, NC, NE]), ALU.is_equal)
                    chain(last)
                    for k in range(top):
                        last = nc.vector.tensor_tensor(hot[:, k], hot[:, k], move[:].unsqueeze(1)
                                                       .to_broadcast([P, NC, NE]), ALU.mult)
                    chain(last)
                    for k in range(top):
                        last = nc.vector.tensor_reduce(add[:, :, k], hot[:, k], AX.X, ALU.add)
                    chain(last)
                    chain(nc.vector.tensor_tensor(pos[par][:], add[:], place[par][:, 0], ALU.add))
                    dve.sem_inc(pos_ready, 1)

                def total(b, i, par):
                    chain.start(setup + CHAIN * b + (FIND if isinstance(b, int) and b == NB - 1 else 2 * FIND))
                    hold(loaded[par], LOADS * i + LOADS)
                    hold(gathered[par], 16 * NC * top * (i + 1))
                    src = y[par][:, :, 0, :]
                    if top == 2:
                        for c in range(NC):
                            last = nc.vector.tensor_scalar(acc[:, c, :], y[par][:, c, 0, :], wts[par][:, c, 0:1], None,
                                                           ALU.mult)
                        chain(last)
                        for c in range(NC):
                            last = nc.vector.scalar_tensor_tensor(out=acc[:, c, :], in0=y[par][:, c, 1, :],
                                                                  scalar=wts[par][:, c, 1:2], in1=acc[:, c, :],
                                                                  op0=ALU.mult, op1=ALU.add)
                        chain(last)
                        src = acc[:]
                    hold(stored[par], 16 * i + 16)
                    chain(nc.vector.tensor_tensor(out[par][:], src, gate[par][:].unsqueeze(1).to_broadcast([P, NC, D]),
                                                  ALU.mult))
                    nc.vector.tensor_tensor(out[par][:], out[par][:], xin[par][:], ALU.add).then_inc(done, 1)

                find(0, 0, 0)
                with dve.Fori(0, NB // 2 - 1) as i:
                    i = dve.snap(i)
                    for par in range(2):
                        b = 2 * i + par
                        find(b + 1, i + par, 1 - par)
                        total(b, i, par)
                find(NB - 1, NB // 2 - 1, 1)
                total(NB - 2, NB // 2 - 1, 0)
                total(NB - 1, NB // 2 - 1, 1)

            @block.scalar
            def _(act):
                def hold(s, v):
                    act.wait_ge(s, v)
                    act.sem_inc(tick["act"], 1)

                with act.Fori(0, NB // 2) as i:
                    i = act.snap(i)
                    for par in range(2):
                        hold(done, 2 * i + par + 3)
                        act.dma_start(xo[2 * i + par].rearrange("(c p) d -> p c d", p=P), out[par][:])\
                            .then_inc(stored[par], 16)
                for par in range(2):
                    act.wait_ge(stored[par], 16 * (NB // 2 + 1))


WIN = 32
NBLK = S // WIN
UNITS = 8
BPU = NBLK // 2
AHEAD = 2


def window_attention(nc, x, xo, cols, gates, w_qkv, w_out, k_ident, k_head, k_band):
    with ExitStack() as ctx:
        sb = lambda n, s, d=F32: ctx.enter_context(nc.sbuf_tensor("wa_" + n, s, d))
        ps = lambda n, s: ctx.enter_context(nc.psum_tensor("wa_" + n, s, F32))
        sem = semaphores_of(nc, ctx, "wa_")
        ident = sb("ident", [P, P])
        head = sb("head", [P, 4])
        band = sb("band", [P, 2, BPU, 2 * WIN])
        wqkv = sb("wqkv", [P, 3 * D])
        wout = sb("wout", [P, D])
        half = sb("half", [P, NC])
        xin = [sb(f"xin{i}", [P, NC, D]) for i in range(2)]
        xres = [sb(f"xres{i}", [P, NC, D]) for i in range(2)]
        mcol = [sb(f"mcol{i}", [P, 4]) for i in range(2)]
        gate = [sb(f"gate{i}", [P, D]) for i in range(2)]
        stat = sb("stat", [P, NC, 6])
        mv = sb("mv", [P, NC, 2])
        rstd = sb("rstd", [P, NC])
        nmr = sb("nmr", [P, NC])
        xn = sb("xn", [P, NC, D])
        hT = sb("hT", [P, WIN + S])
        qT = sb("qT", [P, S])
        qm = [sb(f"qm{i}", [P, NBLK, 4, WIN]) for i in range(2)]
        kT = [sb(f"kT{i}", [P, WIN + S]) for i in range(2)]
        vw = [sb(f"vw{i}", [P, NBLK // 2, 2, D]) for i in range(2)]
        s = [sb(f"s{i}", [P, BPU, 2 * WIN]) for i in range(4)]
        mx = [sb(f"mx{i}", [P, BPU]) for i in range(4)]
        sm = sb("sm", [P, 2, 4, BPU])
        pT = [sb(f"pT{i}", [P, 4, P]) for i in range(2)]
        otok = sb("otok", [P, NC, D])
        oT = sb("oT", [P, S])
        xout = [sb(f"xout{i}", [P, NC, D]) for i in range(2)]
        psc = [ps(f"psc{i}", [P, BPU, 2 * WIN]) for i in range(4)]
        ptr = ps("ptr", [P, 4, P])
        pov = ps("pov", [P, 4, 4, 2, 4 * HD])
        pmisc = ps("pmisc", [P, S])

        names = ("const_in", "cleared", "stats", "rstd_ready", "nmr_ready", "xn_ready", "misc_full", "misc_free",
                 "ht_ready", "kv_ready", "scored", "masked", "lowered", "exped", "summed", "turned", "pT_ready",
                 "weighed", "unpacked", "otok_ready", "oT_ready", "xout_ready", "recip", "gated", "q_ready", "qT_ready")
        (const_in, cleared, stats, rstd_ready, nmr_ready, xn_ready, misc_full, misc_free, ht_ready, kv_ready, scored,
         masked, lowered, exped, summed, turned, pT_ready, weighed, unpacked, otok_ready, oT_ready, xout_ready, recip,
         gated, q_ready, qT_ready) = (sem(n) for n in names)
        loaded = [sem(f"loaded{i}") for i in range(2)]
        kept = [sem(f"kept{i}") for i in range(2)]
        stored = [sem(f"stored{i}") for i in range(2)]
        tick = {e: sem("tick_" + e) for e in ("pe", "dve", "act", "pool", "sp")}

        ORDER = ["T2p", "WOp", "h", "q", "k", "v0", "v1"]
        PRO = ["h", "q", "k", "v0", "v1"]

        class Body:

            def __init__(self, b, half, par, at, prev=True, nxt=True):
                self.b, self.half, self.par, self.at, self.prev, self.nxt = b, half, par, at, prev, nxt
                self.uses = [n for n in ORDER if (prev or n not in ("T2p", "WOp")) and (nxt or n in ("T2p", "WOp"))]

            def nth(self, d):
                return self.half + (self.par + d) // 2

            def use(self, name):
                return self.at + self.uses.index(name)

        def batches(eng, body):
            at1 = 2 * len(PRO)
            body(Body(0, 0, 0, len(PRO), prev=False))
            with eng.Fori(0, (NB - 2) // 2) as i:
                i = eng.snap(i)
                body(Body(2 * i + 1, i, 1, 2 * len(ORDER) * i + at1))
                body(Body(2 * i + 2, i + 1, 0, 2 * len(ORDER) * i + at1 + len(ORDER)))
            at = at1 + (NB - 2) * len(ORDER)
            body(Body(NB - 1, NB // 2 - 1, 1, at, nxt=False))
            return at + 2

        with nc.Block() as block:
            @block.sync
            def _(sp):
                def hold(s_, v):
                    sp.wait_ge(s_, v)
                    sp.sem_inc(tick["sp"], 1)

                for dst, src in ((ident[:], k_ident), (head[:], k_head), (band[:], k_band), (wqkv[:], w_qkv),
                                 (wout[:], w_out)):
                    sp.dma_start(dst, src).then_inc(const_in, 16)

                def load(p, par):
                    if not isinstance(p, int) or p >= 2:
                        hold(ht_ready, p - 1)
                    sp.dma_start(xin[par][:], x[p].rearrange("(c p) d -> p c d", p=P)).then_inc(loaded[par], 16)
                    sp.dma_start(mcol[par][:], cols[p]).then_inc(loaded[par], 16)

                def load_residual(p, par):
                    if not isinstance(p, int) or p >= 2:
                        hold(xout_ready, p - 1)
                    sp.dma_start(xres[par][:], x[p].rearrange("(c p) d -> p c d", p=P)).then_inc(kept[par], 16)
                    sp.dma_start(gate[par][:], gates[p].unsqueeze(0).to_broadcast([P, D])).then_inc(kept[par], 16)

                def store(b, par):
                    hold(xout_ready, b + 1)
                    sp.dma_start(xo[b].rearrange("(c p) d -> p c d", p=P), xout[par][:]).then_inc(stored[par], 16)

                load(0, 0)
                load(1, 1)
                load_residual(0, 0)
                load_residual(1, 1)

                def body(k):
                    if k.prev:
                        if k.nxt:
                            load(k.b + 1, 1 - k.par)
                        store(k.b - 1, 1 - k.par)
                        if k.nxt:
                            load_residual(k.b + 1, 1 - k.par)

                batches(sp, body)
                store(NB - 1, 1)
                for par in range(2):
                    sp.wait_ge(stored[par], 16 * (NB // 2))

            @block.tensor
            def _(pe):
                def hold(s_, v):
                    pe.wait_ge(s_, v)
                    pe.sem_inc(tick["pe"], 1)

                def misc(n):
                    if not isinstance(n, int) or n > 0:
                        hold(misc_free, n)

                def four(src, n):
                    misc(n)
                    for c in range(NC):
                        last = nc.tensor.transpose(pmisc[:, c * P:(c + 1) * P], src[:, c, :], ident[:])
                    last.then_inc(misc_full, 1)

                def turn_x(p, n):
                    hold(xn_ready, p + 1)
                    four(xn, n)

                def project(p, which, n):
                    if which == 0:
                        hold(ht_ready, p + 1)
                    misc(n)
                    nc.tensor.matmul(pmisc[:], wqkv[:, which * D:(which + 1) * D], hT[:, WIN:], start=True, stop=True)\
                        .then_inc(misc_full, 1)

                def values(q, n):
                    misc(n)
                    for m in range(4):
                        for w in range(2):
                            o = WIN * (2 * (4 * q + m) + w)
                            last = nc.tensor.matmul(pmisc[64 * w:64 * w + 64, m * D:(m + 1) * D], hT[:, o:o + 2 * WIN],
                                                    wqkv[:, 2 * D:3 * D], start=True, stop=True, skip_group_check=True)
                    last.then_inc(misc_full, 1)

                def scores(b, par, h2):
                    n = UNITS * b + 4 * h2
                    if h2 == 0:
                        hold(kv_ready, b + 1)
                        hold(q_ready, b + 1)
                    if not isinstance(n, int) or n > 0:
                        hold(masked, n)
                    for i in range(BPU):
                        blk = BPU * h2 + i
                        for g in range(4):
                            rows = slice(32 * g, 32 * g + 32)
                            last = nc.tensor.matmul(psc[g][:, i, :], qm[par][rows, blk].rearrange("p j q -> p (j q)"),
                                                    kT[par][rows, WIN * blk:WIN * blk + 2 * WIN], start=True, stop=True,
                                                    skip_group_check=True)
                            if i == BPU - 1:
                                last.then_inc(scored, 1)

                def turn_p(b, u):
                    n = UNITS * b + u
                    hold(exped, n + 1)
                    if not isinstance(n, int) or n >= 1:
                        hold(pT_ready, n)
                    for m in range(4):
                        last = nc.tensor.transpose(ptr[:, m, :], s[u % 4][:, 2 * m:2 * m + 2, :]
                                                   .rearrange("p b k -> p (b k)"), ident[:])
                    last.then_inc(turned, 1)

                def weigh(b, par, u):
                    n = UNITS * b + u
                    g, h2 = u % 4, u // 4
                    hold(pT_ready, n + 1)
                    if g == 0 and (not isinstance(b, int) or 2 * b + h2 >= 1):
                        hold(unpacked, 2 * b + h2)
                    for m in range(4):
                        last = nc.tensor.matmul(pov[:, g, m], pT[u % 2][:, m, :],
                                                vw[par][:, 4 * h2 + m, :, 32 * g:32 * g + 32], start=True, stop=True,
                                                skip_group_check=True)
                    last.then_inc(weighed, 1)

                def project_out(b, n):
                    hold(oT_ready, b + 1)
                    misc(n)
                    for c in range(NC):
                        last = nc.tensor.matmul(pmisc[:, c * P:(c + 1) * P], oT[:, c * P:(c + 1) * P], wout[:],
                                                start=True, stop=True)
                    last.then_inc(misc_full, 1)

                pe.wait_ge(const_in, 80)
                pe.wait_ge(cleared, 1)
                turn_x(0, 0)
                project(0, 0, 1)
                project(0, 1, 2)
                values(0, 3)
                values(1, 4)
                scores(0, 0, 0)

                def body(k):
                    b, par = k.b, k.par
                    for u in range(UNITS):
                        turn_p(b, u)
                        if u > 0:
                            weigh(b, par, u - 1)
                        elif k.prev:
                            weigh(b - 1, 1 - par, UNITS - 1)
                        if u == 1:
                            scores(b, par, 1)
                            if k.prev:
                                hold(otok_ready, b)
                                four(otok, k.use("T2p"))
                        if u == 2:
                            if k.prev:
                                project_out(b - 1, k.use("WOp"))
                            if k.nxt:
                                turn_x(b + 1, k.use("h"))
                        if k.nxt and u == 3:
                            project(b + 1, 0, k.use("q"))
                            project(b + 1, 1, k.use("k"))
                        if k.nxt and u == 4:
                            values(0, k.use("v0"))
                            values(1, k.use("v1"))
                        if k.nxt and u == 5:
                            scores(b + 1, 1 - par, 0)

                at = batches(pe, body)
                weigh(NB - 1, 1, UNITS - 1)
                hold(otok_ready, NB)
                four(otok, at)
                project_out(NB - 1, at + 1)

            @block.scalar
            def _(act):
                def hold(s_, v):
                    act.wait_ge(s_, v)
                    act.sem_inc(tick["act"], 1)

                def after(s_from, value, s_to):
                    hold(s_from, value)
                    act.sem_inc(s_to, 1)

                def normalise(p, par):
                    hold(nmr_ready, p + 1)
                    if not isinstance(p, int) or p >= 1:
                        hold(ht_ready, p)
                    for c in range(NC):
                        last = nc.scalar.activation(xn[:, c, :], xin[par][:, c, :], ACT.Identity,
                                                    bias=nmr[:, c:c + 1], scale=rstd[:, c:c + 1])
                    last.then_inc(xn_ready, 1)

                def modulate(p, par, n):
                    hold(misc_full, n + 1)
                    nc.scalar.activation(hT[:, WIN:], pmisc[:], ACT.Identity, bias=mcol[par][:, 0:1],
                                         scale=mcol[par][:, 1:2]).then_inc(misc_free, 1)
                    after(misc_free, n + 1, ht_ready)

                def keep(dst, src, n):
                    hold(misc_full, n + 1)
                    nc.scalar.activation(dst, src, ACT.Copy).then_inc(misc_free, 1)

                def rest(p, par, at):
                    if not isinstance(p, int) or p >= 1:
                        hold(q_ready, p)
                    hold(misc_full, at + 2)
                    nc.scalar.activation(qT[:], pmisc[:], ACT.Copy).then_inc(misc_free, 1)
                    after(misc_free, at + 2, qT_ready)
                    keep(kT[par][:, WIN:], pmisc[:], at + 2)

                def vals(p, par, at):
                    for q in range(2):
                        hold(misc_full, at + q + 1)
                        for w in range(2):
                            rows = slice(64 * w, 64 * w + 64)
                            last = nc.scalar.activation(vw[par][rows, 4 * q:4 * q + 4, w, :],
                                                        pmisc[rows].rearrange("p (m d) -> p m d", m=4), ACT.Copy)
                        last.then_inc(misc_free, 1)
                    after(misc_free, at + 2, kv_ready)

                def exponentials(b, u):
                    hold(lowered, UNITS * b + u + 1)
                    nc.scalar.activation(s[u % 4][:], s[u % 4][:], ACT.Exp).then_inc(exped, 1)

                def keep_turned(b, u):
                    n = UNITS * b + u
                    hold(turned, n + 1)
                    if not isinstance(n, int) or n >= 2:
                        hold(weighed, n - 1)
                    nc.scalar.activation(pT[u % 2][:], ptr[:], ACT.Copy).then_inc(pT_ready, 1)

                act.wait_ge(const_in, 80)
                act.wait_ge(cleared, 1)
                normalise(0, 0)
                modulate(0, 0, 0)
                rest(0, 0, 0)
                vals(0, 0, 3)
                exponentials(0, 0)

                def body(k):
                    b, par = k.b, k.par
                    for u in range(UNITS):
                        if u + 1 < UNITS:
                            exponentials(b, u + 1)
                        elif k.nxt:
                            exponentials(b + 1, 0)
                        keep_turned(b, u)
                        if u == 0 and k.nxt:
                            normalise(b + 1, 1 - par)
                        if u == 1 and k.prev:
                            keep(oT[:], pmisc[:], k.use("T2p"))
                            after(misc_free, k.use("T2p") + 1, oT_ready)
                        if u == 2 and k.nxt:
                            modulate(b + 1, 1 - par, k.use("h"))
                        if u == 3 and k.nxt:
                            rest(b + 1, 1 - par, k.use("q") - 1)
                        if u == 4 and k.nxt:
                            vals(b + 1, 1 - par, k.use("v0"))

                at = batches(act, body)
                keep(oT[:], pmisc[:], at)
                after(misc_free, at + 1, oT_ready)

            @block.vector
            def _(dve):
                def hold(s_, v):
                    dve.wait_ge(s_, v)
                    dve.sem_inc(tick["dve"], 1)

                nc.vector.memset(half[:], -0.5)
                nc.vector.memset(hT[:, 0:WIN], 0.0)
                for par in range(2):
                    nc.vector.memset(kT[par][:, 0:WIN], 0.0)
                    last = nc.vector.memset(vw[par][:], 0.0)
                last.then_inc(cleared, 1)
                dve.wait_ge(const_in, 80)

                def statistics(p, par, nth):
                    hold(loaded[par], 32 * nth + 32)
                    if not isinstance(p, int) or p >= 1:
                        hold(xn_ready, p)
                    for c in range(NC):
                        last = nc.vector.bn_stats(stat[:, c, :], xin[par][:, c, :])
                    last.then_inc(stats, 1)
                    hold(stats, 3 * p + 1)
                    for c in range(NC):
                        last = nc.vector.bn_aggr(mv[:, c, :], stat[:, c, :])
                    last.then_inc(stats, 1)
                    hold(stats, 3 * p + 2)
                    nc.vector.tensor_scalar(mv[:, :, 1], mv[:, :, 1], LN_EPS, None, ALU.add).then_inc(stats, 1)

                def shift(p):
                    hold(rstd_ready, p + 1)
                    nc.vector.scalar_tensor_tensor(out=nmr[:], in0=mv[:, :, 0], scalar=-1.0, in1=rstd[:],
                                                   op0=ALU.mult, op1=ALU.mult).then_inc(nmr_ready, 1)

                def by_head(p, par):
                    hold(qT_ready, p + 1)
                    for j in range(4):
                        last = nc.vector.tensor_scalar(qm[par][:, :, j, :], qT[:].rearrange("p (b q) -> p b q", q=WIN),
                                                       head[:, j:j + 1], None, ALU.mult)
                    last.then_inc(q_ready, 1)

                def mask(b, u):
                    n = UNITS * b + u
                    hold(scored, n + 1)
                    if not isinstance(n, int) or n >= 4:
                        hold(turned, n - 3)
                        hold(summed, n - 3)
                    nc.vector.scalar_tensor_tensor(out=s[u % 4][:], in0=psc[u % 4][:], scalar=1.0 / float(np.sqrt(HD)),
                                                   in1=band[:, u // 4], op0=ALU.mult, op1=ALU.add).then_inc(masked, 1)
                    hold(masked, n + 1)
                    nc.vector.tensor_reduce(mx[u % 4][:], s[u % 4][:], AX.X, ALU.max)\
                        .then_inc(gated, 1)

                def total(b, u):
                    n = UNITS * b + u
                    hold(exped, n + 1)
                    if u % 4 == 0 and (not isinstance(b, int) or b >= 1):
                        hold(unpacked, 2 * b + u // 4 - 1)
                    nc.vector.tensor_reduce(sm[:, u // 4, u % 4, :], s[u % 4][:], AX.X, ALU.add).then_inc(summed, 1)

                def unpack(b, h2):
                    n = 2 * b + h2
                    hold(summed, 4 * n + 4)
                    nc.vector.reciprocal(sm[:, h2], sm[:, h2]).then_inc(recip, 1)
                    hold(recip, n + 1)
                    hold(weighed, 4 * n + 4)
                    if h2 == 0 and (not isinstance(b, int) or b >= 1):
                        hold(oT_ready, b)
                    for j in range(4):
                        src = slice(32 * j, 32 * j + 32)
                        for w in range(2):
                            for m2 in range(2):
                                o = 32 * (2 * m2 + w)
                                last = nc.vector.tensor_tensor(
                                    otok[o:o + 32, 2 * h2:2 * h2 + 2, :].rearrange("p c (g f) -> p g c f", g=4)
                                    [:, :, :, 8 * j:8 * j + 8],
                                    pov[src, :, m2::2, w, 8 * j:8 * j + 8],
                                    sm[src, h2, :, 2 * m2 + w::4].unsqueeze(3).to_broadcast([32, 4, 2, HD]), ALU.mult)
                    last.then_inc(unpacked, 1)
                    if h2 == 1:
                        hold(unpacked, n + 1)
                        dve.sem_inc(otok_ready, 1)

                def residual(b, par, nth, n):
                    hold(misc_full, n + 1)
                    hold(kept[par], 32 * nth + 32)
                    if not isinstance(nth, int) or nth >= 1:
                        hold(stored[par], 16 * nth)
                    nc.vector.tensor_tensor(xout[par][:], pmisc[:].rearrange("p (c d) -> p c d", c=NC),
                                            gate[par][:].unsqueeze(1).to_broadcast([P, NC, D]), ALU.mult)\
                        .then_inc(misc_free, 1)
                    hold(misc_free, n + 1)
                    nc.vector.tensor_tensor(xout[par][:], xout[par][:], xres[par][:], ALU.add).then_inc(xout_ready, 1)

                statistics(0, 0, 0)
                shift(0)
                by_head(0, 0)
                for u in range(AHEAD):
                    mask(0, u)

                def body(k):
                    b, par = k.b, k.par
                    for u in range(UNITS):
                        v = u + AHEAD
                        if k.nxt and u == 4:
                            by_head(b + 1, 1 - par)
                        if v < UNITS:
                            mask(b, v)
                        elif k.nxt:
                            mask(b + 1, v - UNITS)
                        total(b, u)
                        if u == 0 and k.prev:
                            unpack(b - 1, 1)
                        if u == 4:
                            unpack(b, 0)
                        if u == 2 and k.prev:
                            residual(b - 1, 1 - par, k.nth(-1), k.use("WOp"))
                        if u == 0 and k.nxt:
                            statistics(b + 1, 1 - par, k.nth(1))
                            shift(b + 1)

                at = batches(dve, body)
                unpack(NB - 1, 1)
                residual(NB - 1, 1, NB // 2 - 1, at + 1)

            @block.gpsimd
            def _(pool):
                def hold(s_, v):
                    pool.wait_ge(s_, v)
                    pool.sem_inc(tick["pool"], 1)

                def deviation(p):
                    hold(stats, 3 * p + 3)
                    nc.gpsimd.tensor_tensor(rstd[:], mv[:, :, 1], half[:], ALU.pow).then_inc(rstd_ready, 1)

                def lower(b, u):
                    hold(gated, UNITS * b + u + 1)
                    nc.gpsimd.tensor_tensor(s[u % 4][:], s[u % 4][:],
                                            mx[u % 4][:].unsqueeze(2).to_broadcast([P, BPU, 2 * WIN]), ALU.subtract)\
                        .then_inc(lowered, 1)

                pool.wait_ge(cleared, 1)
                deviation(0)
                for u in range(AHEAD):
                    lower(0, u)

                def body(k):
                    for u in range(UNITS):
                        v = u + AHEAD
                        if v < UNITS:
                            lower(k.b, v)
                        elif k.nxt:
                            lower(k.b + 1, v - UNITS)
                        if u == 0 and k.nxt:
                            deviation(k.b + 1)

                batches(pool, body)


def program(nc, t, out):
    dram = lambda n, s, d=F32: nc.dram_tensor(n, s, d, kind="Internal").ap()
    cols = [dram(f"cols{l}", (NB, D, 4)) for l in range(2)]
    gates = [dram(f"gates{l}", (2, NB, D)) for l in range(2)]
    shifts = [dram(f"shifts{l}", (NB, 2, D)) for l in range(2)]
    xs = [dram(f"xs{l}", ((NE + 1) * REGION, D)) for l in range(2)]
    ys = [dram(f"ys{l}", (top * NB * S + NE * TILE, D)) for l, top in enumerate((2, 1))]
    cnt = [dram(f"cnt{l}", (1, NE)) for l in range(2)]
    pos = [dram(f"pos{l}", (NB, P, 2, NC, top)) for l, top in enumerate((2, 1))]
    weight = dram("weight", (NB, P, NC, 2))
    xa = dram("xa", (NB, S, D))
    xb = dram("xb", (NB, S, D))
    xc = dram("xc", (NB, S, D))

    modulation(nc, [t["c0T"], t["c1T"]], [t["L0_wmod"], t["L1_wmod"]], cols, gates, shifts)
    decayed_attention(nc, t["L0_attn_x"], xa, cols[0], gates[0][0], t["L0_attn_W_q"], t["L0_attn_W_k"],
                      t["L0_attn_W_v"], t["L0_attn_W_o"], t["L0_attn_W_down_kv"], t["L0_attn_W_up_k"],
                      t["L0_attn_W_up_v"], t["k_rows"], t["k_late"], t["k_ident"])
    route(nc, "r0", xa, shifts[0], t["router0T"], [t["L0_ffn_router_b"], t["L0_ffn_lang_b"]], t["k_ident"],
          t["k_prefix"], t["k_iota"], t["k_base"], t["k_row"], xs[0], pos[0], weight, cnt[0], 2)
    experts(nc, "e0", xs[0], ys[0], cnt[0], t["L0_ffn_w1"], t["b1T0"], t["L0_ffn_w2"], t["L0_ffn_b2"], t["k_ident"],
            t["k_tiles"], False, 2)
    combine(nc, "m0", xa, xb, ys[0], pos[0], weight, cnt[0], gates[0][1], t["k_iota"],
            t["k_base"], 2)
    window_attention(nc, xb, xc, cols[1], gates[1][0], t["L1_attn_w_qkv"], t["L1_attn_w_out"], t["k_ident"],
                     t["k_head"], t["k_band"])
    route(nc, "r1", xc, shifts[1], t["L1_ffn_router_w"], [t["L1_ffn_router_b"]], t["k_ident"], t["k_prefix"],
          t["k_iota"], t["k_base"], t["k_row"], xs[1], pos[1], None, cnt[1], 1)
    experts(nc, "e1", xs[1], ys[1], cnt[1], t["L1_ffn_w1"], t["b1T1"], t["L1_ffn_w2"], t["L1_ffn_b2"], t["k_ident"],
            t["k_tiles"], True, 1)
    combine(nc, "m1", xc, out, ys[1], pos[1], None, cnt[1], gates[1][1], t["k_iota"], t["k_base"], 1)


_OUTS = [((16, 512, 128), 'float32')]


def kernel(**inputs):
    import numpy as _np
    import concourse.bacc as _bacc
    from concourse import mybir as _mybir
    from concourse.bass_utils import run_bass_kernel_spmd as _run

    nc = _bacc.Bacc("TRN2", target_bir_lowering=False, num_devices=1)
    a = {n: _np.asarray(v) for n, v in inputs.items()}
    a["c0T"] = a.pop("L0_c").T
    a["c1T"] = a.pop("L1_c").T
    a["router0T"] = _np.concatenate([a.pop("L0_ffn_router_w"), a.pop("L0_ffn_lang_w")]).T
    for l in range(2):
        b1 = a.pop(f"L{l}_ffn_b1")
        a[f"b1T{l}"] = b1.reshape(b1.shape[0], -1, P).transpose(0, 2, 1)
    a.update(constants())
    arrays = {n: _np.ascontiguousarray(v) for n, v in a.items()}
    t = {n: nc.dram_tensor(n, v.shape, _mybir.dt.from_np(v.dtype), kind="ExternalInput").ap()
         for n, v in arrays.items()}
    out = nc.dram_tensor("out_0_dram", _OUTS[0][0], _mybir.dt.from_np(_np.dtype(_OUTS[0][1])),
                         kind="ExternalOutput").ap()
    program(nc, t, out)
    r = _run(nc, [arrays], core_ids=[0])
    return r.results[0]["out_0_dram"]
```
